# Optimizing a Trainium2 kernel written in Bass

```python
import numpy as np
import jax
import jax.numpy as jnp

def _softmax(x, axis=-1):
    return jax.nn.softmax(x, axis=axis)

def _gelu(x):
    return jax.nn.gelu(x, approximate=True)

def _silu(x):
    return jax.nn.silu(x)

def _sigmoid(x):
    return jax.nn.sigmoid(x)

def _layernorm(x, axis=-1, eps=1e-05):
    m = jnp.mean(x, axis=axis, keepdims=True)
    v = jnp.var(x, axis=axis, keepdims=True)
    return (x - m) / jnp.sqrt(v + eps)

def _scatter_add(tgt, idx, src, axis=0):
    return tgt.at[idx].add(src)

def _segment_sum(src, seg, n):
    return jax.ops.segment_sum(src, seg, n)
kernel_name = 'mk_gps_d2_gnn_r8_1495c2'

def setup_inputs(seed: int=0):
    np.random.seed(seed)
    _w = jnp.asarray

    def _rec_inputs():
        import jax
        import jax.numpy as jnp
        _gk = jax.random.key(seed)
        x = -8.776e-05 + 1 * jax.random.normal(jax.random.fold_in(_gk, 1), (6250, 256), jnp.float32)
        src = jax.random.randint(jax.random.fold_in(_gk, 2), (200000,), 0, 6250, jnp.int32)
        dst = jnp.minimum((6250 * jax.random.uniform(jax.random.fold_in(_gk, 3), (200000,)) ** 2.0).astype(jnp.int32), 49999)
        _o = jnp.argsort(dst, stable=True)
        src = src[_o]
        dst = dst[_o]
        edge_type_8 = jax.random.randint(jax.random.fold_in(_gk, 13), (200000,), 0, 8, jnp.int32)
        node_type_4 = jax.random.randint(jax.random.fold_in(_gk, 14), (6250,), 0, 4, jnp.int32)
        return (x, src, dst, edge_type_8, node_type_4)
    x, src, dst, edge_type_8, node_type_4 = _rec_inputs()

    def _L0_gnn_setup():
        import jax, jax.numpy as jnp
        import numpy as np
        N_NODES = 2500
        N_EDGES = 40000
        IN_DIM = 256
        OUT_DIM = 256
        N_HEADS = 4
        D_K = OUT_DIM // N_HEADS
        N_NTYPES = 4
        N_RELS = 8
        SQRT_DK = float(np.sqrt(D_K))

        def _typed_matmul(x, W, node_type):
            all_t = jnp.einsum('ni,tio->tno', x, W)
            return all_t[node_type, jnp.arange(x.shape[0])]
        key = jax.random.key(seed)
        ks = jax.random.split(key, 12)
        xav = lambda k, shape, fan: jax.random.normal(k, shape, jnp.float32) * (1.0 / np.sqrt(fan))
        return {'h': jax.random.normal(ks[0], (N_NODES, IN_DIM), jnp.float32), 'k_linears': xav(ks[1], (N_NTYPES, IN_DIM, OUT_DIM), IN_DIM), 'q_linears': xav(ks[2], (N_NTYPES, IN_DIM, OUT_DIM), IN_DIM), 'v_linears': xav(ks[3], (N_NTYPES, IN_DIM, OUT_DIM), IN_DIM), 'a_linears': xav(ks[4], (N_NTYPES, OUT_DIM, OUT_DIM), OUT_DIM), 'relation_att': xav(ks[5], (N_RELS, N_HEADS, D_K, D_K), D_K), 'relation_msg': xav(ks[6], (N_RELS, N_HEADS, D_K, D_K), D_K), 'relation_pri': jnp.ones((N_RELS, N_HEADS), jnp.float32), 'skip': jnp.ones((N_NTYPES,), jnp.float32), 'node_type': jax.random.randint(ks[7], (N_NODES,), 0, N_NTYPES), 'etype': jnp.sort(jax.random.randint(ks[8], (N_EDGES,), 0, N_RELS)), 'row_idx': jax.random.randint(ks[9], (N_EDGES,), 0, N_NODES), 'col_idx': jax.random.randint(ks[10], (N_EDGES,), 0, N_NODES)}
    _L0_gnn_all = _L0_gnn_setup()
    _L0_gnn_in = {k: v for k, v in _L0_gnn_all.items() if k in ('k_linears', 'q_linears', 'v_linears', 'a_linears', 'relation_att', 'relation_msg', 'relation_pri', 'skip')}
    del _L0_gnn_all

    def _L0_mix_setup():
        import jax, jax.numpy as jnp
        import numpy as np
        HEADS = 8
        DIM_HEAD = 64
        EPS = 1e-05

        def _inst_norm_lastdim(t):
            mu = jnp.mean(t, axis=-1, keepdims=True)
            var = jnp.mean(jnp.square(t - mu), axis=-1, keepdims=True)
            return (t - mu) * jax.lax.rsqrt(var + EPS)
        key = jax.random.key(seed)
        k1, k2, k3, k4 = jax.random.split(key, 4)
        b, n, dim = (4, 1024, 256)
        inner = HEADS * DIM_HEAD
        x = jax.random.normal(k1, (b, n, dim), dtype=jnp.float32)
        Wqkv = jax.random.normal(k2, (3 * inner, dim), dtype=jnp.float32) * (1.0 / np.sqrt(dim))
        Wout = jax.random.normal(k3, (dim, inner), dtype=jnp.float32) * (1.0 / np.sqrt(inner))
        bout = jax.random.normal(k4, (dim,), dtype=jnp.float32) * 0.01
        return {'x': x, 'Wqkv': Wqkv, 'Wout': Wout, 'bout': bout}
    _L0_mix_all = _L0_mix_setup()
    _L0_mix_in = {k: v for k, v in _L0_mix_all.items() if k in ('Wqkv', 'Wout', 'bout')}
    del _L0_mix_all

    def _L0_ffn_setup():
        import jax, jax.numpy as jnp
        import numpy as np
        B, S, D = (8, 512, 256)
        H = 4 * D
        CAPACITY = 0.5
        key = jax.random.key(seed)
        ks = jax.random.split(key, 6)
        x = jax.random.normal(ks[0], (B, S, D), dtype=jnp.float32)
        attention_mask = jnp.zeros((B, 1, 1, S), dtype=jnp.float32)
        wr = jax.random.normal(ks[1], (D, 1), dtype=jnp.float32) * 0.02
        br = jnp.zeros((1,), dtype=jnp.float32)
        w1 = jax.random.normal(ks[2], (D, H), dtype=jnp.float32) * 0.02
        b1 = jnp.zeros((H,), dtype=jnp.float32)
        w2 = jax.random.normal(ks[3], (H, D), dtype=jnp.float32) * 0.02
        b2 = jnp.zeros((D,), dtype=jnp.float32)
        return {'x': x, 'attention_mask': attention_mask, 'wr': wr, 'br': br, 'w1': w1, 'b1': b1, 'w2': w2, 'b2': b2}
    _L0_ffn_all = _L0_ffn_setup()
    _L0_ffn_in = {k: v for k, v in _L0_ffn_all.items() if k in ('attention_mask', 'wr', 'br', 'w1', 'b1', 'w2', 'b2')}
    del _L0_ffn_all

    def _L1_gnn_setup():
        import jax, jax.numpy as jnp
        import numpy as np
        N = 12500
        E = 400000
        IN_C = 256
        HID = 64
        OUT_C = 2
        EPS = 1e-05

        def gcn_conv(x, W, b, src, dst, n):
            xw = x @ W
            loops = jnp.arange(n, dtype=src.dtype)
            s = jnp.concatenate([src, loops])
            d = jnp.concatenate([dst, loops])
            deg = jax.ops.segment_sum(jnp.ones_like(d, dtype=x.dtype), d, num_segments=n)
            dinv = jax.lax.rsqrt(deg)
            norm = dinv[s] * dinv[d]
            out = jax.ops.segment_sum(norm[:, None] * xw[s], d, num_segments=n)
            return out + b

        def batch_norm(x, gamma, beta):
            mu = jnp.mean(x, axis=0)
            var = jnp.mean(jnp.square(x - mu), axis=0)
            return (x - mu) * jax.lax.rsqrt(var + EPS) * gamma + beta
        key = jax.random.key(seed)
        ks = jax.random.split(key, 8)
        x = jax.random.normal(ks[0], (N, IN_C), dtype=jnp.float32)
        edge_index = jax.random.randint(ks[1], (2, E), 0, N, dtype=jnp.int64)
        W1 = jax.random.normal(ks[2], (IN_C, HID), dtype=jnp.float32) / np.sqrt(IN_C)
        b1 = jnp.zeros((HID,), dtype=jnp.float32)
        W2 = jax.random.normal(ks[3], (HID, OUT_C), dtype=jnp.float32) / np.sqrt(HID)
        b2 = jnp.zeros((OUT_C,), dtype=jnp.float32)
        g1 = jnp.ones((HID,), dtype=jnp.float32)
        be1 = jnp.zeros((HID,), dtype=jnp.float32)
        g2 = jnp.ones((OUT_C,), dtype=jnp.float32)
        be2 = jnp.zeros((OUT_C,), dtype=jnp.float32)
        Wd = jax.random.normal(ks[4], (OUT_C, IN_C), dtype=jnp.float32) / np.sqrt(OUT_C)
        bd = jnp.zeros((IN_C,), dtype=jnp.float32)
        return {'x': x, 'edge_index': edge_index, 'W1': W1, 'b1': b1, 'g1': g1, 'be1': be1, 'W2': W2, 'b2': b2, 'g2': g2, 'be2': be2, 'Wd': Wd, 'bd': bd}
    _L1_gnn_all = _L1_gnn_setup()
    _L1_gnn_in = {k: v for k, v in _L1_gnn_all.items() if k in ('W1', 'b1', 'g1', 'be1', 'W2', 'b2', 'g2', 'be2', 'Wd', 'bd')}
    del _L1_gnn_all

    def _L1_mix_setup():
        import jax, jax.numpy as jnp
        import numpy as np
        EPS_NORM = 1e-06
        EPS_ATTN = 1e-06
        HEADS = 8

        def rmsnorm(x, w):
            ms = jnp.mean(x * x, axis=-1, keepdims=True)
            return w * (x * jax.lax.rsqrt(ms + EPS_NORM))

        def linear_attention(x, w_qkv, w_out, b_out):
            B, N, D = x.shape
            hd = D // HEADS
            qkv = (x @ w_qkv).reshape(B, N, 3, HEADS, hd)
            q, k, v = (qkv[:, :, 0], qkv[:, :, 1], qkv[:, :, 2])
            q = jax.nn.elu(q) + 1.0
            k = jax.nn.elu(k) + 1.0
            kv = jnp.einsum('bnhd,bnhm->bhdm', k, v)
            z = 1.0 / (jnp.einsum('bnhd,bhd->bnh', q, k.sum(axis=1)) + EPS_ATTN)
            out = jnp.einsum('bnhd,bhdm,bnh->bnhm', q, kv, z)
            out = out.reshape(B, N, D)
            return out @ w_out + b_out
        key = jax.random.key(seed)
        ks = jax.random.split(key, 4)
        B, N, D = (16, 1024, 256)
        x = jax.random.normal(ks[0], (B, N, D), dtype=jnp.float32)
        w_norm1 = jnp.ones((D,), dtype=jnp.float32)
        w_qkv = jax.random.normal(ks[1], (D, 3 * D), dtype=jnp.float32) * 0.02
        w_out = jax.random.normal(ks[2], (D, D), dtype=jnp.float32) * 0.02
        b_out = jnp.zeros((D,), dtype=jnp.float32)
        w_norm2 = jnp.ones((D,), dtype=jnp.float32)
        return {'x': x, 'w_norm1': w_norm1, 'w_qkv': w_qkv, 'w_out': w_out, 'b_out': b_out, 'w_norm2': w_norm2}
    _L1_mix_all = _L1_mix_setup()
    _L1_mix_in = {k: v for k, v in _L1_mix_all.items() if k in ('w_norm1', 'w_qkv', 'w_out', 'b_out', 'w_norm2')}
    del _L1_mix_all

    def _L1_ffn_setup():
        import jax, jax.numpy as jnp
        import numpy as np
        BN_EPS = 0.001

        def _bn(h, g, b, m, v):
            return g * (h - m) * jax.lax.rsqrt(v + BN_EPS) + b
        key = jax.random.key(seed)
        ks = jax.random.split(key, 8)
        B, F, Df = (256, 64, 256)
        E, H, D = (8, 256, 256)
        s1 = 1.0 / np.sqrt(Df)
        s2 = 1.0 / np.sqrt(H)
        return {'x': jax.random.normal(ks[0], (B, F, Df), jnp.float32), 'Wr': jax.random.normal(ks[1], (Df, E), jnp.float32) * s1, 'br': jnp.zeros((E,), jnp.float32), 'W1': jax.random.normal(ks[2], (E, Df, H), jnp.float32) * s1, 'b1': jnp.zeros((E, H), jnp.float32), 'g1': jnp.ones((E, H), jnp.float32), 'be1': jnp.zeros((E, H), jnp.float32), 'm1': jnp.zeros((E, H), jnp.float32), 'v1': jnp.ones((E, H), jnp.float32), 'W2': jax.random.normal(ks[3], (E, H, H), jnp.float32) * s2, 'b2': jnp.zeros((E, H), jnp.float32), 'g2': jnp.ones((E, H), jnp.float32), 'be2': jnp.zeros((E, H), jnp.float32), 'm2': jnp.zeros((E, H), jnp.float32), 'v2': jnp.ones((E, H), jnp.float32), 'Wo': jax.random.normal(ks[4], (E, H, D), jnp.float32) * s2, 'bo': jnp.zeros((E, D), jnp.float32)}
    _L1_ffn_all = _L1_ffn_setup()
    _L1_ffn_in = {k: v for k, v in _L1_ffn_all.items() if k in ('Wr', 'br', 'W1', 'b1', 'g1', 'be1', 'm1', 'v1', 'W2', 'b2', 'g2', 'be2', 'm2', 'v2', 'Wo', 'bo')}
    del _L1_ffn_all
    return {'x': x, 'src': src, 'dst': dst, 'edge_type_8': edge_type_8, 'node_type_4': node_type_4, 'L0_gnn_k_linears': _L0_gnn_in['k_linears'], 'L0_gnn_q_linears': _L0_gnn_in['q_linears'], 'L0_gnn_v_linears': _L0_gnn_in['v_linears'], 'L0_gnn_a_linears': _L0_gnn_in['a_linears'], 'L0_gnn_relation_att': _L0_gnn_in['relation_att'], 'L0_gnn_relation_msg': _L0_gnn_in['relation_msg'], 'L0_gnn_relation_pri': _L0_gnn_in['relation_pri'], 'L0_gnn_skip': _L0_gnn_in['skip'], 'L0_mix_Wqkv': _L0_mix_in['Wqkv'], 'L0_mix_Wout': _L0_mix_in['Wout'], 'L0_mix_bout': _L0_mix_in['bout'], 'L0_ffn_attention_mask': _L0_ffn_in['attention_mask'], 'L0_ffn_wr': _L0_ffn_in['wr'], 'L0_ffn_br': _L0_ffn_in['br'], 'L0_ffn_w1': _L0_ffn_in['w1'], 'L0_ffn_b1': _L0_ffn_in['b1'], 'L0_ffn_w2': _L0_ffn_in['w2'], 'L0_ffn_b2': _L0_ffn_in['b2'], 'L1_gnn_W1': _L1_gnn_in['W1'], 'L1_gnn_b1': _L1_gnn_in['b1'], 'L1_gnn_g1': _L1_gnn_in['g1'], 'L1_gnn_be1': _L1_gnn_in['be1'], 'L1_gnn_W2': _L1_gnn_in['W2'], 'L1_gnn_b2': _L1_gnn_in['b2'], 'L1_gnn_g2': _L1_gnn_in['g2'], 'L1_gnn_be2': _L1_gnn_in['be2'], 'L1_gnn_Wd': _L1_gnn_in['Wd'], 'L1_gnn_bd': _L1_gnn_in['bd'], 'L1_mix_w_norm1': _L1_mix_in['w_norm1'], 'L1_mix_w_qkv': _L1_mix_in['w_qkv'], 'L1_mix_w_out': _L1_mix_in['w_out'], 'L1_mix_b_out': _L1_mix_in['b_out'], 'L1_mix_w_norm2': _L1_mix_in['w_norm2'], 'L1_ffn_Wr': _L1_ffn_in['Wr'], 'L1_ffn_br': _L1_ffn_in['br'], 'L1_ffn_W1': _L1_ffn_in['W1'], 'L1_ffn_b1': _L1_ffn_in['b1'], 'L1_ffn_g1': _L1_ffn_in['g1'], 'L1_ffn_be1': _L1_ffn_in['be1'], 'L1_ffn_m1': _L1_ffn_in['m1'], 'L1_ffn_v1': _L1_ffn_in['v1'], 'L1_ffn_W2': _L1_ffn_in['W2'], 'L1_ffn_b2': _L1_ffn_in['b2'], 'L1_ffn_g2': _L1_ffn_in['g2'], 'L1_ffn_be2': _L1_ffn_in['be2'], 'L1_ffn_m2': _L1_ffn_in['m2'], 'L1_ffn_v2': _L1_ffn_in['v2'], 'L1_ffn_Wo': _L1_ffn_in['Wo'], 'L1_ffn_bo': _L1_ffn_in['bo']}

def reference(x, src, dst, edge_type_8, node_type_4, L0_gnn_k_linears, L0_gnn_q_linears, L0_gnn_v_linears, L0_gnn_a_linears, L0_gnn_relation_att, L0_gnn_relation_msg, L0_gnn_relation_pri, L0_gnn_skip, L0_mix_Wqkv, L0_mix_Wout, L0_mix_bout, L0_ffn_attention_mask, L0_ffn_wr, L0_ffn_br, L0_ffn_w1, L0_ffn_b1, L0_ffn_w2, L0_ffn_b2, L1_gnn_W1, L1_gnn_b1, L1_gnn_g1, L1_gnn_be1, L1_gnn_W2, L1_gnn_b2, L1_gnn_g2, L1_gnn_be2, L1_gnn_Wd, L1_gnn_bd, L1_mix_w_norm1, L1_mix_w_qkv, L1_mix_w_out, L1_mix_b_out, L1_mix_w_norm2, L1_ffn_Wr, L1_ffn_br, L1_ffn_W1, L1_ffn_b1, L1_ffn_g1, L1_ffn_be1, L1_ffn_m1, L1_ffn_v1, L1_ffn_W2, L1_ffn_b2, L1_ffn_g2, L1_ffn_be2, L1_ffn_m2, L1_ffn_v2, L1_ffn_Wo, L1_ffn_bo):
    import jax
    import jax.numpy as jnp

    def _L0_gnn_ref(h, k_linears, q_linears, v_linears, a_linears, relation_att, relation_msg, relation_pri, skip, node_type, etype, row_idx, col_idx):
        import jax, jax.numpy as jnp
        import numpy as np
        N_NODES = 2500
        N_EDGES = 40000
        IN_DIM = 256
        OUT_DIM = 256
        N_HEADS = 4
        D_K = OUT_DIM // N_HEADS
        N_NTYPES = 4
        N_RELS = 8
        SQRT_DK = float(np.sqrt(D_K))

        def _typed_matmul(x, W, node_type):
            all_t = jnp.einsum('ni,tio->tno', x, W)
            return all_t[node_type, jnp.arange(x.shape[0])]
        n = h.shape[0]
        k = _typed_matmul(h, k_linears, node_type).reshape(n, N_HEADS, D_K)
        q = _typed_matmul(h, q_linears, node_type).reshape(n, N_HEADS, D_K)
        v = _typed_matmul(h, v_linears, node_type).reshape(n, N_HEADS, D_K)
        q_att = jnp.einsum('nhd,rhde->rnhe', q, relation_att)
        v_msg = jnp.einsum('nhd,rhde->rnhe', v, relation_msg)
        aw_q_edge = q_att[etype, col_idx]
        msg_edge = v_msg[etype, row_idx]
        attn_score = jnp.sum(aw_q_edge * k[row_idx], axis=-1)
        score = attn_score * (relation_pri[etype] / SQRT_DK)
        m = jax.ops.segment_max(score, col_idx, num_segments=n)
        ex = jnp.exp(score - m[col_idx])
        denom = jax.ops.segment_sum(ex, col_idx, num_segments=n)
        alpha = ex / denom[col_idx]
        agg = jax.ops.segment_sum(alpha[..., None] * msg_edge, col_idx, num_segments=n)
        agg = agg.reshape(n, OUT_DIM)
        out = _typed_matmul(agg, a_linears, node_type)
        out = jax.nn.sigmoid(skip)[node_type][:, None] * out
        return out

    def _L0_mix_ref(x, Wqkv, Wout, bout):
        import jax, jax.numpy as jnp
        import numpy as np
        HEADS = 8
        DIM_HEAD = 64
        EPS = 1e-05

        def _inst_norm_lastdim(t):
            mu = jnp.mean(t, axis=-1, keepdims=True)
            var = jnp.mean(jnp.square(t - mu), axis=-1, keepdims=True)
            return (t - mu) * jax.lax.rsqrt(var + EPS)
        b, n, dim = x.shape
        qkv = jnp.einsum('bnc,fc->bnf', x, Wqkv)
        q, k, v = jnp.split(qkv, 3, axis=-1)

        def to_heads(t):
            return t.reshape(b, n, HEADS, DIM_HEAD).transpose(0, 2, 1, 3)
        q, k, v = (to_heads(q), to_heads(k), to_heads(v))
        k = _inst_norm_lastdim(k)
        v = _inst_norm_lastdim(v)
        dots = jnp.einsum('bhnd,bhne->bhde', k, v)
        out = jnp.einsum('bhnd,bhde->bhne', q, dots) / n
        out = out.transpose(0, 2, 1, 3).reshape(b, n, HEADS * DIM_HEAD)
        return jnp.einsum('bnf,cf->bnc', out, Wout) + bout

    def _L0_ffn_ref(x, attention_mask, wr, br, w1, b1, w2, b2):
        import jax, jax.numpy as jnp
        import numpy as np
        B, S, D = (8, 512, 256)
        H = 4 * D
        CAPACITY = 0.5
        b, s, d = x.shape
        weights = (jnp.einsum('bsd,do->bso', x, wr) + br)[..., 0]
        k = max(1, int(CAPACITY * s))
        kk = k - 1 if k > 1 else 1
        _, idx = jax.lax.top_k(weights, k)
        sel_idx = idx[:, :kk]
        sel = jnp.take_along_axis(x, sel_idx[:, :, None], axis=1)
        h = jax.nn.gelu(jnp.einsum('bkd,dh->bkh', sel, w1) + b1)
        y = jnp.einsum('bkh,hd->bkd', h, w2) + b2
        w_sel = jnp.take_along_axis(weights, sel_idx, axis=1)
        y = y * w_sel[..., None]
        batch_idx = jnp.arange(b)[:, None]
        processed = jnp.zeros_like(x).at[batch_idx, sel_idx].set(y)
        return processed + x

    def _L1_gnn_ref(x, edge_index, W1, b1, g1, be1, W2, b2, g2, be2, Wd, bd):
        import jax, jax.numpy as jnp
        import numpy as np
        N = 12500
        E = 400000
        IN_C = 256
        HID = 64
        OUT_C = 2
        EPS = 1e-05

        def gcn_conv(x, W, b, src, dst, n):
            xw = x @ W
            loops = jnp.arange(n, dtype=src.dtype)
            s = jnp.concatenate([src, loops])
            d = jnp.concatenate([dst, loops])
            deg = jax.ops.segment_sum(jnp.ones_like(d, dtype=x.dtype), d, num_segments=n)
            dinv = jax.lax.rsqrt(deg)
            norm = dinv[s] * dinv[d]
            out = jax.ops.segment_sum(norm[:, None] * xw[s], d, num_segments=n)
            return out + b

        def batch_norm(x, gamma, beta):
            mu = jnp.mean(x, axis=0)
            var = jnp.mean(jnp.square(x - mu), axis=0)
            return (x - mu) * jax.lax.rsqrt(var + EPS) * gamma + beta
        src, dst = (edge_index[0], edge_index[1])
        n = x.shape[0]
        h = gcn_conv(x, W1, b1, src, dst, n)
        h = jax.nn.relu(batch_norm(h, g1, be1))
        z = batch_norm(gcn_conv(h, W2, b2, src, dst, n), g2, be2)
        return z @ Wd + bd

    def _L1_mix_ref(x, w_norm1, w_qkv, w_out, b_out, w_norm2):
        import jax, jax.numpy as jnp
        import numpy as np
        EPS_NORM = 1e-06
        EPS_ATTN = 1e-06
        HEADS = 8

        def rmsnorm(x, w):
            ms = jnp.mean(x * x, axis=-1, keepdims=True)
            return w * (x * jax.lax.rsqrt(ms + EPS_NORM))

        def linear_attention(x, w_qkv, w_out, b_out):
            B, N, D = x.shape
            hd = D // HEADS
            qkv = (x @ w_qkv).reshape(B, N, 3, HEADS, hd)
            q, k, v = (qkv[:, :, 0], qkv[:, :, 1], qkv[:, :, 2])
            q = jax.nn.elu(q) + 1.0
            k = jax.nn.elu(k) + 1.0
            kv = jnp.einsum('bnhd,bnhm->bhdm', k, v)
            z = 1.0 / (jnp.einsum('bnhd,bhd->bnh', q, k.sum(axis=1)) + EPS_ATTN)
            out = jnp.einsum('bnhd,bhdm,bnh->bnhm', q, kv, z)
            out = out.reshape(B, N, D)
            return out @ w_out + b_out
        h = x + linear_attention(rmsnorm(x, w_norm1), w_qkv, w_out, b_out)
        return h + rmsnorm(h, w_norm2)

    def _L1_ffn_ref(x, Wr, br, W1, b1, g1, be1, m1, v1, W2, b2, g2, be2, m2, v2, Wo, bo):
        import jax, jax.numpy as jnp
        import numpy as np
        BN_EPS = 0.001

        def _bn(h, g, b, m, v):
            return g * (h - m) * jax.lax.rsqrt(v + BN_EPS) + b
        feat = jnp.mean(x, axis=0)
        w = jax.nn.softmax(feat @ Wr + br, axis=-1)
        h = jnp.einsum('bfd,edh->bfeh', x, W1) + b1
        h = jax.nn.relu(_bn(h, g1, be1, m1, v1))
        h = jnp.einsum('bfeh,ehk->bfek', h, W2) + b2
        h = jax.nn.relu(_bn(h, g2, be2, m2, v2))
        y = jnp.einsum('bfeh,ehd->bfed', h, Wo) + bo
        return jnp.einsum('bfed,fe->bfd', y, w)
    edge_index = jnp.stack([src, dst])
    xn = _layernorm(x, axis=-1)
    x = x + _L0_gnn_ref(xn, L0_gnn_k_linears, L0_gnn_q_linears, L0_gnn_v_linears, L0_gnn_a_linears, L0_gnn_relation_att, L0_gnn_relation_msg, L0_gnn_relation_pri, L0_gnn_skip, node_type_4, edge_type_8, src, dst) + _L0_mix_ref(xn[None], L0_mix_Wqkv, L0_mix_Wout, L0_mix_bout)[0]
    x = x + _L0_ffn_ref(_layernorm(x, axis=-1)[None], L0_ffn_attention_mask, L0_ffn_wr, L0_ffn_br, L0_ffn_w1, L0_ffn_b1, L0_ffn_w2, L0_ffn_b2)[0]
    xn = _layernorm(x, axis=-1)
    x = x + _L1_gnn_ref(xn, edge_index, L1_gnn_W1, L1_gnn_b1, L1_gnn_g1, L1_gnn_be1, L1_gnn_W2, L1_gnn_b2, L1_gnn_g2, L1_gnn_be2, L1_gnn_Wd, L1_gnn_bd) + _L1_mix_ref(xn[None], L1_mix_w_norm1, L1_mix_w_qkv, L1_mix_w_out, L1_mix_b_out, L1_mix_w_norm2)[0]
    x = x + _L1_ffn_ref(_layernorm(x, axis=-1)[None], L1_ffn_Wr, L1_ffn_br, L1_ffn_W1, L1_ffn_b1, L1_ffn_g1, L1_ffn_be1, L1_ffn_m1, L1_ffn_v1, L1_ffn_W2, L1_ffn_b2, L1_ffn_g2, L1_ffn_be2, L1_ffn_m2, L1_ffn_v2, L1_ffn_Wo, L1_ffn_bo)[0]
    return x

_drawn_inputs = setup_inputs


def setup_inputs(seed=0):
    import zlib

    import numpy as np

    out = dict(_drawn_inputs(seed))
    spreads = {'L0_gnn_relation_pri': (1.0, 0.2),
     'L0_gnn_skip': (1.0, 0.6),
     'L0_ffn_b1': (0.0, 0.8),
     'L0_ffn_b2': (0.0, 0.767),
     'L1_gnn_b1': (0.0, 2.0),
     'L1_gnn_g1': (1.0, 0.6),
     'L1_gnn_be1': (0.0, 0.343),
     'L1_gnn_b2': (0.0, 2.0),
     'L1_gnn_g2': (1.0, 0.2),
     'L1_gnn_be2': (0.0, 0.1),
     'L1_gnn_bd': (0.0, 0.336),
     'L1_mix_w_norm1': (1.0, 0.6),
     'L1_mix_b_out': (0.0, 0.313),
     'L1_mix_w_norm2': (1.0, 0.2),
     'L1_ffn_br': (0.0, 0.8),
     'L1_ffn_b1': (0.0, 0.8),
     'L1_ffn_g1': (1.0, 0.6),
     'L1_ffn_be1': (0.0, 0.8),
     'L1_ffn_m1': (0.0, 0.8),
     'L1_ffn_v1': (1.0, 0.6),
     'L1_ffn_b2': (0.0, 0.8),
     'L1_ffn_g2': (1.0, 0.6),
     'L1_ffn_be2': (0.0, 0.8),
     'L1_ffn_m2': (0.0, 0.8),
     'L1_ffn_v2': (1.0, 0.6),
     'L1_ffn_bo': (0.0, 0.714)}
    factors = {'L0_mix_bout': 7.201,
     'L0_ffn_wr': 4.201,
     'L0_ffn_w1': 4.831,
     'L0_ffn_w2': 4.535,
     'L1_mix_w_qkv': 8.0,
     'L1_mix_w_out': 8.0}
    for name, (base, spread) in spreads.items():
        noise = np.random.default_rng([zlib.crc32(name.encode()), seed]).standard_normal(out[name].shape)
        drawn = base * np.exp(spread * noise) if base else spread * noise
        out[name] = jnp.asarray(drawn.astype(out[name].dtype))
    for name, factor in factors.items():
        out[name] = (out[name] * factor).astype(out[name].dtype)
    return out
```

```python
from contextlib import ExitStack

import numpy as np
import concourse.bass as bass
from concourse import mybir

F32 = mybir.dt.float32
I32 = mybir.dt.int32
U32 = mybir.dt.uint32
ALU = mybir.AluOpType
ACT = mybir.ActivationFunctionType
AX = mybir.AxisListType

P = 128
N = 6250
D = 256
E = 200000
NT = 50
NP = NT * P
NB = 50
BW = 127
RB = 13
T = RB * P
G = 8
GROUPS = 204
FULL = E // P
REST = E - FULL * P
NEG = -1.0e30
R, H, DK = 8, 4, 64
C_CNT, C_LAST, C_M, C_EX, C_V = 0, 1, 2, 6, 10
CW = C_V + D


class Chain:

    def __init__(self, eng, sem):
        self.eng, self.sem, self.n, self.base = eng, sem, 0, 0

    def done(self, ins):
        ins.then_inc(self.sem, 1)
        self.n += 1
        return ins

    def settle(self):
        self.eng.wait_ge(self.sem, self.base + self.n)

    def link(self, ins):
        self.done(ins)
        self.settle()

    def enter(self, i, per):
        self.outer, self.per = self.n, per
        self.base, self.n = i * per + self.outer, 0

    def leave(self, count):
        assert self.n == self.per, (self.n, self.per)
        self.base, self.n = 0, self.outer + count * self.per


def wait_alone(eng, gate):
    eng.sem_inc(gate, 1)


def wait_after(eng, sems, i, s, back=0, per=1, less=0):
    j = s - back
    count = (i + j // len(sems) + 1) * per - less
    if not (isinstance(count, int) and count <= 0):
        eng.wait_ge(sems[j % len(sems)], count)


def in_turns(eng, groups, slots, parts):
    most = max(ahead for ahead, _ in parts)
    least = min(ahead for ahead, _ in parts)
    assert most <= slots and least >= -slots and groups % slots == 0

    def written_out(turns):
        for k in turns:
            for ahead, part in parts:
                if 0 <= k + ahead < groups:
                    part((k + ahead) // slots, (k + ahead) % slots)

    written_out(range(-most, slots))
    with eng.Fori(1, groups // slots - 1) as i:
        for s in range(slots):
            for ahead, part in parts:
                part(i + (s + ahead) // slots, (s + ahead) % slots)
    written_out(range(groups - slots, groups - least))


def index_tables(nc, sem, bank, c, dram, src, dst, etype):
    with ExitStack() as ctx:
        def sbt(name, shape, dt=F32):
            return ctx.enter_context(nc.sbuf_tensor(name, shape, dt))

        raw = sbt("raw_edges", [P, 4, RB, P], I32)
        prev_i = sbt("prev_i", [P, RB], I32)
        prev = sbt("prev", [P, RB])
        dn = sbt("dst_next", [P, RB, P])
        et = sbt("etype_f", [P, RB, P])
        tab = sbt("tile_rows_s", [P, RB, 5, P])
        c0 = sbt("continues0", [P, RB])
        cmp = sbt("block_cmp", [P, RB, NB - 1])
        edge_of = sbt("block_edges", [P, RB, NB - 1])
        fb = sbt("first_block", [P, RB])
        start_row = sbt("start_row", [P, T])
        cmp_row = sbt("cmp_row", [P, T])
        cnt = sbt("cnt", [P, RB])
        tile_f = sbt("tile_f", [P, RB])
        tile_i = sbt("tile_i", [P, RB], I32)
        blk = sbt("blk", [P, RB])
        blk_i = sbt("blk_i", [P, RB], I32)
        st = sbt("step_rows", [P, RB, 5, P])
        rel = sbt("rel", [P, RB, P])
        inb = sbt("inb", [P, RB, P])
        rels = sbt("rels", [P, RB, P])
        mask = sbt("mask_s", [P, RB, P + 1])
        key = sbt("key", [P, RB])
        cin = sbt("cin", [P, RB])
        cols = sbt("cols_s", [P, T // G, 5, G], F32)

        loaded, filled, dve, tabled, started, rowed = (sem(x) for x in (
            "edges_loaded", "edges_filled", "index_chain", "tile_rows_written", "starts_written", "start_row_loaded"))
        ready, gathered, turned, copied, stored = (sem(x) for x in (
            "step_tiles_ready", "step_rows_gathered", "columns_turned", "columns_copied", "tables_stored"))
        written = sem("tile_rows_ready")
        starts = sem("starts_ready")
        inblock = sem("block_columns_ready")
        block = ctx.enter_context(nc.Block())
        STORES = 5

        @block.sync
        def _(sp):
            sp.wait_ge(filled, 3)
            for n, (a, off) in enumerate(((dst, 0), (dst, 1), (src, 0), (etype, 0))):
                sp.dma_start(raw[:, n, 0:12, :], a[off:off + 12 * P * P].rearrange("(b p j) -> p b j", p=P, j=P)).then_inc(loaded, 16)
                rows = FULL - 12 * P
                sp.dma_start(raw[0:rows, n, 12, :],
                             a[off + 12 * P * P:off + FULL * P].rearrange("(p j) -> p j", j=P)).then_inc(loaded, 16)
                sp.dma_start(raw[rows:rows + 1, n, 12, 0:REST - off],
                             a[FULL * P + off:E].rearrange("(a j) -> a j", a=1)).then_inc(loaded, 16)
            last = dst[0:FULL * P].rearrange("(t j) -> t j", j=P)[:, P - 1:P]
            sp.dma_start(prev_i[1:P, 0:1], last[0:P - 1, :], allow_slow_non_contiguous=True).then_inc(loaded, 16)
            for b in range(1, RB):
                rows = min(P, FULL - (b * P - 1))
                sp.dma_start(prev_i[0:rows, b:b + 1], last[b * P - 1:b * P - 1 + rows, :],
                             allow_slow_non_contiguous=True).then_inc(loaded, 16)
            sp.wait_ge(written, 1)
            sp.dma_start(dram["tile_rows"].rearrange("(b p) n -> p b n", p=P),
                         tab[:].rearrange("p b c j -> p b (c j)")).then_inc(tabled, 16)
            sp.wait_ge(starts, 1)
            sp.dma_start(dram["starts"].rearrange("(b p) -> p b", p=P), fb[:], allow_slow_non_contiguous=True).then_inc(started, 16)
            sp.wait_ge(started, 16)
            sp.dma_start(start_row[:], dram["starts"].rearrange("(a n) -> a n", a=1).broadcast_to([P, T])
                         ).then_inc(rowed, 16)
            sp.wait_ge(inblock, 1)
            sp.dma_start(dram["rel_rows"].rearrange("(b p) j -> p b j", p=P), rel[:]).then_inc(stored, 16)
            for b in range(RB):
                sp.dma_start(dram["mask"][b * P:(b + 1) * P, :, :],
                             mask[:, b, :].unsqueeze(1).broadcast_to([P, H, P + 1])).then_inc(stored, 16)
            sp.dma_start(dram["keys"].rearrange("(b p) -> p b", p=P), key[:], allow_slow_non_contiguous=True).then_inc(stored, 16)
            sp.dma_start(dram["blocks"].rearrange("(b p) -> p b", p=P), blk_i[:], allow_slow_non_contiguous=True).then_inc(stored, 16)
            sp.wait_ge(copied, RB)
            sp.dma_start(dram["cols"].rearrange("p k c g -> p (k c g)"),
                         cols[:].rearrange("p k c g -> p (k c g)")).then_inc(stored, 16)
            sp.wait_ge(stored, 16 * (4 + RB))

        @block.vector
        def _(v):
            ch = Chain(v, dve)
            v.memset(raw[:, 0:2, :, :], N).then_inc(filled, 1)
            v.memset(raw[:, 2:4, :, :], 0).then_inc(filled, 1)
            v.memset(prev_i[:], -1).then_inc(filled, 1)
            v.wait_ge(loaded, 16 * (12 + RB))
            d_, s_, k_, l_, c_ = (tab[:, :, x, :] for x in range(5))
            ch.done(v.tensor_copy(d_, raw[:, 0]))
            ch.done(v.tensor_copy(dn[:], raw[:, 1]))
            ch.done(v.tensor_copy(s_, raw[:, 2]))
            ch.done(v.tensor_copy(et[:], raw[:, 3]))
            ch.link(v.tensor_copy(prev[:], prev_i[:]))
            v.wait_ge(c["ready"], c["n"])
            ch.done(v.tensor_tensor(l_, d_, dn[:], ALU.not_equal))
            ch.done(v.scalar_tensor_tensor(k_, et[:], float(NP), s_, ALU.mult, ALU.add))
            ch.done(v.tensor_tensor(c_, d_, tab[:, :, 0, 0:1].broadcast_to([P, RB, P]), ALU.is_equal))
            ch.done(v.tensor_tensor(c0[:], tab[:, :, 0, 0], prev[:], ALU.is_equal))
            ch.done(v.tensor_scalar(edge_of[:], c["iota"][:, 0:NB - 1].unsqueeze(1).broadcast_to([P, RB, NB - 1]),
                                    float(BW), float(BW), ALU.mult, ALU.add))
            ch.settle()
            ch.done(v.memset(tab[:, :, 3, P - 1:P], 1.0))
            ch.done(v.tensor_tensor(c_, c_, c0[:].unsqueeze(2).broadcast_to([P, RB, P]), ALU.mult))
            ch.done(v.tensor_tensor(cmp[:], edge_of[:], tab[:, :, 0, 0:1].broadcast_to([P, RB, NB - 1]), ALU.is_le))
            ch.settle()
            v.tensor_copy(tile_f[:], c["tile_no"][:]).then_inc(written, 1)
            ch.link(v.tensor_reduce(fb[:], cmp[:], AX.X, ALU.add))
            v.tensor_tensor(fb[:], fb[:], c["tile_no"][:], ALU.add).then_inc(starts, 1)
            v.wait_ge(rowed, 16)
            for b in range(RB):
                ch.link(v.tensor_scalar(cmp_row[:], start_row[:], c["tile_no"][:, b:b + 1], 0.0,
                                        ALU.is_le, ALU.add, accum_out=cnt[:, b:b + 1]))
            ch.link(v.tensor_scalar(tile_f[:], cnt[:], -1.0, 0.0, ALU.add, ALU.max))
            v.tensor_copy(tile_i[:], tile_f[:]).then_inc(ready, 1)
            ch.link(v.tensor_tensor(blk[:], c["tile_no"][:], tile_f[:], ALU.subtract))
            ch.done(v.tensor_copy(blk_i[:], blk[:]))
            ch.link(v.tensor_scalar(blk[:], blk[:], float(-BW), None, ALU.mult))
            v.wait_ge(gathered, 16 * RB)
            ch.link(v.tensor_tensor(rel[:], st[:, :, 0, :], blk[:].unsqueeze(2).broadcast_to([P, RB, P]), ALU.add))
            ch.done(v.tensor_scalar(inb[:], rel[:], 0.0, None, ALU.is_ge))
            ch.link(v.tensor_scalar(rels[:], rel[:], float(BW - 1), None, ALU.is_le))
            ch.link(v.tensor_tensor(inb[:], inb[:], rels[:], ALU.mult))
            ch.link(v.tensor_scalar(rels[:], rel[:], -1.0, float(BW), ALU.mult, ALU.add))
            ch.link(v.tensor_tensor(rels[:], rels[:], st[:, :, 4, :], ALU.mult))
            ch.link(v.tensor_tensor(rels[:], rels[:], rel[:], ALU.add))
            ch.link(v.scalar_tensor_tensor(rels[:], rels[:], -999.0, inb[:], ALU.add, ALU.mult))
            ch.done(v.tensor_scalar(rels[:], rels[:], 999.0, None, ALU.add))
            ch.done(v.memset(mask[:, :, 0:1], NEG))
            ch.done(v.tensor_scalar(mask[:, :, 1:P + 1], st[:, :, 3, :], NEG, None, ALU.mult))
            ch.link(v.tensor_tensor(cin[:], inb[:, :, 0], st[:, :, 4, 0], ALU.mult))
            ch.link(v.scalar_tensor_tensor(key[:], st[:, :, 0, 0], 1.0, cin[:], ALU.add, ALU.mult))
            v.tensor_scalar(key[:], key[:], -1.0, None, ALU.add).then_inc(inblock, 1)
            for b in range(RB):
                v.wait_ge(turned, b + 1)
                k0, k1 = b * P // G, (b + 1) * P // G
                view = cols[:, k0:k1, :, :]
                for x in range(5):
                    o = view[:, :, x, :]
                    if x < 2:
                        o = o.bitcast(I32)
                    ch.done(v.tensor_copy(o, bank[2 * (b % 2) + x // 4][:, (x % 4) * P:(x % 4 + 1) * P]
                                          .rearrange("p (k g) -> p k g", g=G)))
                ch.settle()
                v.tensor_copy(tile_f[:, 0:1], cnt[:, 0:1]).then_inc(copied, 1)

        @block.gpsimd
        def _(g):
            g.wait_ge(ready, 1)
            g.wait_ge(tabled, 16)
            for b in range(RB):
                g.indirect_dma_start(out=st[:, b, :, :].rearrange("p c j -> p (c j)"), out_offset=None,
                                     in_=dram["tile_rows"],
                                     in_offset=bass.IndirectOffsetOnAxis(ap=tile_i[:, b:b + 1].bitcast(U32), axis=0)
                                     ).then_inc(gathered, 16)

        @block.tensor
        def _(t):
            t.wait_ge(c["ready"], c["n"])
            t.wait_ge(gathered, 16 * RB)
            t.wait_ge(inblock, 1)
            for b in range(RB):
                if b >= 2:
                    t.wait_ge(copied, b - 1)
                for x, a in enumerate((st[:, b, 2, :], st[:, b, 1, :], rels[:, b, :], rel[:, b, :], st[:, b, 3, :])):
                    ins = t.transpose(bank[2 * (b % 2) + x // 4][:, (x % 4) * P:(x % 4 + 1) * P], a, c["ident"][:])
                ins.then_inc(turned, 1)


def constants(nc, sb, sem):
    ident = sb("ident", [P, P])
    iota_i = sb("iota_i", [P, P], I32)
    iota = sb("iota", [P, P])
    pcol_i = sb("pcol_i", [P, 1], I32)
    pcol = sb("pcol", [P, 1])
    tile_no_i = sb("tile_no_i", [P, RB], I32)
    tile_no = sb("tile_no", [P, RB])
    ones = sb("ones", [P, P])
    zero = sb("zero", [P, 512])
    made, ready = sem("iotas_made"), sem("constants_ready")
    with nc.Block() as block:
        @block.gpsimd
        def _(g):
            g.memset(ident[:], 0.0).then_inc(made, 1)
            g.iota(iota_i[:], pattern=[[1, P]], base=0, channel_multiplier=0).then_inc(made, 1)
            g.iota(pcol_i[:], pattern=[[0, 1]], base=0, channel_multiplier=1).then_inc(made, 1)
            g.iota(tile_no_i[:], pattern=[[P, RB]], base=0, channel_multiplier=1).then_inc(made, 1)
            g.wait_ge(made, 4)
            g.affine_select(out=ident[:], in_=ident[:], compare_op=ALU.not_equal, fill=1.0, base=0,
                            pattern=[[-1, P]], channel_multiplier=1).then_inc(ready, 1)

        @block.vector
        def _(v):
            v.wait_ge(made, 4)
            v.tensor_copy(iota[:], iota_i[:]).then_inc(ready, 1)
            v.tensor_copy(pcol[:], pcol_i[:]).then_inc(ready, 1)
            v.tensor_copy(tile_no[:], tile_no_i[:]).then_inc(ready, 1)
            v.memset(ones[:], 1.0).then_inc(ready, 1)
            v.memset(zero[:], 0.0).then_inc(ready, 1)
    return dict(ident=ident, iota=iota, pcol=pcol, tile_no=tile_no, ones=ones, zero=zero, ready=ready, n=6)

EPS_LN = 1e-5


LT = 5


def layernorm_turned(nc, sem, name, bank, c, x_dram, xt, xn_dram=None):
    with ExitStack() as ctx:
        def sbt(nm, shape, dt=F32):
            return ctx.enter_context(nc.sbuf_tensor(f"{name}_{nm}", shape, dt))

        def pair(nm):
            return [sem(f"{name}_{nm}{s}") for s in range(2)]

        groups = NT // LT
        x = sbt("x", [P, 2, LT, D])
        xn = sbt("xn", [P, 2, LT, D])
        stats = sbt("stats", [P, 2, LT, 6])
        mv = sbt("mv", [P, 2, LT, 2])
        sd = sbt("sd", [P, 2, LT])
        rs = sbt("rs", [P, 2, LT])
        eps = sbt("eps", [P, 1])
        x_in, stats_made, var_ready, sd_ready, rs_ready, xn_ready, turned, taken, stored = (
            pair(n) for n in ("x_in", "stats", "var", "sd", "rs", "xn", "turned", "taken", "stored"))
        eps_ready = sem(f"{name}_eps")
        gate = sem(f"{name}_gate")
        block = ctx.enter_context(nc.Block())
        rows = x_dram.rearrange("(g t p) d -> g p t d", p=P, t=LT)

        @block.sync
        def _(sp):
            with sp.Fori(0, groups // 2) as i:
                for s in range(2):
                    sp.wait_ge(xn_ready[s], i * LT)
                    sp.dma_start(x[:, s], rows[bass.ds(i * 2 + s, 1)].rearrange("g p t d -> (g p) t d")
                                 ).then_inc(x_in[s], 16)

        @block.gpsimd
        def _(g):
            if xn_dram is not None:
                out = xn_dram.rearrange("(g t p) d -> g p t d", p=P, t=LT)
                with g.Fori(0, groups // 2) as i:
                    for s in range(2):
                        g.wait_ge(xn_ready[s], i * LT + LT)
                        g.dma_start(out[bass.ds(i * 2 + s, 1)].rearrange("g p t d -> (g p) t d"), xn[:, s]
                                    ).then_inc(stored[s], 16)
                for s in range(2):
                    g.wait_ge(stored[s], groups // 2 * 16)

        @block.vector
        def _(v):
            def statistics(i, s):
                wait_after(v, x_in, i, s, per=16)
                for n in range(LT):
                    v.bn_stats(stats[:, s, n, :], x[:, s, n, :]).then_inc(stats_made[s], 1)
                wait_after(v, stats_made, i, s, per=LT)
                wait_after(v, sd_ready, i, s, 2)
                wait_alone(v, gate)
                for n in range(LT):
                    v.bn_aggr(mv[:, s, n, :], stats[:, s, n, :]).then_inc(var_ready[s], 1)

            def normalise(i, s):
                wait_after(v, sd_ready, i, s)
                v.reciprocal(rs[:, s], sd[:, s]).then_inc(rs_ready[s], 1)
                wait_after(v, rs_ready, i, s)
                wait_after(v, turned, i, s, 2)
                if xn_dram is not None:
                    wait_after(v, stored, i, s, 2, per=16)
                for n in range(LT):
                    v.tensor_scalar(xn[:, s, n, :], x[:, s, n, :], mv[:, s, n, 0:1], rs[:, s, n:n + 1],
                                    ALU.subtract, ALU.mult).then_inc(xn_ready[s], 1)

            def take(i, s):
                wait_after(v, turned, i, s)
                for cc in range(2):
                    for n in range(3):
                        w = min(2, LT - 2 * n)
                        v.tensor_copy(xt[:, cc, bass.ds((i * 2 + s) * LT * P + 2 * n * P, w * P)]
                                      .rearrange("p (t n) -> p t n", n=P),
                                      bank[3 * s + n][:, 0:w * D].rearrange("p (t c n) -> p t c n", c=2, n=P)[:, :, cc, :]
                                      ).then_inc(taken[s], 1)

            v.memset(eps[:], EPS_LN).then_inc(eps_ready, 1)
            in_turns(v, groups, 2, ((1, statistics), (0, normalise), (-1, take)))

        @block.scalar
        def _(a):
            a.wait_ge(eps_ready, 1)
            with a.Fori(0, groups // 2) as i:
                for s in range(2):
                    a.wait_ge(var_ready[s], i * LT + LT)
                    a.wait_ge(rs_ready[s], i)
                    a.activation(sd[:, s, :], mv[:, s, :, 1], ACT.Sqrt, bias=eps[:]).then_inc(sd_ready[s], 1)

        @block.tensor
        def _(t):
            with t.Fori(0, groups // 2) as i:
                for s in range(2):
                    t.wait_ge(taken[s], i * 6)
                    for n in range(LT):
                        t.wait_ge(xn_ready[s], i * LT + n + 1)
                        for cc in range(2):
                            ins = t.transpose(bank[3 * s + n // 2][:, (n % 2) * D + cc * P:(n % 2) * D + (cc + 1) * P],
                                              xn[:, s, n, cc * P:(cc + 1) * P], c["ident"][:])
                    ins.then_inc(turned[s], 1)


def edge_node_tables(nc, sem, bank, c, xt, w, dram):
    with ExitStack() as ctx:
        def sbt(nm, shape, dt=F32):
            return ctx.enter_context(nc.sbuf_tensor(f"tb_{nm}", shape, dt))

        def pair(nm):
            return [sem(f"tb_{nm}{s}") for s in range(2)]

        wk = sbt("wk", [P, 2, 4, D])
        wq = sbt("wq", [P, 2, 4, D])
        wv = sbt("wv", [P, 2, 4, D])
        bd = sbt("bd", [P, 2, R, P])
        rt = sbt("rt", [P, 2, 2, R, P])
        pri = sbt("pri", [P, R * H])
        types = sbt("types", [P, 2, P], I32)
        mask = sbt("mask", [P, 4, P])
        xm = sbt("xm", [P, 2, 2, 4, P])
        kv = sbt("kv", [P, 2, 2, 2, P])
        q = sbt("q", [P, 2, D])
        tab = sbt("tab", [P, 2, R, 2 * D])
        w_in, w_made, w_turned = sem("tb_weights"), sem("tb_weights_made"), sem("tb_weights_turned")
        types_in, masked, q_made, kv_made, kv_taken = (pair(n) for n in ("types", "masked", "q_made", "kv_made", "kv_taken"))
        q_taken, table_made, low_taken, high_taken, stored = (
            pair(n) for n in ("q_taken", "table_made", "low_taken", "high_taken", "stored"))
        zeroed = sem("tb_zeroed")
        dve, act_sem, qstored = sem("tb_chain"), sem("tb_act"), sem("tb_qstored")
        LOADS = 6 + 1 + 8
        block = ctx.enter_context(nc.Block())
        table = dram["table"].rearrange("(r t p) n -> t p r n", r=R, p=P)

        @block.sync
        def _(sp):
            for dst_, src_ in ((wk, w["k"]), (wq, w["q"]), (wv, w["v"])):
                for cc in range(2):
                    sp.dma_start(dst_[:, cc], src_[:, cc * P:(cc + 1) * P, :].rearrange("t p o -> p t o")
                                 ).then_inc(w_in, 16)
            sp.dma_start(pri[:], w["pri"].rearrange("r h -> (r h)").unsqueeze(0).broadcast_to([P, R * H])
                         ).then_inc(w_in, 16)
            sp.wait_ge(zeroed, 2)
            for cc in range(2):
                for hh in range(2):
                    a, b = hh * DK, (hh + 1) * DK
                    sp.dma_start(bd[a:b, cc, :, a:b], w["att"][:, 2 * cc + hh].rearrange("r d e -> d r e")
                                 ).then_inc(w_in, 16)
                    sp.dma_start(rt[a:b, cc, 1, :, a:b], w["msg"][:, 2 * cc + hh].rearrange("r d e -> d r e")
                                 ).then_inc(w_in, 16)
            with sp.Fori(0, NT // 2) as i:
                for s in range(2):
                    sp.wait_ge(masked[s], i)
                    sp.dma_start(types[:, s, :], dram["types"][bass.ds(i * 2 * P + s * P, P)].unsqueeze(0)
                                 .broadcast_to([P, P])).then_inc(types_in[s], 16)

        @block.gpsimd
        def _(g):
            with g.Fori(0, NT // 2) as i:
                for s in range(2):
                    g.wait_ge(q_taken[s], i + 1)
                    g.dma_start(dram["q"][bass.ds(i * 2 * P + s * P, P), :], q[:, s, :]).then_inc(stored[s], 16)
                    g.wait_ge(low_taken[s], (i + 1) * 4)
                    g.wait_ge(high_taken[s], (i + 1) * 4)
                    g.dma_start(table[bass.ds(i * 2 + s, 1)].rearrange("t p r n -> (t p) r n"), tab[:, s, :, :]
                                ).then_inc(stored[s], 16)
            for s in range(2):
                g.wait_ge(stored[s], NT // 2 * 32)

        @block.vector
        def _(v):
            ch = Chain(v, dve)
            v.memset(bd[:], 0.0).then_inc(zeroed, 1)
            v.memset(rt[:], 0.0).then_inc(zeroed, 1)
            v.wait_ge(w_in, 16 * LOADS)
            for cc in range(2):
                for half in range(2):
                    b = cc * 2 + half
                    v.wait_ge(w_turned, b + 1)
                    rr = slice(half * 4, half * 4 + 4)
                    ch.link(v.tensor_scalar(rt[:, cc, 0, rr, :], bank[b][:].rearrange("p (r n) -> p r n", r=4),
                                            float(DK) ** -0.5, None, ALU.mult))
                    for hh in range(2):
                        o = rt[:, cc, 0, rr, hh * DK:(hh + 1) * DK]
                        ph = pri[:].rearrange("p (r h) -> p r h", h=H)[:, rr, 2 * cc + hh:2 * cc + hh + 1]
                        v.tensor_tensor(o, o, ph.broadcast_to([P, 4, DK]), ALU.mult).then_inc(w_made, 1)
            with v.Fori(0, NT // 2) as i:
                ch.enter(i, 2)
                for s in range(2):
                    v.wait_ge(types_in[s], i * 16 + 16)
                    ch.link(v.tensor_tensor(mask[:], types[:, s, :].unsqueeze(1).broadcast_to([P, 4, P]),
                                            c["iota"][:, 0:4].unsqueeze(2).broadcast_to([P, 4, P]), ALU.is_equal))
                    v.wait_ge(kv_made[s], i)
                    v.tensor_tensor(xm[:, s], xt[:, :, bass.ds(i * 2 * P + s * P, P)].unsqueeze(2)
                                    .broadcast_to([P, 2, 4, P]), mask[:].unsqueeze(1).broadcast_to([P, 2, 4, P]),
                                    ALU.mult).then_inc(masked[s], 1)
                    v.wait_ge(kv_made[s], i + 1)
                    v.tensor_copy(kv[:, s].rearrange("p a c n -> p (a c n)"), bank[1][:]).then_inc(kv_taken[s], 1)
                    v.wait_ge(stored[s], i * 32)
                    for n in range(4):
                        v.wait_ge(table_made[s], i * 8 + 2 * n + 1)
                        kind, cc = n // 2, n % 2
                        v.tensor_copy(tab[:, s, 0:4, kind * D + cc * P:kind * D + cc * P + P],
                                      bank[2 + (2 * n) % 6][:].rearrange("p (r n) -> p r n", r=4)
                                      ).then_inc(low_taken[s], 1)
                ch.leave(NT // 2)

        @block.scalar
        def _(a):
            with a.Fori(0, NT // 2) as i:
                for s in range(2):
                    a.wait_ge(stored[s], i * 32)
                    a.wait_ge(q_made[s], i + 1)
                    a.activation(q[:, s, :], bank[0][:, 0:D], ACT.Copy).then_inc(q_taken[s], 1)
                    for n in range(4):
                        a.wait_ge(table_made[s], i * 8 + 2 * n + 2)
                        kind, cc = n // 2, n % 2
                        a.activation(tab[:, s, 4:8, kind * D + cc * P:kind * D + cc * P + P],
                                     bank[2 + (2 * n + 1) % 6][:].rearrange("p (r n) -> p r n", r=4), ACT.Copy
                                     ).then_inc(high_taken[s], 1)

        @block.tensor
        def _(t):
            t.wait_ge(w_in, 16 * LOADS)
            for cc in range(2):
                for half in range(2):
                    for r in range(4):
                        ins = t.transpose(bank[cc * 2 + half][:, r * P:(r + 1) * P], bd[:, cc, half * 4 + r, :], c["ident"][:])
                    ins.then_inc(w_turned, 1)
            t.wait_ge(w_made, 8)
            with t.Fori(0, NT // 2) as i:
                for s in range(2):
                    t.wait_ge(masked[s], i + 1)
                    t.wait_ge(q_taken[1 - s], i + s)
                    for n in range(8):
                        ins = t.matmul(bank[0][:, 0:D], xm[:, s, n // 4, n % 4, :], wq[:, n // 4, n % 4, :],
                                       start=n == 0, stop=n == 7)
                    ins.then_inc(q_made[s], 1)
                    t.wait_ge(kv_taken[1 - s], i + s)
                    for kind, ww in enumerate((wk, wv)):
                        for o in range(2):
                            for n in range(8):
                                ins = t.matmul(bank[1][:, (kind * 2 + o) * P:(kind * 2 + o + 1) * P],
                                               ww[:, n // 4, n % 4, o * P:(o + 1) * P], xm[:, s, n // 4, n % 4, :],
                                               start=n == 0, stop=n == 7)
                    ins.then_inc(kv_made[s], 1)
                    t.wait_ge(kv_taken[s], i + 1)
                    for m in range(8):
                        n, half = m // 2, m % 2
                        kind, cc = n // 2, n % 2
                        taken = (low_taken, high_taken)[half]
                        if m < 6:
                            t.wait_ge(taken[1 - s], (i + s) * 4)
                        else:
                            t.wait_ge(taken[s], i * 4 + 1)
                        t.matmul(bank[2 + m % 6][:], kv[:, s, kind, cc, :],
                                 rt[:, cc, kind, half * 4:half * 4 + 4, :].rearrange("p r n -> p (r n)"),
                                 start=True, stop=True).then_inc(table_made[s], 1)

SLOTS = 3
KC = D - C_V


PACK = 4
BITS = 6


def blocks_of(eng, packed, k):
    words = [eng.value_load(packed[0:1, bass.ds(k * (G // PACK) + m, 1)], min_val=0, max_val=2 ** (PACK * BITS) - 1)
             for m in range(G // PACK)]
    return [((words[n // PACK] >> (n % PACK * BITS)) & (2 ** BITS - 1)).with_bounds(min_val=0, max_val=NB - 1)
            for n in range(G)]


def pack_blocks(v, ch, blocks, packed_f, packed):
    four = blocks[:].rearrange("p (m n) -> p m n", n=PACK)
    ch.link(v.tensor_copy(packed_f[:], four[:, :, PACK - 1]))
    for n in range(PACK - 2, -1, -1):
        ch.link(v.scalar_tensor_tensor(packed_f[:], packed_f[:], float(2 ** BITS), four[:, :, n], ALU.mult, ALU.add))
    ch.link(v.tensor_copy(packed[:], packed_f[:]))


def attention_edges(nc, sem, psum, bank, c, dram):
    with ExitStack() as ctx:
        def sbt(nm, shape, dt=F32):
            return ctx.enter_context(nc.sbuf_tensor(f"ae_{nm}", shape, dt))

        def slots(nm):
            return [sem(f"ae_{nm}{s}") for s in range(SLOTS)]

        qb = sbt("q", [P, NB, D])
        acc = sbt("acc", [P, NB, CW])
        kv = sbt("kv", [P, SLOTS, G, 2 * D])
        index = sbt("index", [P, SLOTS, G])
        col = sbt("col", [P, SLOTS, 3, G])
        mk = sbt("mask", [G * H, SLOTS, P + 1])
        oht = sbt("node_hot", [P, SLOTS, G * P])
        ohs = sbt("edge_hot", [P, G, P])
        sc = sbt("scores", [P, SLOTS, G * H])
        fwd = sbt("fwd", [G * H, P])
        mx = sbt("max", [G * H, P])
        diff = sbt("diff", [G * H, P])
        step_sums = sbt("step_sums", [P, G, CW])
        blocks = sbt("blocks", [1, T], I32)
        packed_f, packed = sbt("packed_f", [1, T // PACK]), sbt("packed", [1, T // PACK], I32)
        less_p = sbt("less_partition", [P, 1])
        q_in, blocks_in, cleared, place_ready = (sem(f"ae_{n}") for n in ("q_in", "blocks_in", "cleared", "place_ready"))
        pack_chain, packed_ready = sem("ae_pack_chain"), sem("ae_packed_ready")
        index_in, rows_in, loaded, gathered, node_hot, expanded, scored, turned = (
            slots(n) for n in ("index_in", "rows_in", "loaded", "gathered", "node_hot", "expanded", "scored", "turned"))
        maxed, back, exps, weighted, edge_hot, marked = (
            slots(n) for n in ("maxed", "back", "exps", "weighted", "edge_hot", "marked"))
        multiplied, swept = slots("multiplied"), slots("swept")
        sum_made, sum_added, sum_copied = (sem(f"ae_{n}") for n in ("sum_made", "sum_added", "sum_copied"))
        carry_stored, acc_stored, gate = sem("ae_carry_stored"), sem("ae_acc_stored"), sem("ae_gate")
        t_gate = sem("ae_tensor_gate")
        block = ctx.enter_context(nc.Block())
        ITER = GROUPS // SLOTS

        @block.sync
        def _(sp):
            sp.dma_start(blocks[:], dram["blocks"].unsqueeze(0)).then_inc(blocks_in, 16)
            for b in range(NB):
                sp.dma_start(qb[:, b, :], dram["q"][b * BW:b * BW + P, :]).then_inc(q_in, 16)
            with sp.Fori(0, ITER) as i:
                for s in range(SLOTS):
                    k = i * SLOTS + s
                    sp.wait_ge(gathered[s], i * 16 * G)
                    sp.dma_start(index[:, s], dram["cols"][:, bass.ds(k, 1), 0].rearrange("p k g -> p (k g)")
                                 ).then_inc(index_in[s], 16)
                    sp.wait_ge(expanded[s], i)
                    sp.dma_start(oht[:, s, :], dram["rel_rows"][bass.ds(k * G, G)].rearrange("g n -> (g n)")
                                 .unsqueeze(0).broadcast_to([P, G * P])).then_inc(rows_in[s], 16)
                    sp.wait_ge(weighted[s], i * 2)
                    sp.wait_ge(edge_hot[s], i)
                    sp.dma_start(col[:, s], dram["cols"][:, bass.ds(k, 1), 2:5].rearrange("p k c g -> p (k c) g")
                                 ).then_inc(loaded[s], 16)
                    sp.dma_start(mk[:, s, :], dram["mask"][bass.ds(k * G, G)].rearrange("g h n -> (g h) n")
                                 ).then_inc(loaded[s], 16)
            sp.wait_ge(sum_added, GROUPS * G)
            for a, b in ((0, 112), (112, BW)):
                sp.dma_start(dram["sums"][0:NB * BW].rearrange("(b p) n -> p b n", p=BW)[a:b], acc[a:b]).then_inc(acc_stored, 16)
            sp.wait_ge(acc_stored, 32)

        @block.gpsimd
        def _(g):
            def gather(i, s, n):
                g.indirect_dma_start(out=kv[:, s, n, :], out_offset=None, in_=dram["table"],
                                     in_offset=bass.IndirectOffsetOnAxis(ap=index[:, s, n:n + 1].bitcast(U32), axis=0)
                                     ).then_inc(gathered[s], 16)

            g.memset(acc[:], 0.0).then_inc(cleared, 1)
            for s in range(SLOTS):
                g.wait_ge(index_in[s], 16)
                for n in range(G):
                    gather(0, s, n)
            with g.Fori(1, ITER) as i:
                for s in range(SLOTS):
                    g.wait_ge(index_in[s], i * 16 + 16)
                    for n in range(G):
                        g.wait_ge(sum_made, ((i - 1) * SLOTS + s) * G + n + 1)
                        wait_alone(g, gate)
                        gather(i, s, n)

        @block.vector
        def _(v):
            def turn(i, s, scores, rest, adds):
                iz, sz = i + (s + 1) // SLOTS, (s + 1) % SLOTS
                ia, sa = i + (s - 1) // SLOTS, (s - 1) % SLOTS
                if adds:
                    ka = ia * SLOTS + sa
                    at = blocks_of(v, packed, ka)

                def add(n):
                    if not adds:
                        return
                    v.wait_ge(sum_copied, ka * G + n + 1)
                    if n or not isinstance(ka, int) or ka:
                        v.wait_ge(sum_added, ka * G + n)
                    o = acc[:, bass.ds(at[n], 1), :].rearrange("p b n -> p (b n)")
                    v.tensor_tensor(o, o, step_sums[:, n, :], ALU.add).then_inc(sum_added, 1)

                if scores:
                    wait_after(v, gathered, iz, sz, per=16 * G)
                    wait_after(v, expanded, iz, sz)
                    k_ = kv[:, sz, :, 0:D]
                    v.tensor_tensor(k_, k_, psum[:, 0:4, :].rearrange("p b (t d) -> p (b t) d", d=D),
                                    ALU.mult).then_inc(multiplied[sz], 1)
                add(0)
                if rest:
                    wait_after(v, turned, i, s)
                    wait_after(v, loaded, i, s, per=32)
                    wait_after(v, back, i, s, 1)
                    st = bank[6][0:G * H, 0:P]
                    v.tensor_tensor_scan(fwd[:], mk[:, s, 0:P], st, NEG, ALU.add, ALU.max).then_inc(swept[s], 1)
                add(1)
                if rest:
                    wait_after(v, swept, i, s, per=2, less=1)
                    v.tensor_tensor_scan(mx[:, ::-1], mk[:, s, 1:P + 1][:, ::-1], fwd[:, ::-1], NEG, ALU.add, ALU.max
                                         ).then_inc(swept[s], 1)
                add(2)
                if rest:
                    wait_after(v, swept, i, s, per=2)
                    v.tensor_tensor(diff[:], st, mx[:], ALU.subtract).then_inc(maxed[s], 1)
                add(3)
                if scores:
                    wait_after(v, multiplied, iz, sz)
                    wait_after(v, turned, iz, sz, SLOTS)
                    v.tensor_reduce(sc[:, sz, :], kv[:, sz, :, 0:D].rearrange("p g (h d) -> p g h d", d=DK), AX.X, ALU.add
                                    ).then_inc(scored[sz], 1)
                add(4)
                if rest:
                    wait_after(v, back, i, s)
                    v.tensor_tensor(kv[:, s, :, KC + C_M:KC + C_EX],
                                    bank[6][:, P:P + G * H].rearrange("p (g h) -> p g h", h=H),
                                    col[:, s, 2, :].unsqueeze(2).broadcast_to([P, G, H]), ALU.mult).then_inc(weighted[s], 1)
                add(5)
                if rest:
                    first = (i * SLOTS + s) * G
                    if not (isinstance(first, int) and first == 0):
                        v.wait_ge(sum_made, first)
                    v.tensor_tensor(ohs[:], c["iota"][:].unsqueeze(1).broadcast_to([P, G, P]),
                                    col[:, s, 0, :].unsqueeze(2).broadcast_to([P, G, P]), ALU.is_equal
                                    ).then_inc(edge_hot[s], 1)
                add(6)
                if rest:
                    wait_after(v, exps, i, s)
                    vv = kv[:, s, :, D:2 * D].rearrange("p g (h d) -> p g h d", h=H)
                    v.tensor_tensor(vv, vv, kv[:, s, :, KC + C_EX:KC + C_V].unsqueeze(3).broadcast_to([P, G, H, DK]),
                                    ALU.mult).then_inc(weighted[s], 1)
                add(7)

            ch = Chain(v, pack_chain)
            v.tensor_scalar(less_p[:], c["pcol"][:], -1.0, None, ALU.mult).then_inc(place_ready, 1)
            v.wait_ge(cleared, 1)
            v.wait_ge(blocks_in, 16)
            pack_blocks(v, ch, blocks, packed_f, packed)
            v.tensor_copy(packed_f[:, 0:1], packed_f[:, 0:1]).then_inc(packed_ready, 1)
            turn(-1, SLOTS - 1, True, False, False)
            for s in range(SLOTS):
                turn(0, s, True, True, s > 0)
            with v.Fori(1, ITER - 1) as i:
                for s in range(SLOTS):
                    turn(i, s, True, True, True)
            for s in range(SLOTS):
                turn(ITER - 1, s, s + 1 < SLOTS, True, True)
            turn(ITER, 0, False, False, True)

        @block.scalar
        def _(a):
            def copy(i, s):
                k = i * SLOTS + s
                if not isinstance(k, int) or k:
                    a.wait_ge(sum_added, k * G)
                    a.wait_ge(carry_stored, k * 16)
                for n in range(G):
                    a.wait_ge(sum_made, k * G + n + 1)
                    a.activation(step_sums[:, n, :], bank[4 + n % 2][:, 0:CW], ACT.Copy).then_inc(sum_copied, 1)

            def exponents(i, s):
                wait_after(a, back, i, s)
                a.activation(kv[:, s, :, KC + C_EX:KC + C_V], bank[7][:, 0:G * H].rearrange("p (g h) -> p g h", h=H),
                             ACT.Exp).then_inc(exps[s], 1)

            def store(i, s):
                k = i * SLOTS + s
                a.wait_ge(sum_copied, k * G + G)
                a.dma_start(dram["carry"][bass.ds(k * G, G)].rearrange("g n -> (g n)").unsqueeze(0),
                            step_sums[P - 1:P, :, :].rearrange("p g n -> p (g n)")).then_inc(carry_stored, 16)

            def mark(i, s):
                wait_after(a, scored, i, s)
                wait_after(a, loaded, i, s, per=32)
                a.activation(kv[:, s, :, KC + C_LAST], col[:, s, 2, :], ACT.Copy).then_inc(marked[s], 1)
                a.activation(kv[:, s, :, KC + C_CNT], c["ones"][:, 0:G], ACT.Copy).then_inc(marked[s], 1)

            def nodes(i, s):
                wait_after(a, rows_in, i, s, per=16)
                a.activation(oht[:, s, :], oht[:, s, :], ACT.Square, bias=less_p[:]).then_inc(node_hot[s], 1)
                wait_after(a, node_hot, i, s, per=2, less=1)
                a.activation(oht[:, s, :], oht[:, s, :], ACT.Relu, bias=c["ones"][:, 0:1], scale=-1.0
                             ).then_inc(node_hot[s], 1)

            a.wait_ge(place_ready, 1)
            in_turns(a, GROUPS, SLOTS, ((-1, copy), (0, exponents), (-1, store), (1, mark), (3, nodes)))
            a.wait_ge(carry_stored, GROUPS * 16)

        @block.tensor
        def _(t):
            def expand(i, s):
                k = i * SLOTS + s
                at = blocks_of(t, packed, k)
                wait_after(t, node_hot, i, s, per=2)
                wait_after(t, multiplied, i, s, 1)
                for n in range(G):
                    ins = t.matmul(bank[n // 2][:, (n % 2) * D:(n % 2 + 1) * D], oht[:, s, n * P:(n + 1) * P],
                                   qb[:, bass.ds(at[n], 1), :].rearrange("p b d -> p (b d)"), start=True, stop=True)
                ins.then_inc(expanded[s], 1)

            def turn(i, s):
                wait_after(t, scored, i, s)
                wait_after(t, maxed, i, s, 1)
                wait_after(t, weighted, i, s, 1, per=2, less=1)
                t.transpose(bank[6][0:G * H, 0:P], sc[:, s, :], c["ident"][:]).then_inc(turned[s], 1)

            def turn_back(i, s):
                wait_after(t, maxed, i, s)
                wait_after(t, exps, i, s, 1)
                wait_alone(t, t_gate)
                t.transpose(bank[7][:, 0:G * H], diff[:], c["ident"][0:G * H, 0:G * H])
                t.transpose(bank[6][:, P:P + G * H], mx[:], c["ident"][0:G * H, 0:G * H]).then_inc(back[s], 1)

            def total(i, s):
                k = i * SLOTS + s
                wait_after(t, marked, i, s, per=2)
                wait_after(t, edge_hot, i, s)
                wait_after(t, exps, i, s)
                wait_after(t, weighted, i, s, per=2)
                for n in range(G):
                    if not isinstance(k, int) or k * G + n > 1:
                        t.wait_ge(sum_copied, k * G + n - 1)
                    t.matmul(bank[4 + n % 2][:, 0:CW], ohs[:, n, :], kv[:, s, n, KC:2 * D], start=True, stop=True
                             ).then_inc(sum_made, 1)

            t.wait_ge(q_in, 16 * NB)
            t.wait_ge(packed_ready, 1)
            in_turns(t, GROUPS, SLOTS, ((0, turn), (-1, total), (0, turn_back), (2, expand)))

BIG = float(1 << 24)
TOP = NB * BW - 1


def merge_carried(nc, sem, psum, bank, c, dram):
    with ExitStack() as ctx:
        def sbt(nm, shape, dt=F32):
            return ctx.enter_context(nc.sbuf_tensor(f"mc_{nm}", shape, dt))

        row = sbt("row", [P, CW])
        keyc, keyr = sbt("keyc", [P, 1]), sbt("keyr", [P, P])
        eq, pen, tri, up = sbt("eq", [P, P]), sbt("pen", [P, P]), sbt("tri", [P, P]), sbt("up", [P, P])
        later, valid, gi_f, si_f = sbt("later", [P, 1]), sbt("valid", [P, 1]), sbt("gi_f", [P, 1]), sbt("si_f", [P, 1])
        gi, si = sbt("gi", [P, 1], I32), sbt("si", [P, 1], I32)
        off, meff, mt, x4 = sbt("off", [P, 1]), sbt("meff", [P, H]), sbt("mt", [H, P]), sbt("x4", [P, H, P])
        ms, dw, w = sbt("ms", [P, H]), sbt("dw", [P, H]), sbt("w", [P, H])
        node, mm, mn = sbt("node", [P, CW]), sbt("mm", [P, H]), sbt("mn", [P, H])
        dab, ab, add = sbt("dab", [P, 2, H]), sbt("ab", [P, 2, H]), sbt("add", [P, CW])
        zrow = sbt("zrow", [NP - NB * BW, CW])
        (rows_in, keys_in, zeroed, zstored, dve, indexed, node_in, merged, scattered, tri_made) = (
            sem(f"mc_{n}") for n in ("rows_in", "keys_in", "zeroed", "zstored", "dve", "indexed", "node_in", "merged",
                                     "scattered", "tri_made"))
        m_ready, m_turned, mt_ready, m_spread, dw_ready, w_ready, scaled, added, dab_ready, ab_ready = (
            sem(f"mc_{n}") for n in ("m_ready", "m_turned", "mt_ready", "m_spread", "dw_ready", "w_ready", "scaled",
                                     "added", "dab_ready", "ab_ready"))
        gate = sem("mc_gate")
        block = ctx.enter_context(nc.Block())
        assert T - GROUPS * G <= NP - NB * BW

        @block.sync
        def _(sp):
            sp.wait_ge(zeroed, 1)
            sp.dma_start(dram["carry"][GROUPS * G:T, :], zrow[0:T - GROUPS * G]).then_inc(zstored, 16)
            sp.dma_start(dram["sums"][NB * BW:NP, :], zrow[:]).then_inc(zstored, 16)
            sp.wait_ge(zstored, 32)
            with sp.Fori(0, RB) as b:
                sp.wait_ge(merged, b)
                sp.dma_start(row[:], dram["carry"][bass.ds(b * P, P), :]).then_inc(rows_in, 16)
                sp.dma_start(keyc[:], dram["keys"][bass.ds(b * P, P)].unsqueeze(1), allow_slow_non_contiguous=True
                             ).then_inc(keys_in, 16)
                sp.dma_start(keyr[:], dram["keys"][bass.ds(b * P, P)].unsqueeze(0).broadcast_to([P, P])
                             ).then_inc(keys_in, 16)

        @block.gpsimd
        def _(g):
            g.memset(pen[:], 1.0).then_inc(tri_made, 1)
            g.wait_ge(tri_made, 1)
            g.affine_select(out=tri[:], in_=pen[:], compare_op=ALU.is_gt, fill=0.0, base=0, pattern=[[1, P]],
                            channel_multiplier=-1).then_inc(tri_made, 1)
            g.memset(zrow[:], 0.0).then_inc(zeroed, 1)
            with g.Fori(0, RB) as b:
                g.wait_ge(indexed, b + 1)
                g.wait_ge(scattered, b * 16)
                wait_alone(g, gate)
                g.indirect_dma_start(out=node[:], out_offset=None, in_=dram["sums"],
                                     in_offset=bass.IndirectOffsetOnAxis(ap=gi[:].bitcast(U32), axis=0)).then_inc(node_in, 16)
                g.wait_ge(merged, b + 1)
                wait_alone(g, gate)
                g.indirect_dma_start(out=dram["sums"], in_=add[:], in_offset=None,
                                     out_offset=bass.IndirectOffsetOnAxis(ap=si[:].bitcast(U32), axis=0),
                                     bounds_check=TOP, oob_is_err=False).then_inc(scattered, 16)
            g.wait_ge(scattered, RB * 16)

        @block.vector
        def _(v):
            ch = Chain(v, dve)
            v.wait_ge(tri_made, 2)
            with v.Fori(0, RB) as b:
                ch.enter(b, 23)
                v.wait_ge(keys_in, b * 32 + 32)
                v.wait_ge(scattered, b * 16)
                ch.done(v.tensor_scalar(eq[:], keyr[:], keyc[:], None, ALU.is_equal))
                ch.link(v.tensor_scalar(valid[:], keyc[:], 0.0, None, ALU.is_ge))
                ch.done(v.tensor_scalar(pen[:], eq[:], -1.0, -NEG, ALU.add, ALU.mult))
                ch.done(v.tensor_tensor(up[:], eq[:], tri[:], ALU.mult))
                ch.done(v.scalar_tensor_tensor(gi_f[:], keyc[:], float(-TOP), valid[:], ALU.add, ALU.mult))
                ch.link(v.tensor_scalar(si_f[:], valid[:], -BIG, BIG, ALU.mult, ALU.add))
                ch.done(v.tensor_scalar(gi[:], gi_f[:], float(TOP), None, ALU.add))
                ch.link(v.tensor_reduce(later[:], up[:], AX.X, ALU.max))
                ch.link(v.scalar_tensor_tensor(si_f[:], later[:], BIG, si_f[:], ALU.mult, ALU.max))
                v.tensor_scalar(si[:], si_f[:], keyc[:], 0.0, ALU.add, ALU.max).then_inc(indexed, 1)
                v.wait_ge(rows_in, b * 16 + 16)
                ch.link(v.tensor_scalar(off[:], row[:, C_LAST:C_LAST + 1], -1.0, -NEG, ALU.add, ALU.mult))
                v.tensor_scalar(meff[:], row[:, C_M:C_EX], off[:], None, ALU.add).then_inc(m_ready, 1)
                v.wait_ge(m_turned, b + 1)
                v.tensor_copy(mt[:], bank[0][0:H, 0:P]).then_inc(mt_ready, 1)
                v.wait_ge(m_spread, b + 1)
                ch.link(v.tensor_tensor(x4[:], bank[1].rearrange("p (h n) -> p h n", h=H),
                                        pen[:].unsqueeze(1).broadcast_to([P, H, P]), ALU.add))
                ch.link(v.tensor_reduce(ms[:], x4[:], AX.X, ALU.max))
                v.wait_ge(m_ready, b + 1)
                v.tensor_tensor(dw[:], meff[:], ms[:], ALU.subtract).then_inc(dw_ready, 1)
                v.wait_ge(w_ready, b + 1)
                v.tensor_tensor(row[:, C_EX:C_V], row[:, C_EX:C_V], w[:], ALU.mult).then_inc(scaled, 1)
                rv = row[:, C_V:CW].rearrange("p (h d) -> p h d", h=H)
                v.tensor_tensor(rv, rv, w[:].unsqueeze(2).broadcast_to([P, H, DK]), ALU.mult).then_inc(scaled, 1)
                v.wait_ge(node_in, b * 16 + 16)
                ch.link(v.tensor_scalar(off[:], node[:, C_LAST:C_LAST + 1], -1.0, -NEG, ALU.add, ALU.mult))
                ch.link(v.tensor_scalar(mm[:], node[:, C_M:C_EX], off[:], None, ALU.add))
                ch.link(v.tensor_tensor(mn[:], mm[:], ms[:], ALU.max))
                ch.done(v.tensor_copy(node[:, C_M:C_EX], mn[:]))
                v.tensor_tensor(dab[:, 0, :], mm[:], mn[:], ALU.subtract).then_inc(dab_ready, 1)
                v.tensor_tensor(dab[:, 1, :], ms[:], mn[:], ALU.subtract).then_inc(dab_ready, 1)
                v.wait_ge(ab_ready, b + 1)
                v.wait_ge(added, b + 1)
                nv, av = (x[:, C_V:CW].rearrange("p (h d) -> p h d", h=H) for x in (node, add))
                sv = bank[2][:, C_V:CW].rearrange("p (h d) -> p h d", h=H)
                ch.done(v.tensor_tensor(node[:, C_EX:C_V], node[:, C_EX:C_V], ab[:, 0, :], ALU.mult))
                ch.done(v.tensor_tensor(nv, nv, ab[:, 0, :].unsqueeze(2).broadcast_to([P, H, DK]), ALU.mult))
                ch.done(v.tensor_tensor(add[:, C_EX:C_V], bank[2][:, C_EX:C_V], ab[:, 1, :], ALU.mult))
                ch.done(v.tensor_tensor(av, sv, ab[:, 1, :].unsqueeze(2).broadcast_to([P, H, DK]), ALU.mult))
                ch.done(v.tensor_copy(add[:, C_CNT:C_CNT + 1], bank[2][:, C_CNT:C_CNT + 1]))
                ch.link(v.memset(add[:, C_LAST:C_EX], 0.0))
                ch.link(v.tensor_tensor(add[:], add[:], node[:], ALU.add))
                v.tensor_scalar(add[:, C_LAST:C_LAST + 1], add[:, C_LAST:C_LAST + 1], 1.0, None, ALU.min).then_inc(merged, 1)
                ch.leave(RB)

        @block.scalar
        def _(a):
            with a.Fori(0, RB) as b:
                a.wait_ge(dw_ready, b + 1)
                a.activation(w[:], dw[:], ACT.Exp).then_inc(w_ready, 1)
                a.wait_ge(dab_ready, b * 2 + 2)
                a.activation(ab[:], dab[:], ACT.Exp).then_inc(ab_ready, 1)

        @block.tensor
        def _(t):
            with t.Fori(0, RB) as b:
                t.wait_ge(m_ready, b + 1)
                t.transpose(bank[0][0:H, 0:P], meff[:], c["ident"][:]).then_inc(m_turned, 1)
                t.wait_ge(mt_ready, b + 1)
                for h in range(H):
                    ins = t.matmul(bank[1][:, h * P:(h + 1) * P], c["ident"][0:H, h:h + 1].broadcast_to([H, P]), mt[:],
                                   start=True, stop=True)
                ins.then_inc(m_spread, 1)
                t.wait_ge(scaled, b * 2 + 2)
                t.matmul(bank[2][:, 0:CW], eq[:], row[:], start=True, stop=True).then_inc(added, 1)

EPS_IN = 1e-5
MH = 8
NI = NT // 2


def mix0_matrix(nc, sem, psum, bank, c, xt, wqkv, wout, wmix):
    INNER = MH * DK
    with ExitStack() as ctx:
        def sbt(nm, shape, dt=F32):
            return ctx.enter_context(nc.sbuf_tensor(f"m0_{nm}", shape, dt))

        def sems(*names):
            return (sem(f"m0_{n}") for n in names)

        w = sbt("w", [P, 12, D])
        wt = sbt("wt", [P, 2, 2 * INNER])
        wo = sbt("wo", [P, 2, INNER])
        wot = sbt("wot", [P, 4, D])
        xs = sbt("xs", [P, 2, 2, P])
        mean = sbt("mean", [P, 2, 16])
        cen = sbt("cen", [P, 2, 16, DK])
        sq = sbt("sq", [P, 2, 16, DK])
        ss = sbt("ss", [P, 2, 16])
        sd = sbt("sd", [P, 2, 16])
        rs = sbt("rs", [P, 2, 16])
        eps = sbt("eps", [P, 1])
        dots = sbt("dots", [P, 4, P])
        m2 = sbt("m2", [P, 4, D])
        w_in, turned, taken, eps_ready, dve, xs_ready, projected, centred, squared, var_ready, sd_ready = sems(
            "w_in", "turned", "taken", "eps_ready", "dve", "xs_ready", "projected", "centred", "squared", "var_ready", "sd_ready")
        normed, summed, dots_ready, m2_made, m2_ready, mix_made, mix_ready = sems(
            "normed", "summed", "dots_ready", "m2_made", "m2_ready", "mix_made", "mix_ready")
        block = ctx.enter_context(nc.Block())

        @block.sync
        def _(sp):
            sp.dma_start(w[:], wqkv.rearrange("(f p) c -> p f c", p=P)).then_inc(w_in, 16)
            sp.dma_start(wo[:], wout.rearrange("(g p) e -> p g e", p=P)).then_inc(w_in, 16)

        @block.tensor
        def _(t):
            t.wait_ge(w_in, 32)
            for n in range(4):
                for j in range(4):
                    ins = t.transpose(bank[n][:, j * P:(j + 1) * P], w[:, 4 + 2 * n + j // 2, (j % 2) * P:(j % 2 + 1) * P],
                                      c["ident"][:])
                ins.then_inc(turned, 1)
            for n in range(2):
                for j in range(4):
                    ins = t.transpose(bank[4 + n][:, j * P:(j + 1) * P],
                                      wo[:, j % 2, (2 * n + j // 2) * P:(2 * n + j // 2 + 1) * P], c["ident"][:])
                ins.then_inc(turned, 1)
            t.wait_ge(taken, 6)
            t.matmul(bank[6], c["zero"][:, 0:P], c["zero"][:], start=True, stop=False, skip_group_check=True)

            def project(i, s):
                t.wait_ge(xs_ready, i * 2 + s + 1)
                t.wait_ge(centred, i * 2)
                for half in range(2):
                    for cc in range(2):
                        ins = t.matmul(bank[2 * s + half], xs[:, s, cc, :], wt[:, cc, half * INNER:(half + 1) * INNER],
                                       start=cc == 0, stop=cc == 1)
                ins.then_inc(projected, 1)

            def add(i, s):
                t.wait_ge(normed, i * 2 + s + 1)
                for j in range(4):
                    k_, v_ = (cen[:, s, x + 2 * j:x + 2 * j + 2, :].rearrange("p h d -> p (h d)") for x in (0, MH))
                    ins = t.matmul(bank[6][:, j * P:(j + 1) * P], v_, k_, start=False, stop=False, skip_group_check=True)
                ins.then_inc(summed, 1)

            with t.Fori(0, NI) as i:
                for s in range(2):
                    project(i, s)
                for s in range(2):
                    add(i, s)
            t.wait_ge(dots_ready, 1)
            for j in range(4):
                ins = t.matmul(bank[j][:, 0:D], dots[:, j, :], wot[:, j, :], start=True, stop=True)
            ins.then_inc(m2_made, 1)
            t.wait_ge(m2_ready, 1)
            for cc in range(2):
                for j in range(4):
                    ins = t.matmul(bank[4][:, cc * D:(cc + 1) * D], w[:, j, cc * P:(cc + 1) * P], m2[:, j, :],
                                   start=j == 0, stop=j == 3)
            ins.then_inc(mix_made, 1)

        @block.scalar
        def _(a):
            a.wait_ge(eps_ready, 1)
            with a.Fori(0, NI) as i:
                for s in range(2):
                    k = i * 2 + s
                    a.wait_ge(var_ready, k + 1)
                    a.activation(sd[:, s, :], ss[:, s, :], ACT.Sqrt, bias=eps[:], scale=1.0 / DK).then_inc(sd_ready, 1)

        @block.gpsimd
        def _(g):
            with g.Fori(0, NI) as i:
                for s in range(2):
                    k = i * 2 + s
                    g.wait_ge(projected, i * 2)
                    g.tensor_copy(xs[:, s], xt[:, :, bass.ds(k * P, P)]).then_inc(xs_ready, 1)
                for s in range(2):
                    g.wait_ge(centred, i * 2 + s + 1)
                    g.tensor_tensor(sq[:, s], cen[:, s], cen[:, s], ALU.mult).then_inc(squared, 1)

        @block.vector
        def _(v):
            ch = Chain(v, dve)
            v.memset(eps[:], EPS_IN).then_inc(eps_ready, 1)
            for n in range(4):
                v.wait_ge(turned, n + 1)
                v.tensor_copy(wt[:, :, n * 2 * P:(n + 1) * 2 * P].rearrange("p c (f n) -> p f c n", f=2),
                              bank[n].rearrange("p (f c n) -> p f c n", f=2, c=2)).then_inc(taken, 1)
            for n in range(2):
                v.wait_ge(turned, 5 + n)
                v.tensor_copy(wot[:, 2 * n:2 * n + 2, :].rearrange("p e n -> p (e n)"), bank[4 + n]).then_inc(taken, 1)
            with v.Fori(0, NI) as i:
                ch.enter(i, 6)
                for s in range(2):
                    v.wait_ge(projected, i * 2 + s + 1)
                    y = psum[:, 2 * s:2 * s + 2, :].rearrange("p b (h d) -> p (b h) d", d=DK)
                    ch.link(v.tensor_reduce(mean[:, s, :], y, AX.X, ALU.add))
                    v.wait_ge(summed, i * 2)
                    ch.link(v.tensor_scalar(mean[:, s, :], mean[:, s, :], 1.0 / DK, None, ALU.mult))
                    v.tensor_tensor(cen[:, s], y, mean[:, s, :].unsqueeze(2).broadcast_to([P, 16, DK]), ALU.subtract
                                    ).then_inc(centred, 1)
                for s in range(2):
                    v.wait_ge(squared, i * 2 + s + 1)
                    v.tensor_reduce(ss[:, s, :], sq[:, s], AX.X, ALU.add).then_inc(var_ready, 1)
                    v.wait_ge(sd_ready, i * 2 + s + 1)
                    ch.link(v.reciprocal(rs[:, s, :], sd[:, s, :]))
                    v.tensor_tensor(cen[:, s], cen[:, s], rs[:, s, :].unsqueeze(2).broadcast_to([P, 16, DK]), ALU.mult
                                    ).then_inc(normed, 1)
                ch.leave(NI)
            ch.link(v.memset(dots[:], 0.0))
            v.wait_ge(summed, NT)
            for hh in range(2):
                a, b = hh * DK, (hh + 1) * DK
                ch.done(v.tensor_scalar(dots[a:b, :, a:b], bank[6].rearrange("p (j n) -> p j n", j=4)[a:b, :, a:b],
                                        1.0 / N, None, ALU.mult))
            ch.settle()
            v.tensor_copy(eps[:], c["ones"][:, 0:1]).then_inc(dots_ready, 1)
            v.wait_ge(m2_made, 1)
            ch.link(v.tensor_copy(m2[:], psum[:, 0:4, 0:D]))
            v.tensor_copy(eps[:], c["ones"][:, 0:1]).then_inc(m2_ready, 1)
            v.wait_ge(mix_made, 1)
            v.tensor_copy(wmix[:].rearrange("p c n -> p (c n)"), bank[4]).then_inc(mix_ready, 1)


def after_attention(nc, sem, psum, bank, c, xt, wmix, w, dram, x_in, x_out, dinv):
    with ExitStack() as ctx:
        def sbt(nm, shape, dt=F32):
            return ctx.enter_context(nc.sbuf_tensor(f"aa_{nm}", shape, dt))

        def sems(*names):
            return (sem(f"aa_{n}") for n in names)

        wa = sbt("wa", [P, 2, 4, D])
        skip = sbt("skip", [P, 4])
        sg = sbt("sg", [P, 4])
        bout = sbt("bout", [P, D])
        types = sbt("types", [P, 2, P], I32)
        mask = sbt("mask", [P, 2, 4, P])
        rows = sbt("rows", [P, 2, CW])
        xr = sbt("xr", [P, 2, D])
        den = sbt("den", [P, 2, H])
        agg = sbt("agg", [P, 2, D])
        aggt = sbt("aggt", [P, 2, D])
        am = sbt("am", [P, 2, 2, 4, P])
        xs = sbt("xs", [P, 2, 2, P])
        y = sbt("y", [P, 2, D])
        cnt = sbt("cnt", [P, NT])
        w_in, sg_ready, wa_ready, loaded, agg_ready, turned, aggt_ready, am_ready, xs_ready, made, out_ready, stored = sems(
            "w_in", "sg_ready", "wa_ready", "loaded", "agg_ready", "turned", "aggt_ready", "am_ready", "xs_ready",
            "made", "out_ready", "stored")
        dve, cnt_ready, sd_ready = sems("dve", "cnt_ready", "sd_ready")
        slot_in = [sem(f"aa_slot_in{s}") for s in range(2)]
        slot_out = [sem(f"aa_slot_out{s}") for s in range(2)]
        block = ctx.enter_context(nc.Block())

        @block.sync
        def _(sp):
            for cc in range(2):
                sp.dma_start(wa[:, cc], w["a"][:, cc * P:(cc + 1) * P, :].rearrange("t p o -> p t o")).then_inc(w_in, 16)
            sp.dma_start(skip[:], w["skip"].unsqueeze(0).broadcast_to([P, 4])).then_inc(w_in, 16)
            sp.dma_start(bout[:], w["bout"].unsqueeze(0).broadcast_to([P, D])).then_inc(w_in, 16)
            with sp.Fori(0, NI) as i:
                for s in range(2):
                    k = i * 2 + s
                    sp.wait_ge(out_ready, i * 2)
                    sp.dma_start(rows[:, s, :], dram["sums"][bass.ds(k * P, P), :]).then_inc(slot_in[s], 16)
                    sp.dma_start(xr[:, s, :], x_in[bass.ds(k * P, P), :]).then_inc(slot_in[s], 16)
                    sp.dma_start(types[:, s, :], dram["types"][bass.ds(k * P, P)].unsqueeze(0).broadcast_to([P, P])
                                 ).then_inc(slot_in[s], 16)

        @block.gpsimd
        def _(g):
            with g.Fori(0, NI) as i:
                for s in range(2):
                    k = i * 2 + s
                    g.wait_ge(made, i * 2)
                    g.tensor_copy(xs[:, s], xt[:, :, bass.ds(k * P, P)]).then_inc(xs_ready, 1)
                for s in range(2):
                    k = i * 2 + s
                    g.wait_ge(out_ready, k + 1)
                    g.dma_start(x_out[bass.ds(k * P, P), :], y[:, s, :]).then_inc(slot_out[s], 16)
            for s in range(2):
                g.wait_ge(slot_out[s], NI * 16)

        @block.scalar
        def _(a):
            a.wait_ge(w_in, 64)
            a.activation(sg[:], skip[:], ACT.Sigmoid).then_inc(sg_ready, 1)
            with a.Fori(0, NI) as i:
                for s in range(2):
                    k = i * 2 + s
                    a.wait_ge(turned, k + 1)
                    a.wait_ge(am_ready, i * 2)
                    a.activation(aggt[:, s, :], bank[s][:, 0:D], ACT.Copy).then_inc(aggt_ready, 1)
            a.wait_ge(cnt_ready, 1)
            a.activation(dinv[:], cnt[:], ACT.Sqrt, bias=c["ones"][:, 0:1]).then_inc(sd_ready, 1)

        @block.vector
        def _(v):
            ch = Chain(v, dve)
            v.wait_ge(sg_ready, 1)
            v.tensor_tensor(wa[:], wa[:], sg[:].unsqueeze(1).unsqueeze(3).broadcast_to([P, 2, 4, D]), ALU.mult
                            ).then_inc(wa_ready, 1)
            with v.Fori(0, NI) as i:
                ch.enter(i, 2 * 6)
                for s in range(2):
                    k = i * 2 + s
                    v.wait_ge(slot_in[s], i * 48 + 48)
                    ch.done(v.tensor_tensor(mask[:, s], types[:, s, :].unsqueeze(1).broadcast_to([P, 4, P]),
                                            c["iota"][:, 0:4].unsqueeze(2).broadcast_to([P, 4, P]), ALU.is_equal))
                    ch.done(v.tensor_copy(cnt[:, bass.ds(k, 1)], rows[:, s, 0:1]))
                    ch.link(v.tensor_scalar(den[:, s, :], rows[:, s, C_EX:C_V], 1e-30, None, ALU.max))
                    ch.link(v.reciprocal(den[:, s, :], den[:, s, :]))
                    v.tensor_tensor(agg[:, s].rearrange("p (h d) -> p h d", h=H),
                                    rows[:, s, C_V:CW].rearrange("p (h d) -> p h d", h=H),
                                    den[:, s, :].unsqueeze(2).broadcast_to([P, H, DK]), ALU.mult).then_inc(agg_ready, 1)
                for s in range(2):
                    k = i * 2 + s
                    v.wait_ge(aggt_ready, k + 1)
                    v.wait_ge(made, i * 2)
                    v.tensor_tensor(am[:, s], aggt[:, s].rearrange("p (c n) -> p c n", c=2).unsqueeze(2)
                                    .broadcast_to([P, 2, 4, P]), mask[:, s].unsqueeze(1).broadcast_to([P, 2, 4, P]),
                                    ALU.mult).then_inc(am_ready, 1)
                for s in range(2):
                    k = i * 2 + s
                    v.wait_ge(made, k + 1)
                    v.wait_ge(slot_out[s], i * 16)
                    ch.link(v.tensor_tensor(y[:, s], bank[2 + s][:, 0:D], xr[:, s], ALU.add))
                    v.wait_ge(w_in, 64)
                    ch.done(v.tensor_copy(den[:, s, 0:1], c["ones"][:, 0:1]))
                    v.tensor_tensor(y[:, s], y[:, s], bout[:], ALU.add).then_inc(out_ready, 1)
                ch.leave(NI)
            ch.link(v.tensor_copy(cnt[:, 0:1], cnt[:, 0:1]))
            v.tensor_copy(cnt[:, 1:2], cnt[:, 1:2]).then_inc(cnt_ready, 1)
            v.wait_ge(sd_ready, 1)
            ch.link(v.reciprocal(dinv[:], dinv[:]))

        @block.tensor
        def _(t):
            t.wait_ge(wa_ready, 1)
            with t.Fori(0, NI) as i:
                for s in range(2):
                    k = i * 2 + s
                    t.wait_ge(agg_ready, k + 1)
                    t.wait_ge(aggt_ready, i * 2)
                    t.transpose(bank[s][:, 0:P], agg[:, s, 0:P], c["ident"][:])
                    t.transpose(bank[s][:, P:D], agg[:, s, P:D], c["ident"][:]).then_inc(turned, 1)
                for s in range(2):
                    k = i * 2 + s
                    t.wait_ge(xs_ready, k + 1)
                    t.wait_ge(out_ready, i * 2)
                    for cc in range(2):
                        t.matmul(bank[2 + s][:, 0:D], xs[:, s, cc, :], wmix[:, cc, :], start=cc == 0, stop=False)
                    t.wait_ge(am_ready, k + 1)
                    for n in range(8):
                        ins = t.matmul(bank[2 + s][:, 0:D], am[:, s, n // 4, n % 4, :], wa[:, n // 4, n % 4, :],
                                       start=False, stop=n == 7)
                    ins.then_inc(made, 1)

FH = 1024
FC = FH // P
CAP = max(1, int(0.5 * N)) - 1
LOW = -3.0e38


def routed_ffn(nc, sem, psum, bank, c, xt, w, dram, x_in, xn_in, x_out):
    with ExitStack() as ctx:
        def sbt(nm, shape, dt=F32):
            return ctx.enter_context(nc.sbuf_tensor(f"rf_{nm}", shape, dt))

        def sems(*names):
            return (sem(f"rf_{n}") for n in names)

        w1, w2 = sbt("w1", [P, 2, FH]), sbt("w2", [P, FC, D])
        b1, b2 = sbt("b1", [P, FC]), sbt("b2", [P, D])
        wr, br = sbt("wr", [P, 2]), sbt("br", [1, 1])
        wrow = sbt("wrow", [1, NP])
        wbc = sbt("wbc", [P, NP])
        junk = sbt("junk", [P, NP], mybir.dt.bfloat16)
        wcol, gt, sel, eq = sbt("wcol", [P, NT]), sbt("gt", [P, NT]), sbt("sel", [P, NT]), sbt("eq", [P, NT])
        node = sbt("node", [P, NT])
        tile_i = sbt("node_i", [P, NT], I32)
        tri = sbt("tri", [P, P])
        gm = sbt("gm", [P, 1])
        g1 = sbt("g1", [1, 1])
        gbc = sbt("gbc", [P, 1])
        before, tot, coef = sbt("before", [P, NT]), sbt("tot", [P, NT]), sbt("coef", [P, NT])
        ht = sbt("ht", [P, FC, 2 * P])
        y = sbt("y", [P, NT, D])
        xr, xn = sbt("xr", [P, 2, D]), sbt("xn", [P, 2, D])
        o = sbt("o", [P, 2, D])
        w_in, row_made, row_taken, row_stored, row_in, masked, counted, dve = sems(
            "w_in", "row_made", "row_taken", "row_stored", "row_in", "masked", "counted", "dve")
        h_made, h_ready, h_used, y_made, y_taken, iota_made, tri_made = sems(
            "h_made", "h_ready", "h_used", "y_made", "y_taken", "iota_made", "tri_made")
        gm_ready, gm_turned, g1_ready, g_spread, eq_ready, ranked, out_ready, routed = sems(
            "gm_ready", "gm_turned", "g1_ready", "g_spread", "eq_ready", "ranked", "out_ready", "routed")
        slot_in = [sem(f"rf_slot_in{s}") for s in range(2)]
        slot_out = [sem(f"rf_slot_out{s}") for s in range(2)]
        LOADS = 6
        block = ctx.enter_context(nc.Block())

        @block.sync
        def _(sp):
            sp.dma_start(wr[:], w["wr"].rearrange("(c p) o -> p (c o)", p=P), allow_slow_non_contiguous=True
                         ).then_inc(w_in, 16)
            sp.dma_start(br[:], w["br"].unsqueeze(0)).then_inc(w_in, 16)
            sp.dma_start(w1[:], w["w1"].rearrange("(c p) n -> p c n", p=P)).then_inc(w_in, 16)
            sp.dma_start(w2[:], w["w2"].rearrange("(c p) n -> p c n", p=P)).then_inc(w_in, 16)
            sp.dma_start(b1[:], w["b1"].rearrange("(c p) -> p c", p=P), allow_slow_non_contiguous=True).then_inc(w_in, 16)
            sp.dma_start(b2[:], w["b2"].unsqueeze(0).broadcast_to([P, D])).then_inc(w_in, 16)
            sp.wait_ge(row_taken, NI)
            sp.dma_start(dram["router"].unsqueeze(0), wrow[:]).then_inc(row_stored, 16)
            sp.wait_ge(row_stored, 16)
            sp.dma_start(wcol[:], dram["router"].rearrange("(t p) -> p t", p=P), allow_slow_non_contiguous=True
                         ).then_inc(row_in, 16)
            sp.dma_start(wbc[:], dram["router"].unsqueeze(0).broadcast_to([P, NP])).then_inc(row_in, 16)
            with sp.Fori(0, NI) as i:
                for s in range(2):
                    k = i * 2 + s
                    sp.wait_ge(out_ready, i * 2)
                    sp.dma_start(xr[:, s, :], x_in[bass.ds(k * P, P), :]).then_inc(slot_in[s], 16)
                    sp.dma_start(xn[:, s, :], xn_in[bass.ds(k * P, P), :]).then_inc(slot_in[s], 16)

        @block.gpsimd
        def _(g):
            g.iota(tile_i[:], pattern=[[P, NT]], base=0, channel_multiplier=1).then_inc(iota_made, 1)
            g.affine_select(out=tri[:], in_=c["ones"][:], compare_op=ALU.is_gt, fill=0.0, base=0, pattern=[[1, P]],
                            channel_multiplier=-1).then_inc(tri_made, 1)
            with g.Fori(0, NI) as i:
                for s in range(2):
                    k = i * 2 + s
                    g.wait_ge(out_ready, k + 1)
                    g.dma_start(x_out[bass.ds(k * P, P), :], o[:, s, :]).then_inc(slot_out[s], 16)
            for s in range(2):
                g.wait_ge(slot_out[s], NI * 16)

        @block.tensor
        def _(t):
            t.wait_ge(w_in, 16 * LOADS)
            with t.Fori(0, NI) as i:
                t.wait_ge(row_taken, i)
                for cc in range(2):
                    ins = t.matmul(bank[6][0:1, 0:2 * P], wr[:, cc:cc + 1], xt[:, cc, bass.ds(i * 2 * P, 2 * P)],
                                   start=cc == 0, stop=cc == 1)
                ins.then_inc(row_made, 1)
            with t.Fori(0, NI) as i:
                for b in range(4):
                    t.wait_ge(h_ready, i * 4)
                    for j in range(2):
                        f = 2 * b + j
                        for cc in range(2):
                            ins = t.matmul(bank[b][:, j * 2 * P:(j + 1) * 2 * P], w1[:, cc, f * P:(f + 1) * P],
                                           xt[:, cc, bass.ds(i * 2 * P, 2 * P)], start=cc == 0, stop=cc == 1)
                    ins.then_inc(h_made, 1)
                t.wait_ge(h_ready, i * 4 + 4)
                for s in range(2):
                    t.wait_ge(y_taken, i * 2)
                    for f in range(FC):
                        ins = t.matmul(bank[4 + s][:, 0:D], ht[:, f, s * P:(s + 1) * P], w2[:, f, :],
                                       start=f == 0, stop=f == FC - 1)
                    ins.then_inc(y_made, 1)
            t.wait_ge(gm_ready, 1)
            t.transpose(bank[6][0:1, 0:P], gm[:], c["ident"][:]).then_inc(gm_turned, 1)
            t.wait_ge(g1_ready, 1)
            t.matmul(bank[7][:, 0:1], c["ones"][0:1, :], g1[:], start=True, stop=True).then_inc(g_spread, 1)
            t.wait_ge(eq_ready, 1)
            t.wait_ge(tri_made, 1)
            t.matmul(bank[6][:, 0:NT], tri[:], eq[:], start=True, stop=True)
            t.matmul(bank[6][:, NT:2 * NT], c["ones"][:], eq[:], start=True, stop=True).then_inc(ranked, 1)

        @block.scalar
        def _(a):
            a.wait_ge(w_in, 16 * LOADS)
            with a.Fori(0, NI) as i:
                a.wait_ge(row_made, i + 1)
                a.activation(wrow[:, bass.ds(i * 2 * P, 2 * P)], bank[6][0:1, 0:2 * P], ACT.Identity, bias=br[:]
                             ).then_inc(row_taken, 1)
            with a.Fori(0, NI) as i:
                for b in range(4):
                    a.wait_ge(h_made, i * 4 + b + 1)
                    a.wait_ge(y_made, i * 2)
                    for j in range(2):
                        f = 2 * b + j
                        ins = a.activation(ht[:, f, :], bank[b][:, j * 2 * P:(j + 1) * 2 * P], ACT.Gelu_apprx_tanh,
                                           bias=b1[:, f:f + 1])
                        if j:
                            ins.then_inc(h_ready, 1)

        @block.vector
        def _(v):
            ch = Chain(v, dve)
            v.wait_ge(iota_made, 1)
            ch.link(v.tensor_copy(node[:], tile_i[:]))
            v.wait_ge(row_in, 32)
            ch.link(v.tensor_scalar(node[:], node[:], float(N), LOW, ALU.is_ge, ALU.mult))
            ch.done(v.tensor_tensor(wcol[:], wcol[:], node[:], ALU.add))
            ch.done(v.memset(wbc[:, N:NP], LOW))
            ch.settle()
            with v.Fori(0, NI) as i:
                ch.enter(i, 2)
                for s in range(2):
                    k = i * 2 + s
                    ch.settle()
                    ch.done(v.tensor_scalar(junk[:], wbc[:], wcol[:, bass.ds(k, 1)], 0.0, ALU.is_gt, ALU.add,
                                            accum_out=gt[:, bass.ds(k, 1)]))
                    v.wait_ge(y_made, k + 1)
                    v.tensor_tensor(y[:, bass.ds(k, 1), :].rearrange("p t d -> p (t d)"), bank[4 + s][:, 0:D], b2[:],
                                    ALU.add).then_inc(y_taken, 1)
                ch.leave(NI)
            ch.settle()
            ch.link(v.tensor_scalar(sel[:], gt[:], float(CAP), None, ALU.is_lt))
            ch.link(v.tensor_tensor(eq[:], gt[:], sel[:], ALU.mult))
            v.tensor_reduce(gm[:], eq[:], AX.X, ALU.max).then_inc(gm_ready, 1)
            v.wait_ge(gm_turned, 1)
            v.tensor_reduce(g1[:], bank[6][0:1, 0:P], AX.X, ALU.max).then_inc(g1_ready, 1)
            v.wait_ge(g_spread, 1)
            ch.link(v.tensor_copy(gbc[:], bank[7][:, 0:1]))
            ch.done(v.tensor_scalar(sel[:], gt[:], gbc[:], None, ALU.is_lt))
            v.tensor_scalar(eq[:], gt[:], gbc[:], None, ALU.is_equal).then_inc(eq_ready, 1)
            v.wait_ge(ranked, 1)
            ch.done(v.tensor_copy(tot[:], bank[6][:, NT:2 * NT]))
            ch.link(v.tensor_scalar(before[:], bank[6][:, 0:NT], gbc[:], None, ALU.add))
            ch.link(v.tensor_tensor_scan(coef[:], tot[:], c["zero"][:, 0:NT], 0.0, ALU.add, ALU.add))
            ch.link(v.tensor_tensor(coef[:], coef[:], tot[:], ALU.subtract))
            ch.link(v.tensor_tensor(before[:], before[:], coef[:], ALU.add))
            ch.link(v.scalar_tensor_tensor(before[:], before[:], float(CAP), eq[:], ALU.is_lt, ALU.mult))
            ch.link(v.tensor_tensor(sel[:], sel[:], before[:], ALU.add))
            ch.link(v.tensor_tensor(coef[:], sel[:], wcol[:], ALU.mult))
            n0 = ch.n
            with v.Fori(0, NI) as i:
                ch.enter(i, 2 * 1)
                for s in range(2):
                    k = i * 2 + s
                    v.wait_ge(slot_in[s], i * 32 + 32)
                    v.wait_ge(slot_out[s], i * 16)
                    ch.link(v.tensor_tensor(o[:, s], xr[:, s], xn[:, s], ALU.add))
                    v.scalar_tensor_tensor(o[:, s], y[:, bass.ds(k, 1), :].rearrange("p t d -> p (t d)"),
                                           coef[:, bass.ds(k, 1)], o[:, s], ALU.mult, ALU.add).then_inc(out_ready, 1)
                ch.leave(NI)

EPS_RMS = 1e-6
EPS_BN = 1e-5
HID = 64
HD1 = D // MH
QKV = 3 * D


def project_layer1(nc, sem, psum, bank, c, xt, w, xn_in, q_out, y_out, dinv, ksum, kvm):
    with ExitStack() as ctx:
        def sbt(nm, shape, dt=F32):
            return ctx.enter_context(nc.sbuf_tensor(f"p1_{nm}", shape, dt))

        def sems(*names):
            return (sem(f"p1_{n}") for n in names)

        W = QKV + HID
        wa = sbt("wa", [P, 2, W])
        wn = sbt("wn", [P, 2])
        wo = sbt("wo", [P, 2, D])
        xn = sbt("xn", [P, 2, D])
        junk = sbt("junk", [P, 2, D])
        ss, rs = sbt("ss", [P, NT]), sbt("rs", [P, NT])
        eps = sbt("eps", [P, 1])
        node, valid = sbt("node_i", [P, NT], I32), sbt("valid", [P, NT])
        xs = sbt("xs", [P, 2, 2, P])
        z = sbt("z", [P, 2, 2 * D])
        ez = sbt("ez", [P, 2, 2 * D])
        qk = sbt("qk", [P, 2, 2 * D])
        vv = sbt("vv", [P, 2, D])
        yy = sbt("yy", [P, 2, HID])
        kvd = sbt("kvd", [P, 2, P])
        w_in, dve, ready, ss_ready, sd_ready, xs_ready, made, z_ready, exped, k_ready, summed = sems(
            "w_in", "dve", "ready", "ss_ready", "sd_ready", "xs_ready", "made", "z_ready", "exped", "k_ready", "summed")
        kvd_ready, joined, iota_made, y_ready, sq_done, pos = sems(
            "kvd_ready", "joined", "iota_made", "y_ready", "sq_done", "pos")
        slot_in = [sem(f"p1_slot_in{s}") for s in range(2)]
        slot_out = [sem(f"p1_slot_out{s}") for s in range(2)]
        block = ctx.enter_context(nc.Block())

        @block.sync
        def _(sp):
            sp.dma_start(wa[:, :, 0:QKV], w["w_qkv"].rearrange("(c p) n -> p c n", p=P)).then_inc(w_in, 16)
            sp.dma_start(wa[:, :, QKV:W], w["W1"].rearrange("(c p) n -> p c n", p=P)).then_inc(w_in, 16)
            sp.dma_start(wn[:], w["w_norm1"].rearrange("(c p) -> p c", p=P), allow_slow_non_contiguous=True).then_inc(w_in, 16)
            sp.dma_start(wo[:], w["w_out"].rearrange("(c p) n -> p c n", p=P)).then_inc(w_in, 16)
            with sp.Fori(0, NI) as i:
                for s in range(2):
                    sp.wait_ge(sq_done, i * 2)
                    sp.dma_start(xn[:, s, :], xn_in[bass.ds((i * 2 + s) * P, P), :]).then_inc(slot_in[s], 16)

        @block.gpsimd
        def _(g):
            g.iota(node[:], pattern=[[P, NT]], base=0, channel_multiplier=1).then_inc(iota_made, 1)
            with g.Fori(0, NI) as i:
                for s in range(2):
                    k = i * 2 + s
                    g.wait_ge(made, i * 2)
                    g.tensor_copy(xs[:, s], xt[:, :, bass.ds(k * P, P)]).then_inc(xs_ready, 1)
                for s in range(2):
                    k = i * 2 + s
                    g.wait_ge(y_ready, k + 1)
                    g.dma_start(y_out[bass.ds(k * P, P), :], yy[:, s, :]).then_inc(slot_out[s], 16)
                    g.wait_ge(k_ready, k + 1)
                    g.dma_start(q_out[bass.ds(k * P, P), :], qk[:, s, 0:D]).then_inc(slot_out[s], 16)
            for s in range(2):
                g.wait_ge(slot_out[s], NI * 32)

        @block.scalar
        def _(a):
            a.wait_ge(ss_ready, 1)
            a.activation(rs[:], ss[:], ACT.Sqrt, bias=eps[:], scale=1.0 / D).then_inc(sd_ready, 1)
            with a.Fori(0, NI) as i:
                for s in range(2):
                    a.wait_ge(z_ready, i * 2 + s + 1)
                    a.activation(ez[:, s], z[:, s], ACT.Exp).then_inc(exped, 1)

        @block.vector
        def _(v):
            ch = Chain(v, dve)
            ch.done(v.memset(eps[:], EPS_RMS))
            v.wait_ge(iota_made, 1)
            ch.link(v.tensor_copy(valid[:], node[:]))
            ch.done(v.tensor_scalar(valid[:], valid[:], float(N), None, ALU.is_lt))
            v.wait_ge(w_in, 64)
            for cc in range(2):
                ch.done(v.tensor_scalar(wa[:, cc, 0:QKV], wa[:, cc, 0:QKV], wn[:, cc:cc + 1], None, ALU.mult))
            ch.settle()
            with v.Fori(0, NI) as i:
                for s in range(2):
                    v.wait_ge(slot_in[s], i * 16 + 16)
                    v.wait_ge(sq_done, i * 2)
                    v.scalar_tensor_tensor(junk[:, s], xn[:, s], 1.0, xn[:, s], ALU.mult, ALU.mult,
                                           accum_out=ss[:, bass.ds(i * 2 + s, 1)]).then_inc(sq_done, 1)
            v.wait_ge(sq_done, NT)
            v.tensor_copy(junk[:, 0, 0:1], eps[:]).then_inc(ss_ready, 1)
            v.wait_ge(sd_ready, 1)
            ch.link(v.reciprocal(rs[:], rs[:]))
            v.tensor_copy(junk[:, 1, 0:1], rs[:, 0:1]).then_inc(ready, 1)
            with v.Fori(0, NI) as i:
                ch.enter(i, 2 * 2)
                for s in range(2):
                    k = i * 2 + s
                    v.wait_ge(made, k + 1)
                    v.wait_ge(summed, i * 2)
                    v.wait_ge(slot_out[s], i * 32)
                    r = rs[:, bass.ds(k, 1)]
                    v.tensor_scalar(z[:, s], bank[2 * s], r, None, ALU.mult).then_inc(z_ready, 1)
                    ch.done(v.tensor_scalar(vv[:, s], bank[2 * s + 1][:, 0:D], r, None, ALU.mult))
                    v.tensor_scalar(yy[:, s], bank[2 * s + 1][:, D:D + HID], dinv[:, bass.ds(k, 1)], None, ALU.mult
                                    ).then_inc(y_ready, 1)
                for s in range(2):
                    k = i * 2 + s
                    v.wait_ge(exped, k + 1)
                    v.tensor_scalar(z[:, s], z[:, s], 0.0, None, ALU.max).then_inc(pos, 1)
                    v.wait_ge(pos, k + 1)
                    ch.link(v.scalar_tensor_tensor(qk[:, s], ez[:, s], 1.0, z[:, s], ALU.min, ALU.add))
                    v.tensor_scalar(qk[:, s, D:2 * D], qk[:, s, D:2 * D], valid[:, bass.ds(k, 1)], None, ALU.mult
                                    ).then_inc(k_ready, 1)
                ch.leave(NI)
            v.wait_ge(summed, NT)
            ch.done(v.tensor_copy(ksum[:], bank[5][:, 0:D]))
            ch.link(v.memset(kvd[:], 0.0))
            for b in range(4):
                a_, b_ = b * HD1, (b + 1) * HD1
                ch.done(v.tensor_copy(kvd[a_:b_, :, a_:b_],
                                      bank[4][:, 0:D].rearrange("p (c n) -> p c n", c=2)[a_:b_, :, a_:b_]))
            ch.settle()
            v.tensor_copy(junk[:, 0, 0:1], rs[:, 0:1]).then_inc(kvd_ready, 1)
            v.wait_ge(joined, 1)
            ch.link(v.tensor_copy(kvm[:].rearrange("p c n -> p (c n)"), bank[6]))

        @block.tensor
        def _(t):
            t.wait_ge(ready, 1)
            for b in (4, 5):
                t.matmul(bank[b], c["zero"][:, 0:P], c["zero"][:], start=True, stop=False, skip_group_check=True)
            with t.Fori(0, NI) as i:
                for s in range(2):
                    k = i * 2 + s
                    t.wait_ge(xs_ready, k + 1)
                    t.wait_ge(y_ready, i * 2)
                    for b, (lo, hi) in enumerate(((0, 512), (512, W))):
                        for cc in range(2):
                            ins = t.matmul(bank[2 * s + b][:, 0:hi - lo], xs[:, s, cc, :], wa[:, cc, lo:hi],
                                           start=cc == 0, stop=cc == 1)
                    ins.then_inc(made, 1)
                for s in range(2):
                    k = i * 2 + s
                    t.wait_ge(k_ready, k + 1)
                    for cc in range(2):
                        t.matmul(bank[4][:, cc * P:(cc + 1) * P], vv[:, s, cc * P:(cc + 1) * P],
                                 qk[:, s, D + cc * P:D + (cc + 1) * P], start=False, stop=False, skip_group_check=True)
                    t.matmul(bank[5][:, 0:D], c["ones"][:], qk[:, s, D:2 * D], start=False, stop=False,
                             skip_group_check=True).then_inc(summed, 1)
            t.wait_ge(kvd_ready, 1)
            for cc in range(2):
                ins = t.matmul(bank[6][:, cc * D:(cc + 1) * D], kvd[:, cc, :], wo[:, cc, :], start=True, stop=True)
            ins.then_inc(joined, 1)


def gcn_edges(nc, sem, psum, bank, c, dram, name, W, table, out):
    with ExitStack() as ctx:
        def sbt(nm, shape, dt=F32):
            return ctx.enter_context(nc.sbuf_tensor(f"{name}_{nm}", shape, dt))

        def slots(nm):
            return [sem(f"{name}_{nm}{s}") for s in range(SLOTS)]

        acc = sbt("acc", [P, NB, W])
        row = sbt("row", [P, SLOTS, G, W])
        col = sbt("col", [P, SLOTS, 5, G])
        hot = sbt("hot", [P, SLOTS, G, P])
        step_sums = sbt("step_sums", [P, SLOTS, G, W])
        blocks = sbt("blocks", [1, T], I32)
        zrow = sbt("zrow", [NP - NB * BW, W])
        blocks_in, cleared, added, stored, gate = (sem(f"{name}_{n}") for n in ("blocks_in", "cleared", "added", "stored", "gate"))
        loaded, gathered, hot_made, made, copied = (slots(n) for n in ("loaded", "gathered", "hot_made", "made", "copied"))
        block = ctx.enter_context(nc.Block())
        ITER = GROUPS // SLOTS

        @block.sync
        def _(sp):
            sp.dma_start(blocks[:], dram["blocks"].unsqueeze(0)).then_inc(blocks_in, 16)
            with sp.Fori(0, ITER) as i:
                for s in range(SLOTS):
                    k = i * SLOTS + s
                    sp.wait_ge(made[s], i)
                    sp.dma_start(col[:, s], dram["cols"][:, bass.ds(k, 1)].rearrange("p k c g -> p (k c) g")
                                 ).then_inc(loaded[s], 16)
            sp.wait_ge(added, GROUPS * G)
            sp.wait_ge(cleared, 2)
            for a, b in ((0, 112), (112, BW)):
                sp.dma_start(out[0:NB * BW].rearrange("(b p) n -> p b n", p=BW)[a:b], acc[a:b]).then_inc(stored, 16)
            sp.dma_start(out[NB * BW:NP], zrow[:]).then_inc(stored, 16)
            sp.wait_ge(stored, 48)

        @block.gpsimd
        def _(g):
            g.memset(acc[:], 0.0).then_inc(cleared, 1)
            g.memset(zrow[:], 0.0).then_inc(cleared, 1)
            with g.Fori(0, ITER) as i:
                for s in range(SLOTS):
                    g.wait_ge(loaded[s], i * 16 + 16)
                    wait_alone(g, gate)
                    for n in range(G):
                        g.indirect_dma_start(out=row[:, s, n, :], out_offset=None, in_=table,
                                             in_offset=bass.IndirectOffsetOnAxis(
                                                 ap=col[:, s, 1, n:n + 1].bitcast(U32), axis=0)).then_inc(gathered[s], 16)

        @block.vector
        def _(v):
            v.wait_ge(cleared, 1)
            v.wait_ge(blocks_in, 16)

            def front(i, s):
                v.wait_ge(loaded[s], i * 16 + 16)
                v.wait_ge(made[s], i)
                v.tensor_tensor(hot[:, s], c["iota"][:].unsqueeze(1).broadcast_to([P, G, P]),
                                col[:, s, 3, :].unsqueeze(2).broadcast_to([P, G, P]), ALU.is_equal).then_inc(hot_made[s], 1)

            def back(i, s):
                k = i * SLOTS + s
                regs = [v.value_load(blocks[0:1, bass.ds(k * G + n, 1)], min_val=0, max_val=NB - 1) for n in range(G)]
                v.wait_ge(copied[s], i + 1)
                for n in range(G):
                    v.wait_ge(added, k * G + n)
                    o = acc[:, bass.ds(regs[n], 1), :].rearrange("p b n -> p (b n)")
                    v.tensor_tensor(o, o, step_sums[:, s, n, :], ALU.add).then_inc(added, 1)

            front(0, 0)
            with v.Fori(0, ITER - 1) as i:
                for s in range(SLOTS):
                    front(i + (s + 1) // SLOTS, (s + 1) % SLOTS)
                    back(i, s)
            for s in range(SLOTS):
                if s + 1 < SLOTS:
                    front(ITER - 1, s + 1)
                back(ITER - 1, s)

        @block.scalar
        def _(a):
            with a.Fori(0, ITER) as i:
                for s in range(SLOTS):
                    a.wait_ge(made[s], i + 1)
                    a.wait_ge(added, i * SLOTS * G)
                    a.activation(step_sums[:, s].rearrange("p g n -> p (g n)"), bank[s][:, 0:G * W], ACT.Copy
                                 ).then_inc(copied[s], 1)

        @block.tensor
        def _(t):
            with t.Fori(0, ITER) as i:
                for s in range(SLOTS):
                    t.wait_ge(hot_made[s], i + 1)
                    t.wait_ge(gathered[s], i * 16 * G + 16 * G)
                    t.wait_ge(copied[s], i)
                    for n in range(G):
                        ins = t.matmul(bank[s][:, n * W:(n + 1) * W], hot[:, s, n, :], row[:, s, n, :], start=True, stop=True)
                    ins.then_inc(made[s], 1)


def gcn_norm(nc, sem, psum, bank, c, name, W, sums_in, own, dinv, w, relu, w_next, out):
    with ExitStack() as ctx:
        def sbt(nm, shape, dt=F32):
            return ctx.enter_context(nc.sbuf_tensor(f"{name}_{nm}", shape, dt))

        def sems(*names):
            return (sem(f"{name}_{n}") for n in names)

        h, o, sq = sbt("h", [P, NT, W]), sbt("o", [P, NT, W]), sbt("sq", [P, NT, W])
        vec = sbt("vec", [P, 3, W])
        wnx = sbt("wnx", [P, W, 2]) if w_next is not None else None
        node, valid = sbt("node_i", [P, NT], I32), sbt("valid", [P, NT])
        part, mu, sd, eps = sbt("part", [P, W]), sbt("mu", [P, W]), sbt("sd", [P, W]), sbt("eps", [P, 1])
        w_in, dve, iota_made, part_ready, mean_made, var_ready, sd_ready, out_ready, stored = sems(
            "w_in", "dve", "iota_made", "part_ready", "mean_made", "var_ready", "sd_ready", "out_ready", "stored")
        loads = 5 + (w_next is not None)
        block = ctx.enter_context(nc.Block())

        @block.sync
        def _(sp):
            sp.dma_start(h[:], sums_in.rearrange("(t p) n -> p t n", p=P)).then_inc(w_in, 16)
            sp.dma_start(o[:], own.rearrange("(t p) n -> p t n", p=P)).then_inc(w_in, 16)
            for n, x in enumerate(w):
                sp.dma_start(vec[:, n, :], x.unsqueeze(0).broadcast_to([P, W])).then_inc(w_in, 16)
            if w_next is not None:
                sp.dma_start(wnx[:].rearrange("p a b -> p (a b)"),
                             w_next.rearrange("a b -> (a b)").unsqueeze(0).broadcast_to([P, W * 2])).then_inc(w_in, 16)
                sp.wait_ge(out_ready, 1)
                sp.dma_start(out[0].rearrange("(t p) n -> p t n", p=P), out[1][:]).then_inc(stored, 16)
                sp.wait_ge(stored, 16)

        @block.gpsimd
        def _(g):
            g.iota(node[:], pattern=[[P, NT]], base=0, channel_multiplier=1).then_inc(iota_made, 1)

        @block.tensor
        def _(t):
            for n in range(2):
                t.wait_ge(part_ready, n + 1)
                t.matmul(bank[0][:, 0:W], c["ones"][:], part[:], start=True, stop=True).then_inc(mean_made, 1)

        @block.scalar
        def _(a):
            a.wait_ge(var_ready, 1)
            a.activation(sd[:], part[:], ACT.Sqrt, bias=eps[:]).then_inc(sd_ready, 1)

        @block.vector
        def _(v):
            ch = Chain(v, dve)

            def over_nodes(x):
                return x.unsqueeze(1).broadcast_to([P, NT, W])

            def over_features(x):
                return x.unsqueeze(2).broadcast_to([P, NT, W])

            ch.done(v.memset(eps[:], EPS_BN))
            v.wait_ge(iota_made, 1)
            ch.link(v.tensor_copy(valid[:], node[:]))
            ch.done(v.tensor_scalar(valid[:], valid[:], float(N), None, ALU.is_lt))
            v.wait_ge(w_in, 16 * loads)
            ch.link(v.tensor_tensor(h[:], h[:], o[:], ALU.add))
            ch.link(v.tensor_tensor(h[:], h[:], over_features(dinv[:]), ALU.mult))
            ch.link(v.tensor_tensor(h[:], h[:], over_nodes(vec[:, 0, :]), ALU.add))
            ch.link(v.tensor_tensor(h[:], h[:], over_features(valid[:]), ALU.mult))
            v.tensor_reduce(part[:], h[:].rearrange("p t n -> p n t"), AX.X, ALU.add).then_inc(part_ready, 1)
            v.wait_ge(mean_made, 1)
            ch.link(v.tensor_scalar(mu[:], bank[0][:, 0:W], 1.0 / N, None, ALU.mult))
            ch.link(v.tensor_tensor(h[:], h[:], over_nodes(mu[:]), ALU.subtract))
            ch.link(v.tensor_tensor(h[:], h[:], over_features(valid[:]), ALU.mult))
            ch.link(v.tensor_tensor(sq[:], h[:], h[:], ALU.mult))
            v.tensor_reduce(part[:], sq[:].rearrange("p t n -> p n t"), AX.X, ALU.add).then_inc(part_ready, 1)
            v.wait_ge(mean_made, 2)
            v.tensor_scalar(part[:], bank[0][:, 0:W], 1.0 / N, None, ALU.mult).then_inc(var_ready, 1)
            v.wait_ge(sd_ready, 1)
            ch.link(v.reciprocal(mu[:], sd[:]))
            ch.link(v.tensor_tensor(mu[:], mu[:], vec[:, 1, :], ALU.mult))
            ch.link(v.tensor_tensor(h[:], h[:], over_nodes(mu[:]), ALU.mult))
            dst_ = out[1] if w_next is None else h
            ch.link(v.tensor_tensor(dst_[:], h[:], over_nodes(vec[:, 2, :]), ALU.add))
            if w_next is not None:
                ch.link(v.tensor_scalar(h[:], h[:], 0.0, None, ALU.max))
                for n in range(2):
                    ch.link(v.tensor_tensor(sq[:], h[:], over_nodes(wnx[:, :, n]), ALU.mult))
                    ch.link(v.tensor_reduce(out[1][:, :, n], sq[:], AX.X, ALU.add))
                v.tensor_tensor(out[1][:], out[1][:], dinv[:].unsqueeze(2).broadcast_to([P, NT, 2]), ALU.mult
                                ).then_inc(out_ready, 1)
                v.wait_ge(out_ready, 1)


def finish_layer1(nc, sem, psum, bank, c, w, x_in, xn_in, q_in, zn, ksum, kvm, x_out):
    with ExitStack() as ctx:
        def sbt(nm, shape, dt=F32):
            return ctx.enter_context(nc.sbuf_tensor(f"f1_{nm}", shape, dt))

        def sems(*names):
            return (sem(f"f1_{n}") for n in names)

        vec = sbt("vec", [P, 5, D])
        x, xn, q = sbt("x", [P, 2, D]), sbt("xn", [P, 2, D]), sbt("q", [P, 2, D])
        qt = sbt("qt", [P, 2, D])
        t1, h, o = sbt("t1", [P, 2, D]), sbt("h", [P, 2, D]), sbt("o", [P, 2, D])
        den, ss, sd, eps = sbt("den", [P, 2, MH]), sbt("ss", [P, 2]), sbt("sd", [P, 2]), sbt("eps", [P, 1])
        w_in, dve, q_ready, turned, qt_ready, made, ss_ready, sd_ready, out_ready, scaled = sems(
            "w_in", "dve", "q_ready", "turned", "qt_ready", "made", "ss_ready", "sd_ready", "out_ready", "scaled")
        slot_in = [sem(f"f1_slot_in{s}") for s in range(2)]
        slot_out = [sem(f"f1_slot_out{s}") for s in range(2)]
        block = ctx.enter_context(nc.Block())

        @block.sync
        def _(sp):
            for n, a in enumerate((w["b_out"], w["w_norm2"], w["bd"], w["Wd"][0], w["Wd"][1])):
                sp.dma_start(vec[:, n, :], a.unsqueeze(0).broadcast_to([P, D])).then_inc(w_in, 16)
            with sp.Fori(0, NI) as i:
                for s in range(2):
                    k = i * 2 + s
                    sp.wait_ge(out_ready, i * 2)
                    for dst_, src_ in ((x, x_in), (xn, xn_in), (q, q_in)):
                        sp.dma_start(dst_[:, s, :], src_[bass.ds(k * P, P), :]).then_inc(slot_in[s], 16)

        @block.gpsimd
        def _(g):
            with g.Fori(0, NI) as i:
                for s in range(2):
                    k = i * 2 + s
                    g.wait_ge(out_ready, k + 1)
                    g.dma_start(x_out[bass.ds(k * P, P), :], o[:, s, :]).then_inc(slot_out[s], 16)
            for s in range(2):
                g.wait_ge(slot_out[s], NI * 16)

        @block.scalar
        def _(a):
            with a.Fori(0, NI) as i:
                for s in range(2):
                    a.wait_ge(turned, i * 2 + s + 1)
                    a.activation(qt[:, s], bank[s][:, 0:D], ACT.Identity).then_inc(qt_ready, 1)
                for s in range(2):
                    a.wait_ge(ss_ready, i * 2 + s + 1)
                    a.activation(sd[:, s:s + 1], ss[:, s:s + 1], ACT.Sqrt, bias=eps[:], scale=1.0 / D).then_inc(sd_ready, 1)

        @block.tensor
        def _(t):
            with t.Fori(0, NI) as i:
                for s in range(2):
                    t.wait_ge(q_ready, i * 2 + s + 1)
                    t.transpose(bank[s][:, 0:P], q[:, s, 0:P], c["ident"][:])
                    t.transpose(bank[s][:, P:D], q[:, s, P:D], c["ident"][:]).then_inc(turned, 1)
                for s in range(2):
                    t.wait_ge(qt_ready, i * 2 + s + 1)
                    for cc in range(2):
                        ins = t.matmul(bank[2 + s][:, 0:D], qt[:, s, cc * P:(cc + 1) * P], kvm[:, cc, :],
                                       start=cc == 0, stop=cc == 1)
                    ins.then_inc(made, 1)

        @block.vector
        def _(v):
            ch = Chain(v, dve)
            ch.link(v.memset(eps[:], EPS_RMS))
            v.wait_ge(w_in, 80)
            with v.Fori(0, NI) as i:
                ch.enter(i, 2 * 11)
                for s in range(2):
                    k = i * 2 + s
                    v.wait_ge(slot_in[s], i * 48 + 48)
                    qh, th = (a[:, s].rearrange("p (h d) -> p h d", h=MH) for a in (q, t1))
                    ch.link(v.tensor_tensor(t1[:, s], q[:, s], ksum[:], ALU.mult))
                    ch.link(v.tensor_reduce(den[:, s, :], th, AX.X, ALU.add))
                    ch.link(v.tensor_scalar(den[:, s, :], den[:, s, :], EPS_RMS, None, ALU.add))
                    ch.link(v.reciprocal(den[:, s, :], den[:, s, :]))
                    v.tensor_tensor(qh, qh, den[:, s, :].unsqueeze(2).broadcast_to([P, MH, HD1]), ALU.mult).then_inc(q_ready, 1)
                for s in range(2):
                    k = i * 2 + s
                    ch.link(v.tensor_tensor(h[:, s], xn[:, s], vec[:, 0, :], ALU.add))
                    v.wait_ge(made, k + 1)
                    ch.link(v.tensor_tensor(h[:, s], h[:, s], bank[2 + s][:, 0:D], ALU.add))
                    v.scalar_tensor_tensor(t1[:, s], h[:, s], 1.0, h[:, s], ALU.mult, ALU.mult,
                                           accum_out=ss[:, s:s + 1]).then_inc(ss_ready, 1)
                for s in range(2):
                    k = i * 2 + s
                    v.wait_ge(slot_out[s], i * 16)
                    ch.link(v.tensor_tensor(o[:, s], x[:, s], vec[:, 2, :], ALU.add))
                    for n in range(2):
                        ch.link(v.scalar_tensor_tensor(o[:, s], vec[:, 3 + n, :],
                                                       zn[:, bass.ds(k, 1), n:n + 1].rearrange("p a b -> p (a b)"),
                                                       o[:, s], ALU.mult, ALU.add))
                    v.wait_ge(sd_ready, k + 1)
                    ch.link(v.reciprocal(ss[:, s:s + 1], sd[:, s:s + 1]))
                    ch.done(v.tensor_tensor(o[:, s], o[:, s], h[:, s], ALU.add))
                    v.scalar_tensor_tensor(t1[:, s], h[:, s], ss[:, s:s + 1], vec[:, 1, :], ALU.mult, ALU.mult
                                           ).then_inc(scaled, 1)
                    v.wait_ge(scaled, k + 1)
                    ch.settle()
                    v.tensor_tensor(o[:, s], o[:, s], t1[:, s], ALU.add).then_inc(out_ready, 1)
                ch.leave(NI)

NE = 8
EPS_EXP = 1e-3


def expert_mixture(nc, sem, psum, bank, c, xt, w, x_in, out):
    with ExitStack() as ctx:
        def sbt(nm, shape, dt=F32):
            return ctx.enter_context(nc.sbuf_tensor(f"em_{nm}", shape, dt))

        def sems(*names):
            return (sem(f"em_{n}") for n in names)

        w1, w2, wo = (sbt(n, [P, 2, NE, D]) for n in ("w1", "w2", "wo"))
        bo = sbt("bo", [P, NE, D])
        wr, br = sbt("wr", [P, 2, NE]), sbt("br", [NE, 1])
        bn = sbt("bn", [2 * NE, 2, 5, P])
        root, fac = sbt("root", [2 * NE, 2, P]), sbt("fac", [2 * NE, 2, 2, P])
        affine = sbt("affine", [P, 2, 2, 2 * NE])
        eps = sbt("eps", [2 * NE, 1])
        lt = sbt("logits_turned", [NE, 2 * P])
        we, top, tot = sbt("weights", [P, NT, NE]), sbt("top", [P, NT]), sbt("tot", [P, NT])
        h1, h2 = sbt("h1", [P, 2, 2, 2 * P]), sbt("h2", [P, 2, 2, 2 * P])
        x, o = sbt("x", [P, 2, D]), sbt("o", [P, 2, D])
        w_in, bn_in, dve, eps_ready, root_ready, fac_ready, fac_turned, affine_ready = sems(
            "w_in", "bn_in", "dve", "eps_ready", "root_ready", "fac_ready", "fac_turned", "affine_ready")
        logits_made, logits_biased, logits_turned, logits_taken, centred, exped, x_in_sem, started = sems(
            "logits_made", "logits_biased", "logits_turned", "logits_taken", "centred", "exped", "x_in", "started")
        h1_made, h1_taken, h2_made, h2_taken, y_made, y_added, stored = sems(
            "h1_made", "h1_taken", "h2_made", "h2_taken", "y_made", "y_added", "stored")
        gate = sem("em_gate")
        block = ctx.enter_context(nc.Block())
        rows = x_in.rearrange("(t p) d -> p t d", p=P)
        ROW_LAST = N - (NT - 2) * P

        @block.sync
        def _(sp):
            for n, l in enumerate(("1", "2")):
                for m, a in enumerate(("b", "g", "be", "m", "v")):
                    sp.dma_start(bn[:, n, m, :], w[a + l].rearrange("e (c p) -> (e c) p", p=P)).then_inc(bn_in, 16)
            sp.dma_start(wr[:], w["Wr"].rearrange("(c p) e -> p c e", p=P)).then_inc(w_in, 16)
            sp.dma_start(br[:], w["br"].unsqueeze(1), allow_slow_non_contiguous=True).then_inc(w_in, 16)
            for o_, i_ in ((w1, w["W1"]), (w2, w["W2"]), (wo, w["Wo"])):
                for cc in range(2):
                    sp.dma_start(o_[:, cc], i_[:, cc * P:(cc + 1) * P, :].rearrange("e p n -> p e n")).then_inc(w_in, 16)
            sp.dma_start(bo[:].rearrange("p e n -> p (e n)"),
                         w["bo"].rearrange("e n -> (e n)").unsqueeze(0).broadcast_to([P, NE * D])).then_inc(w_in, 16)
            with sp.Fori(0, NI) as i:
                sp.wait_ge(started, i * 2)
                sp.dma_start(x[:], rows[:, bass.ds(i * 2, 2), :]).then_inc(x_in_sem, 16)

        @block.gpsimd
        def _(g):
            with g.Fori(0, NI - 1) as i:
                g.wait_ge(y_added, i * 2 * NE + 2 * NE)
                g.dma_start(out[bass.ds(i * 2 * P, 2 * P), :].rearrange("(t p) d -> p t d", p=P), o[:]).then_inc(stored, 16)
            g.wait_ge(y_added, NI * 2 * NE)
            g.dma_start(out[(NT - 2) * P:N, :], o[0:ROW_LAST, 0, :]).then_inc(stored, 16)
            g.wait_ge(stored, 16 * NI)

        @block.tensor
        def _(t):
            t.wait_ge(fac_ready, 1)
            for n in range(4):
                ins = t.transpose(bank[7][:, n * 2 * NE:(n + 1) * 2 * NE], fac[:, n // 2, n % 2, :],
                                  c["ident"][0:2 * NE, 0:2 * NE])
            ins.then_inc(fac_turned, 1)
            t.wait_ge(affine_ready, 1)
            t.wait_ge(w_in, 16 * 9)
            with t.Fori(0, NI) as i:
                t.wait_ge(logits_biased, i)
                for cc in range(2):
                    ins = t.matmul(bank[6][0:NE, 0:2 * P], wr[:, cc, :], xt[:, cc, bass.ds(i * 2 * P, 2 * P)],
                                   start=cc == 0, stop=cc == 1)
                ins.then_inc(logits_made, 1)
                t.wait_ge(logits_taken, i)
                t.wait_ge(logits_biased, i + 1)
                wait_alone(t, gate)
                for s in range(2):
                    ins = t.transpose(bank[7][:, s * NE:(s + 1) * NE], lt[:, s * P:(s + 1) * P], c["ident"][0:NE, 0:NE])
                ins.then_inc(logits_turned, 1)
            with t.Fori(0, NI) as i:
                for e in range(NE + 2):
                    if e < NE:
                        t.wait_ge(h1_taken, i * NE + max(e - 1, 0))
                        for o_ in range(2):
                            for cc in range(2):
                                ins = t.matmul(bank[e % 2][:, o_ * 2 * P:(o_ + 1) * 2 * P], w1[:, cc, e, o_ * P:(o_ + 1) * P],
                                               xt[:, cc, bass.ds(i * 2 * P, 2 * P)], start=cc == 0, stop=cc == 1)
                        ins.then_inc(h1_made, 1)
                    if 1 <= e <= NE:
                        f = e - 1
                        t.wait_ge(h1_taken, i * NE + f + 1)
                        t.wait_ge(h2_taken, i * NE + max(f - 1, 0))
                        for o_ in range(2):
                            for cc in range(2):
                                ins = t.matmul(bank[2 + f % 2][:, o_ * 2 * P:(o_ + 1) * 2 * P],
                                               w2[:, cc, f, o_ * P:(o_ + 1) * P], h1[:, f % 2, cc, :],
                                               start=cc == 0, stop=cc == 1)
                        ins.then_inc(h2_made, 1)
                    if e >= 2:
                        f = e - 2
                        t.wait_ge(h2_taken, i * NE + f + 1)
                        t.wait_ge(y_added, i * 2 * NE + 2 * max(f - 1, 0))
                        for s in range(2):
                            for cc in range(2):
                                ins = t.matmul(bank[4 + f % 2][:, s * D:(s + 1) * D], h2[:, f % 2, cc, s * P:(s + 1) * P],
                                               wo[:, cc, f, :], start=cc == 0, stop=cc == 1)
                        ins.then_inc(y_made, 1)

        @block.scalar
        def _(a):
            a.wait_ge(bn_in, 160)
            a.wait_ge(eps_ready, 1)
            a.activation(root[:], bn[:, :, 4, :], ACT.Sqrt, bias=eps[:]).then_inc(root_ready, 1)
            a.wait_ge(w_in, 16 * 9)
            with a.Fori(0, NI) as i:
                a.wait_ge(logits_made, i + 1)
                a.wait_ge(logits_turned, i)
                a.activation(lt[:], bank[6][0:NE, 0:2 * P], ACT.Identity, bias=br[:]).then_inc(logits_biased, 1)
            a.wait_ge(centred, 1)
            a.activation(we[:], we[:], ACT.Exp).then_inc(exped, 1)
            a.wait_ge(affine_ready, 1)
            with a.Fori(0, NI) as i:
                for e in range(NE + 1):
                    for layer, f, made, taken, read, b, h in ((0, e, h1_made, h1_taken, h2_made, 0, h1),
                                                              (1, e - 1, h2_made, h2_taken, y_made, 2, h2)):
                        if not 0 <= f < NE:
                            continue
                        a.wait_ge(made, i * NE + f + 1)
                        a.wait_ge(read, i * NE + max(f - 1, 0))
                        for cc in range(2):
                            k = 2 * f + cc
                            ins = a.activation(h[:, f % 2, cc, :], bank[b + f % 2][:, cc * 2 * P:(cc + 1) * 2 * P], ACT.Relu,
                                               bias=affine[:, layer, 1, k:k + 1], scale=affine[:, layer, 0, k:k + 1])
                        ins.then_inc(taken, 1)

        @block.vector
        def _(v):
            ch = Chain(v, dve)
            v.memset(eps[:], EPS_EXP).then_inc(eps_ready, 1)
            v.wait_ge(root_ready, 1)
            ch.link(v.reciprocal(root[:], root[:]))
            ch.link(v.tensor_tensor(fac[:, :, 0, :], root[:], bn[:, :, 1, :], ALU.mult))
            ch.link(v.tensor_tensor(root[:], bn[:, :, 0, :], bn[:, :, 3, :], ALU.subtract))
            ch.link(v.tensor_tensor(root[:], root[:], fac[:, :, 0, :], ALU.mult))
            v.tensor_tensor(fac[:, :, 1, :], root[:], bn[:, :, 2, :], ALU.add).then_inc(fac_ready, 1)
            v.wait_ge(fac_turned, 1)
            v.tensor_copy(affine[:].rearrange("p l a k -> p (l a k)"), bank[7][:, 0:8 * NE]).then_inc(affine_ready, 1)
            with v.Fori(0, NI) as i:
                v.wait_ge(logits_turned, i + 1)
                v.tensor_copy(we[:, bass.ds(i * 2, 2), :].rearrange("p t e -> p (t e)"), bank[7][:, 0:2 * NE]
                              ).then_inc(logits_taken, 1)
            v.wait_ge(logits_taken, NI)
            ch.link(v.tensor_reduce(top[:], we[:], AX.X, ALU.max))
            v.tensor_tensor(we[:], we[:], top[:].unsqueeze(2).broadcast_to([P, NT, NE]), ALU.subtract).then_inc(centred, 1)
            v.wait_ge(exped, 1)
            ch.link(v.tensor_reduce(tot[:], we[:], AX.X, ALU.add))
            ch.link(v.reciprocal(tot[:], tot[:]))
            ch.link(v.tensor_tensor(we[:], we[:], tot[:].unsqueeze(2).broadcast_to([P, NT, NE]), ALU.mult))
            v.wait_ge(w_in, 16 * 9)
            with v.Fori(0, NI) as i:
                ch.enter(i, 2 * (NE - 1))

                def weight(s, e):
                    return we[:, bass.ds(i * 2 + s, 1), e:e + 1].rearrange("p a b -> p (a b)")

                v.wait_ge(x_in_sem, i * 16 + 16)
                v.wait_ge(stored, i * 16)
                for e in range(NE):
                    for s in range(2):
                        ins = v.scalar_tensor_tensor(o[:, s, :], bo[:, e, :], weight(s, e), (x if e == 0 else o)[:, s, :],
                                                     ALU.mult, ALU.add)
                        if e == 0:
                            ins.then_inc(started, 1)
                        else:
                            ch.done(ins)
                    if e == 0:
                        v.wait_ge(started, i * 2 + 2)
                    else:
                        ch.settle()
                for e in range(NE):
                    v.wait_ge(y_made, i * NE + e + 1)
                    v.wait_ge(y_added, i * 2 * NE + 2 * e)
                    for s in range(2):
                        v.scalar_tensor_tensor(o[:, s, :], bank[4 + e % 2][:, s * D:(s + 1) * D], weight(s, e), o[:, s, :],
                                               ALU.mult, ALU.add).then_inc(y_added, 1)
                ch.leave(NI)
def padded_inputs(nc, sem, c, x, types, x_pad, types_pad):
    rest = (NP - N)
    with ExitStack() as ctx:
        z = ctx.enter_context(nc.sbuf_tensor("pad_types", [1, rest], I32))
        cleared, stored = sem("pad_cleared"), sem("pad_stored")
        block = ctx.enter_context(nc.Block())

        @block.vector
        def _(v):
            v.memset(z[:], 0).then_inc(cleared, 1)

        @block.sync
        def _(sp):
            sp.dma_start(x_pad[0:N, :], x).then_inc(stored, 16)
            sp.dma_start(types_pad[0:N], types).then_inc(stored, 16)
            sp.wait_ge(c["ready"], c["n"])
            sp.dma_start(x_pad[N:N + P, :], c["zero"][:, 0:D]).then_inc(stored, 16)
            sp.dma_start(x_pad[N + P:NP, :], c["zero"][0:rest - P, 0:D]).then_inc(stored, 16)
            sp.wait_ge(cleared, 1)
            sp.dma_start(types_pad[N:NP].unsqueeze(0), z[:]).then_inc(stored, 16)
            sp.wait_ge(stored, 80)


def stage(build, nc, *args):
    taken = []

    def sem(name):
        taken.append(nc.alloc_semaphore(name=name))
        return taken[-1]

    build(nc, sem, *args)
    nc.all_engine_barrier()
    nc.clear_and_free_semaphores(taken)
    nc.all_engine_barrier()


def graph_network(nc, args, out):
    def scratch(name, shape, dt=F32):
        return nc.dram_tensor(name, shape, dt).ap()

    L0 = {k[3:]: v for k, v in args.items() if k.startswith("L0_")}
    L1 = {k[3:]: v for k, v in args.items() if k.startswith("L1_")}
    gnn0, mix0, ffn0 = ({k[4:]: v for k, v in L0.items() if k.startswith(g)} for g in ("gnn_", "mix_", "ffn_"))
    gnn1, mix1, ffn1 = ({k[4:]: v for k, v in L1.items() if k.startswith(g)} for g in ("gnn_", "mix_", "ffn_"))

    dram = dict(
        tile_rows=scratch("tile_rows", (T, 5 * P)), starts=scratch("starts", (T,)), rel_rows=scratch("rel_rows", (T, P)),
        mask=scratch("run_ends", (T, H, P + 1)), keys=scratch("carry_keys", (T,)), blocks=scratch("step_blocks", (T,), I32),
        cols=scratch("edge_columns", (P, T // G, 5, G)), table=scratch("edge_table", (R * NP, 2 * D)),
        q=scratch("queries", (NP, D)), sums=scratch("node_sums", (NP, CW)), carry=scratch("carried", (T, CW)),
        types=scratch("types_padded", (NP,), I32), router=scratch("router", (NP,)))
    x0, x1, x2, x3 = (scratch(f"x{n}", (NP, D)) for n in range(4))
    xn1, xn2 = scratch("xn1", (NP, D)), scratch("xn2", (NP, D))
    q1, y1, s1 = scratch("q1", (NP, D)), scratch("y1", (NP, HID)), scratch("s1", (NP, HID))
    z2, s2 = scratch("z2", (NP, 2)), scratch("s2", (NP, 2))
    xt_kept = scratch("xt_kept", (P, 2, NP))

    with ExitStack() as ctx:
        def sb(name, shape, dt=F32):
            return ctx.enter_context(nc.sbuf_tensor(name, shape, dt))

        psum = ctx.enter_context(nc.psum_tensor("psum", [P, 8, 512], F32))
        bank = [psum[:, b, :] for b in range(8)]
        c = constants(nc, sb, lambda name: ctx.enter_context(nc.semaphore(name)))
        wmix, dinv = sb("wmix", [P, 2, D]), sb("dinv", [P, NT])
        ksum, kvm = sb("ksum", [P, D]), sb("kvm", [P, 2, D])
        zt, zn = sb("zt", [P, NT, 2]), sb("zn", [P, NT, 2])

        stage(padded_inputs, nc, c, args["x"], args["node_type_4"], x0, dram["types"])
        stage(index_tables, nc, bank, c, dram, args["src"], args["dst"], args["edge_type_8"])
        with nc.sbuf_tensor("xt0", [P, 2, NP], F32) as xt:
            stage(layernorm_turned, nc, "ln0", bank, c, x0, xt)
            stage(edge_node_tables, nc, bank, c, xt, dict(
                k=gnn0["k_linears"], q=gnn0["q_linears"], v=gnn0["v_linears"], att=gnn0["relation_att"],
                msg=gnn0["relation_msg"], pri=gnn0["relation_pri"]), dram)
            stage(mix0_matrix, nc, psum, bank, c, xt, mix0["Wqkv"], mix0["Wout"], wmix)
            stage(move_turned, nc, "keep", xt[:], xt_kept)
        stage(attention_edges, nc, psum, bank, c, dram)
        stage(merge_carried, nc, psum, bank, c, dram)
        with nc.sbuf_tensor("xt1", [P, 2, NP], F32) as xt:
            stage(move_turned, nc, "restore", xt_kept, xt[:])
            stage(after_attention, nc, psum, bank, c, xt, wmix, dict(
                a=gnn0["a_linears"], skip=gnn0["skip"], bout=mix0["bout"]), dram, x0, x1, dinv)
            stage(layernorm_turned, nc, "ln1", bank, c, x1, xt, xn1)
            stage(routed_ffn, nc, psum, bank, c, xt, ffn0, dram, x1, xn1, x2)
        w1 = dict(mix1, W1=gnn1["W1"], bd=gnn1["bd"], Wd=gnn1["Wd"])
        with nc.sbuf_tensor("xt2", [P, 2, NP], F32) as xt:
            stage(layernorm_turned, nc, "ln2", bank, c, x2, xt, xn2)
            stage(project_layer1, nc, psum, bank, c, xt, w1, xn2, q1, y1, dinv, ksum, kvm)
        stage(gcn_edges, nc, psum, bank, c, dram, "g1", HID, y1, s1)
        stage(gcn_norm, nc, psum, bank, c, "n1", HID, s1, y1, dinv, (gnn1["b1"], gnn1["g1"], gnn1["be1"]), True,
                 gnn1["W2"], (z2, zt))
        stage(gcn_edges, nc, psum, bank, c, dram, "g2", 2, z2, s2)
        stage(gcn_norm, nc, psum, bank, c, "n2", 2, s2, z2, dinv, (gnn1["b2"], gnn1["g2"], gnn1["be2"]), False,
                 None, (None, zn))
        stage(finish_layer1, nc, psum, bank, c, w1, x2, xn2, q1, zn, ksum, kvm, x3)
        with nc.sbuf_tensor("xt3", [P, 2, NP], F32) as xt:
            stage(layernorm_turned, nc, "ln3", bank, c, x3, xt)
            stage(expert_mixture, nc, psum, bank, c, xt, ffn1, x3, out)


def move_turned(nc, sem, name, src, dst):
    moved = sem(f"{name}_moved")
    with nc.Block() as block:
        @block.sync
        def _(sp):
            for cc in range(2):
                sp.dma_start(dst[:, cc], src[:, cc]).then_inc(moved, 16)
            sp.wait_ge(moved, 32)



def kernel(**inputs):
    import concourse.bacc as bacc
    from concourse.bass_utils import run_bass_kernel_spmd

    nc = bacc.Bacc("TRN2", target_bir_lowering=False, num_devices=1)
    arrays, args = {}, {}
    for name in inputs:
        if name == "L0_ffn_attention_mask":
            continue
        a = np.ascontiguousarray(inputs[name])
        arrays[f"in_{name}"] = a
        args[name] = nc.dram_tensor(f"in_{name}", a.shape, mybir.dt.from_np(a.dtype), kind="ExternalInput").ap()
    out = nc.dram_tensor("out", (N, D), F32, kind="ExternalOutput").ap()
    graph_network(nc, args, out)
    return run_bass_kernel_spmd(nc, [arrays], core_ids=[0]).results[0]["out"]
```

```python
from contextlib import ExitStack

import numpy as np
import concourse.bass as bass
from concourse import mybir

F32 = mybir.dt.float32
I32 = mybir.dt.int32
U32 = mybir.dt.uint32
ALU = mybir.AluOpType
ACT = mybir.ActivationFunctionType
AX = mybir.AxisListType

P = 128
N = 6250
D = 256
E = 200000
NT = 50
NP = NT * P
NB = 50
BW = 127
RB = 13
T = RB * P
G = 8
GROUPS = 204
FULL = E // P
REST = E - FULL * P
NEG = -1.0e30
R, H, DK = 8, 4, 64
C_CNT, C_LAST, C_M, C_EX, C_V = 0, 1, 2, 6, 10
CW = C_V + D


class Chain:

    def __init__(self, eng, sem):
        self.eng, self.sem, self.n, self.base = eng, sem, 0, 0

    def done(self, ins):
        ins.then_inc(self.sem, 1)
        self.n += 1
        return ins

    def settle(self):
        self.eng.wait_ge(self.sem, self.base + self.n)

    def link(self, ins):
        self.done(ins)
        self.settle()

    def enter(self, i, per):
        self.outer, self.per = self.n, per
        self.base, self.n = i * per + self.outer, 0

    def leave(self, count):
        assert self.n == self.per, (self.n, self.per)
        self.base, self.n = 0, self.outer + count * self.per


def wait_alone(eng, gate):
    eng.sem_inc(gate, 1)


def wait_after(eng, sems, i, s, back=0, per=1, less=0):
    j = s - back
    count = (i + j // len(sems) + 1) * per - less
    if not (isinstance(count, int) and count <= 0):
        eng.wait_ge(sems[j % len(sems)], count)


def wait_count(eng, sem, count):
    if not (isinstance(count, int) and count <= 0):
        eng.wait_ge(sem, count)


def in_turns(eng, groups, slots, parts):
    most = max(ahead for ahead, _ in parts)
    least = min(ahead for ahead, _ in parts)
    assert most <= slots and least >= -slots and groups % slots == 0

    def written_out(turns):
        for k in turns:
            for ahead, part in parts:
                if 0 <= k + ahead < groups:
                    part((k + ahead) // slots, (k + ahead) % slots)

    written_out(range(-most, slots))
    with eng.Fori(1, groups // slots - 1) as i:
        for s in range(slots):
            for ahead, part in parts:
                part(i + (s + ahead) // slots, (s + ahead) % slots)
    written_out(range(groups - slots, groups - least))


def index_tables(nc, sem, bank, c, dram, src, dst, etype):
    with ExitStack() as ctx:
        def sbt(name, shape, dt=F32):
            return ctx.enter_context(nc.sbuf_tensor(name, shape, dt))

        raw = sbt("raw_edges", [P, 4, RB, P], I32)
        prev_i = sbt("prev_i", [P, RB], I32)
        prev = sbt("prev", [P, RB])
        dn = sbt("dst_next", [P, RB, P])
        et = sbt("etype_f", [P, RB, P])
        tab = sbt("tile_rows_s", [P, RB, 5, P])
        c0 = sbt("continues0", [P, RB])
        cmp = sbt("block_cmp", [P, RB, NB - 1])
        edge_of = sbt("block_edges", [P, RB, NB - 1])
        fb = sbt("first_block", [P, RB])
        start_row = sbt("start_row", [P, T])
        cmp_row = sbt("cmp_row", [P, T])
        cnt = sbt("cnt", [P, RB])
        tile_f = sbt("tile_f", [P, RB])
        tile_i = sbt("tile_i", [P, RB], I32)
        blk = sbt("blk", [P, RB])
        blk_i = sbt("blk_i", [P, RB], I32)
        st = sbt("step_rows", [P, RB, 5, P])
        rel = sbt("rel", [P, RB, P])
        inb = sbt("inb", [P, RB, P])
        rels = sbt("rels", [P, RB, P])
        mask = sbt("mask_s", [P, RB, P + 1])
        key = sbt("key", [P, RB])
        cin = sbt("cin", [P, RB])
        cols = sbt("cols_s", [P, T // G, 5, G], F32)

        loaded, filled, dve, tabled, started, rowed = (sem(x) for x in (
            "edges_loaded", "edges_filled", "index_chain", "tile_rows_written", "starts_written", "start_row_loaded"))
        ready, gathered, turned, copied, stored = (sem(x) for x in (
            "step_tiles_ready", "step_rows_gathered", "columns_turned", "columns_copied", "tables_stored"))
        written = sem("tile_rows_ready")
        starts = sem("starts_ready")
        inblock = sem("block_columns_ready")
        block = ctx.enter_context(nc.Block())

        @block.sync
        def _(sp):
            sp.wait_ge(filled, 3)
            for n, (a, off) in enumerate(((dst, 0), (dst, 1), (src, 0), (etype, 0))):
                sp.dma_start(raw[:, n, 0:12, :], a[off:off + 12 * P * P].rearrange("(b p j) -> p b j", p=P, j=P)).then_inc(loaded, 16)
                rows = FULL - 12 * P
                sp.dma_start(raw[0:rows, n, 12, :],
                             a[off + 12 * P * P:off + FULL * P].rearrange("(p j) -> p j", j=P)).then_inc(loaded, 16)
                sp.dma_start(raw[rows:rows + 1, n, 12, 0:REST - off],
                             a[FULL * P + off:E].rearrange("(a j) -> a j", a=1)).then_inc(loaded, 16)
            last = dst[0:FULL * P].rearrange("(t j) -> t j", j=P)[:, P - 1:P]
            sp.dma_start(prev_i[1:P, 0:1], last[0:P - 1, :], allow_slow_non_contiguous=True).then_inc(loaded, 16)
            for b in range(1, RB):
                rows = min(P, FULL - (b * P - 1))
                sp.dma_start(prev_i[0:rows, b:b + 1], last[b * P - 1:b * P - 1 + rows, :],
                             allow_slow_non_contiguous=True).then_inc(loaded, 16)
            sp.wait_ge(written, 1)
            sp.dma_start(dram["tile_rows"].rearrange("(b p) n -> p b n", p=P),
                         tab[:].rearrange("p b c j -> p b (c j)")).then_inc(tabled, 16)
            sp.wait_ge(starts, 1)
            sp.dma_start(dram["starts"].rearrange("(b p) -> p b", p=P), fb[:], allow_slow_non_contiguous=True).then_inc(started, 16)
            sp.wait_ge(started, 16)
            sp.dma_start(start_row[:], dram["starts"].rearrange("(a n) -> a n", a=1).broadcast_to([P, T])
                         ).then_inc(rowed, 16)
            sp.wait_ge(inblock, 1)
            sp.dma_start(dram["rel_rows"].rearrange("(b p) j -> p b j", p=P), rel[:]).then_inc(stored, 16)
            for b in range(RB):
                sp.dma_start(dram["mask"][b * P:(b + 1) * P, :, :],
                             mask[:, b, :].unsqueeze(1).broadcast_to([P, H, P + 1])).then_inc(stored, 16)
            sp.dma_start(dram["keys"].rearrange("(b p) -> p b", p=P), key[:], allow_slow_non_contiguous=True).then_inc(stored, 16)
            sp.dma_start(dram["blocks"].rearrange("(b p) -> p b", p=P), blk_i[:], allow_slow_non_contiguous=True).then_inc(stored, 16)
            sp.wait_ge(copied, RB)
            sp.dma_start(dram["cols"].rearrange("p k c g -> p (k c g)"),
                         cols[:].rearrange("p k c g -> p (k c g)")).then_inc(stored, 16)
            sp.wait_ge(stored, 16 * (4 + RB))

        @block.vector
        def _(v):
            ch = Chain(v, dve)
            v.memset(raw[:, 0:2, :, :], N).then_inc(filled, 1)
            v.memset(raw[:, 2:4, :, :], 0).then_inc(filled, 1)
            v.memset(prev_i[:], -1).then_inc(filled, 1)
            v.wait_ge(loaded, 16 * (12 + RB))
            d_, s_, k_, l_, c_ = (tab[:, :, x, :] for x in range(5))
            ch.done(v.tensor_copy(d_, raw[:, 0]))
            ch.done(v.tensor_copy(dn[:], raw[:, 1]))
            ch.done(v.tensor_copy(s_, raw[:, 2]))
            ch.done(v.tensor_copy(et[:], raw[:, 3]))
            ch.link(v.tensor_copy(prev[:], prev_i[:]))
            v.wait_ge(c["ready"], c["n"])
            ch.done(v.tensor_tensor(l_, d_, dn[:], ALU.not_equal))
            ch.done(v.scalar_tensor_tensor(k_, et[:], float(NP), s_, ALU.mult, ALU.add))
            ch.done(v.tensor_tensor(c_, d_, tab[:, :, 0, 0:1].broadcast_to([P, RB, P]), ALU.is_equal))
            ch.done(v.tensor_tensor(c0[:], tab[:, :, 0, 0], prev[:], ALU.is_equal))
            ch.done(v.tensor_scalar(edge_of[:], c["iota"][:, 0:NB - 1].unsqueeze(1).broadcast_to([P, RB, NB - 1]),
                                    float(BW), float(BW), ALU.mult, ALU.add))
            ch.settle()
            ch.done(v.memset(tab[:, :, 3, P - 1:P], 1.0))
            ch.done(v.tensor_tensor(c_, c_, c0[:].unsqueeze(2).broadcast_to([P, RB, P]), ALU.mult))
            ch.done(v.tensor_tensor(cmp[:], edge_of[:], tab[:, :, 0, 0:1].broadcast_to([P, RB, NB - 1]), ALU.is_le))
            ch.settle()
            v.tensor_copy(tile_f[:], c["tile_no"][:]).then_inc(written, 1)
            ch.link(v.tensor_reduce(fb[:], cmp[:], AX.X, ALU.add))
            v.tensor_tensor(fb[:], fb[:], c["tile_no"][:], ALU.add).then_inc(starts, 1)
            v.wait_ge(rowed, 16)
            for b in range(RB):
                ch.link(v.tensor_scalar(cmp_row[:], start_row[:], c["tile_no"][:, b:b + 1], 0.0,
                                        ALU.is_le, ALU.add, accum_out=cnt[:, b:b + 1]))
            ch.link(v.tensor_scalar(tile_f[:], cnt[:], -1.0, 0.0, ALU.add, ALU.max))
            v.tensor_copy(tile_i[:], tile_f[:]).then_inc(ready, 1)
            ch.link(v.tensor_tensor(blk[:], c["tile_no"][:], tile_f[:], ALU.subtract))
            ch.done(v.tensor_copy(blk_i[:], blk[:]))
            ch.link(v.tensor_scalar(blk[:], blk[:], float(-BW), None, ALU.mult))
            v.wait_ge(gathered, 16 * RB)
            ch.link(v.tensor_tensor(rel[:], st[:, :, 0, :], blk[:].unsqueeze(2).broadcast_to([P, RB, P]), ALU.add))
            ch.done(v.tensor_scalar(inb[:], rel[:], 0.0, None, ALU.is_ge))
            ch.link(v.tensor_scalar(rels[:], rel[:], float(BW - 1), None, ALU.is_le))
            ch.link(v.tensor_tensor(inb[:], inb[:], rels[:], ALU.mult))
            ch.link(v.tensor_scalar(rels[:], rel[:], -1.0, float(BW), ALU.mult, ALU.add))
            ch.link(v.tensor_tensor(rels[:], rels[:], st[:, :, 4, :], ALU.mult))
            ch.link(v.tensor_tensor(rels[:], rels[:], rel[:], ALU.add))
            ch.link(v.scalar_tensor_tensor(rels[:], rels[:], -999.0, inb[:], ALU.add, ALU.mult))
            ch.done(v.tensor_scalar(rels[:], rels[:], 999.0, None, ALU.add))
            ch.done(v.memset(mask[:, :, 0:1], NEG))
            ch.done(v.tensor_scalar(mask[:, :, 1:P + 1], st[:, :, 3, :], NEG, None, ALU.mult))
            ch.link(v.tensor_tensor(cin[:], inb[:, :, 0], st[:, :, 4, 0], ALU.mult))
            ch.link(v.scalar_tensor_tensor(key[:], st[:, :, 0, 0], 1.0, cin[:], ALU.add, ALU.mult))
            v.tensor_scalar(key[:], key[:], -1.0, None, ALU.add).then_inc(inblock, 1)
            for b in range(RB):
                v.wait_ge(turned, b + 1)
                k0, k1 = b * P // G, (b + 1) * P // G
                view = cols[:, k0:k1, :, :]
                for x in range(5):
                    o = view[:, :, x, :]
                    if x < 2:
                        o = o.bitcast(I32)
                    ch.done(v.tensor_copy(o, bank[2 * (b % 2) + x // 4][:, (x % 4) * P:(x % 4 + 1) * P]
                                          .rearrange("p (k g) -> p k g", g=G)))
                ch.settle()
                v.tensor_copy(tile_f[:, 0:1], cnt[:, 0:1]).then_inc(copied, 1)

        @block.gpsimd
        def _(g):
            g.wait_ge(ready, 1)
            g.wait_ge(tabled, 16)
            for b in range(RB):
                g.indirect_dma_start(out=st[:, b, :, :].rearrange("p c j -> p (c j)"), out_offset=None,
                                     in_=dram["tile_rows"],
                                     in_offset=bass.IndirectOffsetOnAxis(ap=tile_i[:, b:b + 1].bitcast(U32), axis=0)
                                     ).then_inc(gathered, 16)

        @block.tensor
        def _(t):
            t.wait_ge(c["ready"], c["n"])
            t.wait_ge(gathered, 16 * RB)
            t.wait_ge(inblock, 1)
            for b in range(RB):
                if b >= 2:
                    t.wait_ge(copied, b - 1)
                for x, a in enumerate((st[:, b, 2, :], st[:, b, 1, :], rels[:, b, :], rel[:, b, :], st[:, b, 3, :])):
                    ins = t.transpose(bank[2 * (b % 2) + x // 4][:, (x % 4) * P:(x % 4 + 1) * P], a, c["ident"][:])
                ins.then_inc(turned, 1)


def constants(nc, sb, sem):
    ident = sb("ident", [P, P])
    iota_i = sb("iota_i", [P, P], I32)
    iota = sb("iota", [P, P])
    pcol_i = sb("pcol_i", [P, 1], I32)
    pcol = sb("pcol", [P, 1])
    tile_no_i = sb("tile_no_i", [P, RB], I32)
    tile_no = sb("tile_no", [P, RB])
    ones = sb("ones", [P, P])
    zero = sb("zero", [P, 512])
    made, ready = sem("iotas_made"), sem("constants_ready")
    with nc.Block() as block:
        @block.gpsimd
        def _(g):
            g.memset(ident[:], 0.0).then_inc(made, 1)
            g.iota(iota_i[:], pattern=[[1, P]], base=0, channel_multiplier=0).then_inc(made, 1)
            g.iota(pcol_i[:], pattern=[[0, 1]], base=0, channel_multiplier=1).then_inc(made, 1)
            g.iota(tile_no_i[:], pattern=[[P, RB]], base=0, channel_multiplier=1).then_inc(made, 1)
            g.wait_ge(made, 4)
            g.affine_select(out=ident[:], in_=ident[:], compare_op=ALU.not_equal, fill=1.0, base=0,
                            pattern=[[-1, P]], channel_multiplier=1).then_inc(ready, 1)

        @block.vector
        def _(v):
            v.wait_ge(made, 4)
            v.tensor_copy(iota[:], iota_i[:]).then_inc(ready, 1)
            v.tensor_copy(pcol[:], pcol_i[:]).then_inc(ready, 1)
            v.tensor_copy(tile_no[:], tile_no_i[:]).then_inc(ready, 1)
            v.memset(ones[:], 1.0).then_inc(ready, 1)
            v.memset(zero[:], 0.0).then_inc(ready, 1)
    return dict(ident=ident, iota=iota, pcol=pcol, tile_no=tile_no, ones=ones, zero=zero, ready=ready, n=6)

EPS_LN = 1e-5


LT = 5


def layernorm_turned(nc, sem, name, bank, c, x_dram, xt, xn_dram=None):
    with ExitStack() as ctx:
        def sbt(nm, shape, dt=F32):
            return ctx.enter_context(nc.sbuf_tensor(f"{name}_{nm}", shape, dt))

        def pair(nm):
            return [sem(f"{name}_{nm}{s}") for s in range(2)]

        groups = NT // LT
        x = sbt("x", [P, 2, LT, D])
        xn = sbt("xn", [P, 2, LT, D])
        stats = sbt("stats", [P, 2, LT, 6])
        mv = sbt("mv", [P, 2, LT, 2])
        sd = sbt("sd", [P, 2, LT])
        rs = sbt("rs", [P, 2, LT])
        eps = sbt("eps", [P, 1])
        x_in, stats_made, var_ready, sd_ready, rs_ready, xn_ready, turned, taken, stored = (
            pair(n) for n in ("x_in", "stats", "var", "sd", "rs", "xn", "turned", "taken", "stored"))
        eps_ready = sem(f"{name}_eps")
        gate = sem(f"{name}_gate")
        block = ctx.enter_context(nc.Block())
        rows = x_dram.rearrange("(g t p) d -> g p t d", p=P, t=LT)

        @block.sync
        def _(sp):
            with sp.Fori(0, groups // 2) as i:
                for s in range(2):
                    sp.wait_ge(xn_ready[s], i * LT)
                    sp.dma_start(x[:, s], rows[bass.ds(i * 2 + s, 1)].rearrange("g p t d -> (g p) t d")
                                 ).then_inc(x_in[s], 16)

        @block.gpsimd
        def _(g):
            if xn_dram is not None:
                out = xn_dram.rearrange("(g t p) d -> g p t d", p=P, t=LT)
                with g.Fori(0, groups // 2) as i:
                    for s in range(2):
                        g.wait_ge(xn_ready[s], i * LT + LT)
                        g.dma_start(out[bass.ds(i * 2 + s, 1)].rearrange("g p t d -> (g p) t d"), xn[:, s]
                                    ).then_inc(stored[s], 16)
                for s in range(2):
                    g.wait_ge(stored[s], groups // 2 * 16)

        @block.vector
        def _(v):
            def statistics(i, s):
                wait_after(v, x_in, i, s, per=16)
                for n in range(LT):
                    v.bn_stats(stats[:, s, n, :], x[:, s, n, :]).then_inc(stats_made[s], 1)
                wait_after(v, stats_made, i, s, per=LT)
                wait_after(v, sd_ready, i, s, 2)
                wait_alone(v, gate)
                for n in range(LT):
                    v.bn_aggr(mv[:, s, n, :], stats[:, s, n, :]).then_inc(var_ready[s], 1)

            def normalise(i, s):
                wait_after(v, sd_ready, i, s)
                v.reciprocal(rs[:, s], sd[:, s]).then_inc(rs_ready[s], 1)
                wait_after(v, rs_ready, i, s)
                wait_after(v, turned, i, s, 2)
                if xn_dram is not None:
                    wait_after(v, stored, i, s, 2, per=16)
                for n in range(LT):
                    v.tensor_scalar(xn[:, s, n, :], x[:, s, n, :], mv[:, s, n, 0:1], rs[:, s, n:n + 1],
                                    ALU.subtract, ALU.mult).then_inc(xn_ready[s], 1)

            def take(i, s):
                wait_after(v, turned, i, s)
                for cc in range(2):
                    for n in range(3):
                        w = min(2, LT - 2 * n)
                        v.tensor_copy(xt[:, cc, bass.ds((i * 2 + s) * LT * P + 2 * n * P, w * P)]
                                      .rearrange("p (t n) -> p t n", n=P),
                                      bank[3 * s + n][:, 0:w * D].rearrange("p (t c n) -> p t c n", c=2, n=P)[:, :, cc, :]
                                      ).then_inc(taken[s], 1)

            v.memset(eps[:], EPS_LN).then_inc(eps_ready, 1)
            in_turns(v, groups, 2, ((0, normalise), (1, statistics), (-1, take)))

        @block.scalar
        def _(a):
            a.wait_ge(eps_ready, 1)
            with a.Fori(0, groups // 2) as i:
                for s in range(2):
                    a.wait_ge(var_ready[s], i * LT + LT)
                    a.wait_ge(rs_ready[s], i)
                    a.activation(sd[:, s, :], mv[:, s, :, 1], ACT.Sqrt, bias=eps[:]).then_inc(sd_ready[s], 1)

        @block.tensor
        def _(t):
            with t.Fori(0, groups // 2) as i:
                for s in range(2):
                    t.wait_ge(taken[s], i * 6)
                    for n in range(LT):
                        t.wait_ge(xn_ready[s], i * LT + n + 1)
                        for cc in range(2):
                            ins = t.transpose(bank[3 * s + n // 2][:, (n % 2) * D + cc * P:(n % 2) * D + (cc + 1) * P],
                                              xn[:, s, n, cc * P:(cc + 1) * P], c["ident"][:])
                    ins.then_inc(turned[s], 1)


def edge_node_tables(nc, sem, bank, c, xt, w, dram):
    with ExitStack() as ctx:
        def sbt(nm, shape, dt=F32):
            return ctx.enter_context(nc.sbuf_tensor(f"tb_{nm}", shape, dt))

        def pair(nm):
            return [sem(f"tb_{nm}{s}") for s in range(2)]

        wk = sbt("wk", [P, 2, 4, D])
        wq = sbt("wq", [P, 2, 4, D])
        wv = sbt("wv", [P, 2, 4, D])
        bd = sbt("bd", [P, 2, R, P])
        rt = sbt("rt", [P, 2, 2, R, P])
        pri = sbt("pri", [P, R * H])
        types = sbt("types", [P, 2, P], I32)
        mask = sbt("mask", [P, 4, P])
        xm = sbt("xm", [P, 2, 2, 4, P])
        kv = sbt("kv", [P, 2, 2, 2, P])
        q = sbt("q", [P, 2, D])
        tab = sbt("tab", [P, 2, R, 2 * D])
        w_in, w_made, w_turned = sem("tb_weights"), sem("tb_weights_made"), sem("tb_weights_turned")
        types_in, masked, q_made, kv_made, kv_taken = (pair(n) for n in ("types", "masked", "q_made", "kv_made", "kv_taken"))
        mask_made, q_stored = pair("mask_made"), pair("q_stored")
        q_taken, table_made, low_taken, high_taken, stored = (
            pair(n) for n in ("q_taken", "table_made", "low_taken", "high_taken", "stored"))
        zeroed = sem("tb_zeroed")
        dve = sem("tb_chain")
        LOADS = 6 + 1 + 8
        block = ctx.enter_context(nc.Block())
        table = dram["table"].rearrange("(r t p) n -> t p r n", r=R, p=P)

        @block.sync
        def _(sp):
            for dst_, src_ in ((wk, w["k"]), (wq, w["q"]), (wv, w["v"])):
                for cc in range(2):
                    sp.dma_start(dst_[:, cc], src_[:, cc * P:(cc + 1) * P, :].rearrange("t p o -> p t o")
                                 ).then_inc(w_in, 16)
            sp.dma_start(pri[:], w["pri"].rearrange("r h -> (r h)").unsqueeze(0).broadcast_to([P, R * H])
                         ).then_inc(w_in, 16)
            sp.wait_ge(zeroed, 2)
            for cc in range(2):
                for hh in range(2):
                    a, b = hh * DK, (hh + 1) * DK
                    sp.dma_start(bd[a:b, cc, :, a:b], w["att"][:, 2 * cc + hh].rearrange("r d e -> d r e")
                                 ).then_inc(w_in, 16)
                    sp.dma_start(rt[a:b, cc, 1, :, a:b], w["msg"][:, 2 * cc + hh].rearrange("r d e -> d r e")
                                 ).then_inc(w_in, 16)
            with sp.Fori(0, NT // 2) as i:
                for s in range(2):
                    sp.wait_ge(masked[s], i)
                    sp.dma_start(types[:, s, :], dram["types"][bass.ds(i * 2 * P + s * P, P)].unsqueeze(0)
                                 .broadcast_to([P, P])).then_inc(types_in[s], 16)

        @block.gpsimd
        def _(g):
            def store(i, s):
                k = i * 2 + s
                wait_after(g, q_taken, i, s)
                g.dma_start(dram["q"][bass.ds(k * P, P), :], q[:, s, :]).then_inc(q_stored[s], 16)
                wait_after(g, low_taken, i, s, per=4)
                wait_after(g, high_taken, i, s, per=4)
                g.dma_start(table[bass.ds(k, 1)].rearrange("t p r n -> (t p) r n"), tab[:, s, :, :]
                            ).then_inc(stored[s], 16)

            in_turns(g, NT, 2, ((0, store),))
            for s in range(2):
                g.wait_ge(stored[s], NT // 2 * 16)
                g.wait_ge(q_stored[s], NT // 2 * 16)

        @block.vector
        def _(v):
            ch = Chain(v, dve)
            v.memset(bd[:], 0.0).then_inc(zeroed, 1)
            v.memset(rt[:], 0.0).then_inc(zeroed, 1)
            v.wait_ge(w_in, 16 * LOADS)
            for cc in range(2):
                for half in range(2):
                    b = cc * 2 + half
                    v.wait_ge(w_turned, b + 1)
                    rr = slice(half * 4, half * 4 + 4)
                    ch.link(v.tensor_scalar(rt[:, cc, 0, rr, :], bank[b][:].rearrange("p (r n) -> p r n", r=4),
                                            float(DK) ** -0.5, None, ALU.mult))
                    for hh in range(2):
                        o = rt[:, cc, 0, rr, hh * DK:(hh + 1) * DK]
                        ph = pri[:].rearrange("p (r h) -> p r h", h=H)[:, rr, 2 * cc + hh:2 * cc + hh + 1]
                        v.tensor_tensor(o, o, ph.broadcast_to([P, 4, DK]), ALU.mult).then_inc(w_made, 1)

            def masked_rows(i, s):
                wait_after(v, types_in, i, s, per=16)
                wait_after(v, masked, i, s, 1)
                v.tensor_tensor(mask[:], types[:, s, :].unsqueeze(1).broadcast_to([P, 4, P]),
                                c["iota"][:, 0:4].unsqueeze(2).broadcast_to([P, 4, P]), ALU.is_equal).then_inc(mask_made[s], 1)
                wait_after(v, mask_made, i, s)
                wait_after(v, kv_made, i, s, 2)
                v.tensor_tensor(xm[:, s], xt[:, :, bass.ds((i * 2 + s) * P, P)].unsqueeze(2)
                                .broadcast_to([P, 2, 4, P]), mask[:].unsqueeze(1).broadcast_to([P, 2, 4, P]),
                                ALU.mult).then_inc(masked[s], 1)

            def take_kv(i, s):
                wait_after(v, kv_made, i, s)
                wait_after(v, table_made, i, s, 2, per=8)
                v.tensor_copy(kv[:, s].rearrange("p a c n -> p (a c n)"), bank[1][:]).then_inc(kv_taken[s], 1)

            def low(i, s):
                wait_after(v, stored, i, s, 2, per=16)
                for n in range(4):
                    wait_after(v, table_made, i, s, per=8, less=7 - 2 * n)
                    kind, cc = n // 2, n % 2
                    v.tensor_copy(tab[:, s, 0:4, kind * D + cc * P:kind * D + cc * P + P],
                                  bank[2 + (2 * n) % 6][:].rearrange("p (r n) -> p r n", r=4)
                                  ).then_inc(low_taken[s], 1)

            in_turns(v, NT, 2, ((1, take_kv), (2, masked_rows), (0, low)))

        @block.scalar
        def _(a):
            def take_q(i, s):
                wait_after(a, q_made, i, s)
                wait_after(a, q_stored, i, s, 2, per=16)
                a.activation(q[:, s, :], bank[0][:, 0:D], ACT.Copy).then_inc(q_taken[s], 1)

            def high(i, s):
                wait_after(a, stored, i, s, 2, per=16)
                for n in range(4):
                    wait_after(a, table_made, i, s, per=8, less=6 - 2 * n)
                    kind, cc = n // 2, n % 2
                    a.activation(tab[:, s, 4:8, kind * D + cc * P:kind * D + cc * P + P],
                                 bank[2 + (2 * n + 1) % 6][:].rearrange("p (r n) -> p r n", r=4), ACT.Copy
                                 ).then_inc(high_taken[s], 1)

            in_turns(a, NT, 2, ((1, take_q), (0, high)))

        @block.tensor
        def _(t):
            t.wait_ge(w_in, 16 * LOADS)
            for cc in range(2):
                for half in range(2):
                    for r in range(4):
                        ins = t.transpose(bank[cc * 2 + half][:, r * P:(r + 1) * P], bd[:, cc, half * 4 + r, :], c["ident"][:])
                    ins.then_inc(w_turned, 1)
            t.wait_ge(w_made, 8)

            def project(i, s):
                wait_after(t, masked, i, s)
                wait_after(t, q_taken, i, s, 1)
                for n in range(8):
                    ins = t.matmul(bank[0][:, 0:D], xm[:, s, n // 4, n % 4, :], wq[:, n // 4, n % 4, :],
                                   start=n == 0, stop=n == 7)
                ins.then_inc(q_made[s], 1)
                wait_after(t, kv_taken, i, s, 1)
                for kind, ww in enumerate((wk, wv)):
                    for o in range(2):
                        for n in range(8):
                            ins = t.matmul(bank[1][:, (kind * 2 + o) * P:(kind * 2 + o + 1) * P],
                                           ww[:, n // 4, n % 4, o * P:(o + 1) * P], xm[:, s, n // 4, n % 4, :],
                                           start=n == 0, stop=n == 7)
                ins.then_inc(kv_made[s], 1)

            def relate(i, s):
                wait_after(t, kv_taken, i, s)
                for m in range(8):
                    n, half = m // 2, m % 2
                    kind, cc = n // 2, n % 2
                    taken = (low_taken, high_taken)[half]
                    if m < 6:
                        wait_after(t, taken, i, s, 1, per=4)
                    else:
                        wait_after(t, taken, i, s, per=4, less=3)
                    t.matmul(bank[2 + m % 6][:], kv[:, s, kind, cc, :],
                             rt[:, cc, kind, half * 4:half * 4 + 4, :].rearrange("p r n -> p (r n)"),
                             start=True, stop=True).then_inc(table_made[s], 1)

            in_turns(t, NT, 2, ((1, project), (0, relate)))

SLOTS = 3
KC = D - C_V


PACK = 4
BITS = 6


def blocks_of(eng, packed, k):
    words = [eng.value_load(packed[0:1, bass.ds(k * (G // PACK) + m, 1)], min_val=0, max_val=2 ** (PACK * BITS) - 1)
             for m in range(G // PACK)]
    return [((words[n // PACK] >> (n % PACK * BITS)) & (2 ** BITS - 1)).with_bounds(min_val=0, max_val=NB - 1)
            for n in range(G)]


def pack_blocks(v, ch, blocks, packed_f, packed):
    four = blocks[:].rearrange("p (m n) -> p m n", n=PACK)
    ch.link(v.tensor_copy(packed_f[:], four[:, :, PACK - 1]))
    for n in range(PACK - 2, -1, -1):
        ch.link(v.scalar_tensor_tensor(packed_f[:], packed_f[:], float(2 ** BITS), four[:, :, n], ALU.mult, ALU.add))
    ch.link(v.tensor_copy(packed[:], packed_f[:]))


def attention_edges(nc, sem, psum, bank, c, dram):
    with ExitStack() as ctx:
        def sbt(nm, shape, dt=F32):
            return ctx.enter_context(nc.sbuf_tensor(f"ae_{nm}", shape, dt))

        def slots(nm):
            return [sem(f"ae_{nm}{s}") for s in range(SLOTS)]

        qb = sbt("q", [P, NB, D])
        acc = sbt("acc", [P, NB, CW])
        kv = sbt("kv", [P, SLOTS, G, 2 * D])
        index = sbt("index", [P, SLOTS, G])
        col = sbt("col", [P, SLOTS, 3, G])
        mk = sbt("mask", [G * H, SLOTS, P + 1])
        oht = sbt("node_hot", [P, SLOTS, G * P])
        ohs = sbt("edge_hot", [P, G, P])
        sc = sbt("scores", [P, SLOTS, G * H])
        fwd = sbt("fwd", [G * H, P])
        mx = sbt("max", [G * H, P])
        diff = sbt("diff", [G * H, P])
        step_sums = sbt("step_sums", [P, G, CW])
        blocks = sbt("blocks", [1, T], I32)
        packed_f, packed = sbt("packed_f", [1, T // PACK]), sbt("packed", [1, T // PACK], I32)
        less_p = sbt("less_partition", [P, 1])
        q_in, blocks_in, cleared, place_ready = (sem(f"ae_{n}") for n in ("q_in", "blocks_in", "cleared", "place_ready"))
        pack_chain, packed_ready = sem("ae_pack_chain"), sem("ae_packed_ready")
        index_in, rows_in, loaded, gathered, node_hot, expanded, scored, turned = (
            slots(n) for n in ("index_in", "rows_in", "loaded", "gathered", "node_hot", "expanded", "scored", "turned"))
        maxed, back, exps, weighted, edge_hot, marked = (
            slots(n) for n in ("maxed", "back", "exps", "weighted", "edge_hot", "marked"))
        multiplied, swept, edge_far = slots("multiplied"), slots("swept"), slots("edge_far")
        sum_made, sum_added, sum_copied = (sem(f"ae_{n}") for n in ("sum_made", "sum_added", "sum_copied"))
        carry_stored, acc_stored, gate = sem("ae_carry_stored"), sem("ae_acc_stored"), sem("ae_gate")
        t_gate = sem("ae_tensor_gate")
        block = ctx.enter_context(nc.Block())
        ITER = GROUPS // SLOTS

        @block.sync
        def _(sp):
            sp.dma_start(blocks[:], dram["blocks"].unsqueeze(0)).then_inc(blocks_in, 16)
            for b in range(NB):
                sp.dma_start(qb[:, b, :], dram["q"][b * BW:b * BW + P, :]).then_inc(q_in, 16)
            with sp.Fori(0, ITER) as i:
                for s in range(SLOTS):
                    k = i * SLOTS + s
                    sp.wait_ge(gathered[s], i * 16 * G)
                    sp.dma_start(index[:, s], dram["cols"][:, bass.ds(k, 1), 0].rearrange("p k g -> p (k g)")
                                 ).then_inc(index_in[s], 16)
                    sp.wait_ge(expanded[s], i)
                    sp.dma_start(oht[:, s, :], dram["rel_rows"][bass.ds(k * G, G)].rearrange("g n -> (g n)")
                                 .unsqueeze(0).broadcast_to([P, G * P])).then_inc(rows_in[s], 16)
                    sp.wait_ge(weighted[s], i * 2)
                    sp.wait_ge(edge_hot[s], i)
                    sp.dma_start(col[:, s], dram["cols"][:, bass.ds(k, 1), 2:5].rearrange("p k c g -> p (k c) g")
                                 ).then_inc(loaded[s], 16)
                    sp.dma_start(mk[:, s, :], dram["mask"][bass.ds(k * G, G)].rearrange("g h n -> (g h) n")
                                 ).then_inc(loaded[s], 16)
            sp.wait_ge(sum_added, GROUPS * G)
            for a, b in ((0, 112), (112, BW)):
                sp.dma_start(dram["sums"][0:NB * BW].rearrange("(b p) n -> p b n", p=BW)[a:b], acc[a:b]).then_inc(acc_stored, 16)
            sp.wait_ge(acc_stored, 32)

        @block.gpsimd
        def _(g):
            def gather(i, s, n):
                g.indirect_dma_start(out=kv[:, s, n, :], out_offset=None, in_=dram["table"],
                                     in_offset=bass.IndirectOffsetOnAxis(ap=index[:, s, n:n + 1].bitcast(U32), axis=0)
                                     ).then_inc(gathered[s], 16)

            g.memset(acc[:], 0.0).then_inc(cleared, 1)
            for s in range(SLOTS):
                g.wait_ge(index_in[s], 16)
                for n in range(G):
                    gather(0, s, n)
            with g.Fori(1, ITER) as i:
                for s in range(SLOTS):
                    g.wait_ge(index_in[s], i * 16 + 16)
                    for n in range(G):
                        g.wait_ge(sum_made, ((i - 1) * SLOTS + s) * G + n + 1)
                        wait_alone(g, gate)
                        gather(i, s, n)

        @block.vector
        def _(v):
            def turn(i, s, scores, rest, adds):
                iz, sz = i + (s + 1) // SLOTS, (s + 1) % SLOTS
                ia, sa = i + (s - 1) // SLOTS, (s - 1) % SLOTS
                if adds:
                    ka = ia * SLOTS + sa
                    at = blocks_of(v, packed, ka)

                def add(n):
                    if not adds:
                        return
                    v.wait_ge(sum_copied, ka * G + n + 1)
                    if n or not isinstance(ka, int) or ka:
                        v.wait_ge(sum_added, ka * G + n)
                    o = acc[:, bass.ds(at[n], 1), :].rearrange("p b n -> p (b n)")
                    v.tensor_tensor(o, o, step_sums[:, n, :], ALU.add).then_inc(sum_added, 1)

                if scores:
                    wait_after(v, gathered, iz, sz, per=16 * G)
                    wait_after(v, expanded, iz, sz)
                    k_ = kv[:, sz, :, 0:D]
                    v.tensor_tensor(k_, k_, psum[:, 0:4, :].rearrange("p b (t d) -> p (b t) d", d=D),
                                    ALU.mult).then_inc(multiplied[sz], 1)
                add(0)
                if rest:
                    wait_after(v, turned, i, s)
                    wait_after(v, loaded, i, s, per=32)
                    wait_after(v, back, i, s, 1)
                    st = bank[6][0:G * H, 0:P]
                    v.tensor_tensor_scan(fwd[:], mk[:, s, 0:P], st, NEG, ALU.add, ALU.max).then_inc(swept[s], 1)
                add(1)
                if rest:
                    wait_after(v, swept, i, s, per=2, less=1)
                    v.tensor_tensor_scan(mx[:, ::-1], mk[:, s, 1:P + 1][:, ::-1], fwd[:, ::-1], NEG, ALU.add, ALU.max
                                         ).then_inc(swept[s], 1)
                add(2)
                if rest:
                    wait_after(v, swept, i, s, per=2)
                    v.tensor_tensor(diff[:], st, mx[:], ALU.subtract).then_inc(maxed[s], 1)
                add(3)
                if scores:
                    wait_after(v, multiplied, iz, sz)
                    wait_after(v, turned, iz, sz, SLOTS)
                    v.tensor_reduce(sc[:, sz, :], kv[:, sz, :, 0:D].rearrange("p g (h d) -> p g h d", d=DK), AX.X, ALU.add
                                    ).then_inc(scored[sz], 1)
                add(4)
                if rest:
                    wait_after(v, back, i, s)
                    v.tensor_tensor(kv[:, s, :, KC + C_M:KC + C_EX],
                                    bank[6][:, P:P + G * H].rearrange("p (g h) -> p g h", h=H),
                                    col[:, s, 2, :].unsqueeze(2).broadcast_to([P, G, H]), ALU.mult).then_inc(weighted[s], 1)
                add(5)
                add(6)
                if rest:
                    wait_after(v, exps, i, s)
                    vv = kv[:, s, :, D:2 * D].rearrange("p g (h d) -> p g h d", h=H)
                    v.tensor_tensor(vv, vv, kv[:, s, :, KC + C_EX:KC + C_V].unsqueeze(3).broadcast_to([P, G, H, DK]),
                                    ALU.mult).then_inc(weighted[s], 1)
                add(7)

            ch = Chain(v, pack_chain)
            v.tensor_scalar(less_p[:], c["pcol"][:], -1.0, None, ALU.mult).then_inc(place_ready, 1)
            v.wait_ge(cleared, 1)
            v.wait_ge(blocks_in, 16)
            pack_blocks(v, ch, blocks, packed_f, packed)
            v.tensor_copy(packed_f[:, 0:1], packed_f[:, 0:1]).then_inc(packed_ready, 1)
            turn(-1, SLOTS - 1, True, False, False)
            for s in range(SLOTS):
                turn(0, s, True, True, s > 0)
            with v.Fori(1, ITER - 1) as i:
                for s in range(SLOTS):
                    turn(i, s, True, True, True)
            for s in range(SLOTS):
                turn(ITER - 1, s, s + 1 < SLOTS, True, True)
            turn(ITER, 0, False, False, True)

        @block.scalar
        def _(a):
            def copy(i, s):
                k = i * SLOTS + s
                if not isinstance(k, int) or k:
                    a.wait_ge(sum_added, k * G)
                    a.wait_ge(carry_stored, k * 16)
                for n in range(G):
                    a.wait_ge(sum_made, k * G + n + 1)
                    a.activation(step_sums[:, n, :], bank[4 + n % 2][:, 0:CW], ACT.Copy).then_inc(sum_copied, 1)

            def exponents(i, s):
                wait_after(a, back, i, s)
                a.activation(kv[:, s, :, KC + C_EX:KC + C_V], bank[7][:, 0:G * H].rearrange("p (g h) -> p g h", h=H),
                             ACT.Exp).then_inc(exps[s], 1)

            def store(i, s):
                k = i * SLOTS + s
                a.wait_ge(sum_copied, k * G + G)
                a.dma_start(dram["carry"][bass.ds(k * G, G)].rearrange("g n -> (g n)").unsqueeze(0),
                            step_sums[P - 1:P, :, :].rearrange("p g n -> p (g n)")).then_inc(carry_stored, 16)

            def mark(i, s):
                wait_after(a, scored, i, s)
                wait_after(a, loaded, i, s, per=32)
                a.activation(kv[:, s, :, KC + C_LAST], col[:, s, 2, :], ACT.Copy).then_inc(marked[s], 1)
                a.activation(kv[:, s, :, KC + C_CNT], c["ones"][:, 0:G], ACT.Copy).then_inc(marked[s], 1)

            def places(i, s):
                k = i * SLOTS + s
                wait_after(a, loaded, i, s, per=32)
                wait_count(a, sum_made, k * G)
                for n in range(G):
                    a.activation(ohs[:, n, :], c["iota"][:], ACT.Square, bias=col[:, s, 0, n:n + 1], scale=-1.0
                                 ).then_inc(edge_far[s], 1)
                wait_after(a, edge_far, i, s, per=G)
                a.activation(ohs[:], ohs[:], ACT.Relu, bias=c["ones"][:, 0:1], scale=-1.0).then_inc(edge_hot[s], 1)

            def nodes(i, s):
                wait_after(a, rows_in, i, s, per=16)
                a.activation(oht[:, s, :], oht[:, s, :], ACT.Square, bias=less_p[:]).then_inc(node_hot[s], 1)
                wait_after(a, node_hot, i, s, per=2, less=1)
                a.activation(oht[:, s, :], oht[:, s, :], ACT.Relu, bias=c["ones"][:, 0:1], scale=-1.0
                             ).then_inc(node_hot[s], 1)

            a.wait_ge(place_ready, 1)
            in_turns(a, GROUPS, SLOTS, ((-1, copy), (0, exponents), (-1, store), (0, places), (1, mark), (3, nodes)))
            a.wait_ge(carry_stored, GROUPS * 16)

        @block.tensor
        def _(t):
            at = []

            def look_up(i, s):
                at[:] = [t.snap(x) for x in blocks_of(t, packed, i * SLOTS + s)]

            def expand(i, s):
                wait_after(t, node_hot, i, s, per=2)
                wait_after(t, multiplied, i, s, 1)
                for n in range(G):
                    ins = t.matmul(bank[n // 2][:, (n % 2) * D:(n % 2 + 1) * D], oht[:, s, n * P:(n + 1) * P],
                                   qb[:, bass.ds(at[n], 1), :].rearrange("p b d -> p (b d)"), start=True, stop=True)
                ins.then_inc(expanded[s], 1)

            def turn(i, s):
                wait_after(t, scored, i, s)
                wait_after(t, maxed, i, s, 1)
                wait_after(t, weighted, i, s, 1, per=2, less=1)
                t.transpose(bank[6][0:G * H, 0:P], sc[:, s, :], c["ident"][:]).then_inc(turned[s], 1)

            def turn_back(i, s):
                wait_after(t, maxed, i, s)
                wait_after(t, exps, i, s, 1)
                wait_alone(t, t_gate)
                t.transpose(bank[7][:, 0:G * H], diff[:], c["ident"][0:G * H, 0:G * H])
                t.transpose(bank[6][:, P:P + G * H], mx[:], c["ident"][0:G * H, 0:G * H]).then_inc(back[s], 1)

            def total(i, s):
                k = i * SLOTS + s
                wait_after(t, marked, i, s, per=2)
                wait_after(t, edge_hot, i, s)
                wait_after(t, exps, i, s)
                wait_after(t, weighted, i, s, per=2)
                for n in range(G):
                    if not isinstance(k, int) or k * G + n > 1:
                        t.wait_ge(sum_copied, k * G + n - 1)
                    t.matmul(bank[4 + n % 2][:, 0:CW], ohs[:, n, :], kv[:, s, n, KC:2 * D], start=True, stop=True
                             ).then_inc(sum_made, 1)

            t.wait_ge(q_in, 16 * NB)
            t.wait_ge(packed_ready, 1)
            in_turns(t, GROUPS, SLOTS, ((2, look_up), (0, turn), (-1, total), (0, turn_back), (2, expand)))

BIG = float(1 << 24)
TOP = NB * BW - 1


def merge_carried(nc, sem, psum, bank, c, dram, xt_kept, xt):
    with ExitStack() as ctx:
        def sbt(nm, shape, dt=F32):
            return ctx.enter_context(nc.sbuf_tensor(f"mc_{nm}", shape, dt))

        row = sbt("row", [P, CW])
        keyc, keyr = sbt("keyc", [P, 1]), sbt("keyr", [P, P])
        eq, pen, tri, up = sbt("eq", [P, P]), sbt("pen", [P, P]), sbt("tri", [P, P]), sbt("up", [P, P])
        later, valid, gi_f, si_f = sbt("later", [P, 1]), sbt("valid", [P, 1]), sbt("gi_f", [P, 1]), sbt("si_f", [P, 1])
        gi, si = sbt("gi", [P, 1], I32), sbt("si", [P, 1], I32)
        off, meff, mt, x4 = sbt("off", [P, 1]), sbt("meff", [P, H]), sbt("mt", [H, P]), sbt("x4", [P, H, P])
        ms, dw, w = sbt("ms", [P, H]), sbt("dw", [P, H]), sbt("w", [P, H])
        node, mm, mn = sbt("node", [P, CW]), sbt("mm", [P, H]), sbt("mn", [P, H])
        dab, ab, add = sbt("dab", [P, 2, H]), sbt("ab", [P, 2, H]), sbt("add", [P, CW])
        zrow = sbt("zrow", [NP - NB * BW, CW])
        (rows_in, keys_in, zeroed, zstored, dve, indexed, node_in, merged, scattered, tri_made) = (
            sem(f"mc_{n}") for n in ("rows_in", "keys_in", "zeroed", "zstored", "dve", "indexed", "node_in", "merged",
                                     "scattered", "tri_made"))
        m_ready, m_turned, mt_ready, m_spread, dw_ready, w_ready, scaled, added, dab_ready, ab_ready = (
            sem(f"mc_{n}") for n in ("m_ready", "m_turned", "mt_ready", "m_spread", "dw_ready", "w_ready", "scaled",
                                     "added", "dab_ready", "ab_ready"))
        gate, moved = sem("mc_gate"), sem("mc_moved")
        block = ctx.enter_context(nc.Block())
        assert T - GROUPS * G <= NP - NB * BW

        @block.sync
        def _(sp):
            sp.wait_ge(zeroed, 1)
            sp.dma_start(dram["carry"][GROUPS * G:T, :], zrow[0:T - GROUPS * G]).then_inc(zstored, 16)
            sp.dma_start(dram["sums"][NB * BW:NP, :], zrow[:]).then_inc(zstored, 16)
            sp.wait_ge(zstored, 32)
            for cc in range(2):
                sp.dma_start(xt[:, cc], xt_kept[:, cc]).then_inc(moved, 16)
            with sp.Fori(0, RB) as b:
                sp.wait_ge(merged, b)
                sp.dma_start(row[:], dram["carry"][bass.ds(b * P, P), :]).then_inc(rows_in, 16)
                sp.dma_start(keyc[:], dram["keys"][bass.ds(b * P, P)].unsqueeze(1), allow_slow_non_contiguous=True
                             ).then_inc(keys_in, 16)
                sp.dma_start(keyr[:], dram["keys"][bass.ds(b * P, P)].unsqueeze(0).broadcast_to([P, P])
                             ).then_inc(keys_in, 16)

            sp.wait_ge(moved, 32)

        @block.gpsimd
        def _(g):
            g.memset(pen[:], 1.0).then_inc(tri_made, 1)
            g.wait_ge(tri_made, 1)
            g.affine_select(out=tri[:], in_=pen[:], compare_op=ALU.is_gt, fill=0.0, base=0, pattern=[[1, P]],
                            channel_multiplier=-1).then_inc(tri_made, 1)
            g.memset(zrow[:], 0.0).then_inc(zeroed, 1)
            with g.Fori(0, RB) as b:
                g.wait_ge(indexed, b + 1)
                g.wait_ge(scattered, b * 16)
                wait_alone(g, gate)
                g.indirect_dma_start(out=node[:], out_offset=None, in_=dram["sums"],
                                     in_offset=bass.IndirectOffsetOnAxis(ap=gi[:].bitcast(U32), axis=0)).then_inc(node_in, 16)
                g.wait_ge(merged, b + 1)
                wait_alone(g, gate)
                g.indirect_dma_start(out=dram["sums"], in_=add[:], in_offset=None,
                                     out_offset=bass.IndirectOffsetOnAxis(ap=si[:].bitcast(U32), axis=0),
                                     bounds_check=TOP, oob_is_err=False).then_inc(scattered, 16)
            g.wait_ge(scattered, RB * 16)

        @block.vector
        def _(v):
            ch = Chain(v, dve)
            v.wait_ge(tri_made, 2)
            with v.Fori(0, RB) as b:
                ch.enter(b, 23)
                v.wait_ge(keys_in, b * 32 + 32)
                v.wait_ge(scattered, b * 16)
                ch.done(v.tensor_scalar(eq[:], keyr[:], keyc[:], None, ALU.is_equal))
                ch.link(v.tensor_scalar(valid[:], keyc[:], 0.0, None, ALU.is_ge))
                ch.done(v.tensor_scalar(pen[:], eq[:], -1.0, -NEG, ALU.add, ALU.mult))
                ch.done(v.tensor_tensor(up[:], eq[:], tri[:], ALU.mult))
                ch.done(v.scalar_tensor_tensor(gi_f[:], keyc[:], float(-TOP), valid[:], ALU.add, ALU.mult))
                ch.link(v.tensor_scalar(si_f[:], valid[:], -BIG, BIG, ALU.mult, ALU.add))
                ch.done(v.tensor_scalar(gi[:], gi_f[:], float(TOP), None, ALU.add))
                ch.link(v.tensor_reduce(later[:], up[:], AX.X, ALU.max))
                ch.link(v.scalar_tensor_tensor(si_f[:], later[:], BIG, si_f[:], ALU.mult, ALU.max))
                v.tensor_scalar(si[:], si_f[:], keyc[:], 0.0, ALU.add, ALU.max).then_inc(indexed, 1)
                v.wait_ge(rows_in, b * 16 + 16)
                ch.link(v.tensor_scalar(off[:], row[:, C_LAST:C_LAST + 1], -1.0, -NEG, ALU.add, ALU.mult))
                v.tensor_scalar(meff[:], row[:, C_M:C_EX], off[:], None, ALU.add).then_inc(m_ready, 1)
                v.wait_ge(m_turned, b + 1)
                v.tensor_copy(mt[:], bank[0][0:H, 0:P]).then_inc(mt_ready, 1)
                v.wait_ge(m_spread, b + 1)
                ch.link(v.tensor_tensor(x4[:], bank[1].rearrange("p (h n) -> p h n", h=H),
                                        pen[:].unsqueeze(1).broadcast_to([P, H, P]), ALU.add))
                ch.link(v.tensor_reduce(ms[:], x4[:], AX.X, ALU.max))
                v.wait_ge(m_ready, b + 1)
                v.tensor_tensor(dw[:], meff[:], ms[:], ALU.subtract).then_inc(dw_ready, 1)
                v.wait_ge(w_ready, b + 1)
                v.tensor_tensor(row[:, C_EX:C_V], row[:, C_EX:C_V], w[:], ALU.mult).then_inc(scaled, 1)
                rv = row[:, C_V:CW].rearrange("p (h d) -> p h d", h=H)
                v.tensor_tensor(rv, rv, w[:].unsqueeze(2).broadcast_to([P, H, DK]), ALU.mult).then_inc(scaled, 1)
                v.wait_ge(node_in, b * 16 + 16)
                ch.link(v.tensor_scalar(off[:], node[:, C_LAST:C_LAST + 1], -1.0, -NEG, ALU.add, ALU.mult))
                ch.link(v.tensor_scalar(mm[:], node[:, C_M:C_EX], off[:], None, ALU.add))
                ch.link(v.tensor_tensor(mn[:], mm[:], ms[:], ALU.max))
                ch.done(v.tensor_copy(node[:, C_M:C_EX], mn[:]))
                v.tensor_tensor(dab[:, 0, :], mm[:], mn[:], ALU.subtract).then_inc(dab_ready, 1)
                v.tensor_tensor(dab[:, 1, :], ms[:], mn[:], ALU.subtract).then_inc(dab_ready, 1)
                v.wait_ge(ab_ready, b + 1)
                v.wait_ge(added, b + 1)
                nv, av = (x[:, C_V:CW].rearrange("p (h d) -> p h d", h=H) for x in (node, add))
                sv = bank[2][:, C_V:CW].rearrange("p (h d) -> p h d", h=H)
                ch.done(v.tensor_tensor(node[:, C_EX:C_V], node[:, C_EX:C_V], ab[:, 0, :], ALU.mult))
                ch.done(v.tensor_tensor(nv, nv, ab[:, 0, :].unsqueeze(2).broadcast_to([P, H, DK]), ALU.mult))
                ch.done(v.tensor_tensor(add[:, C_EX:C_V], bank[2][:, C_EX:C_V], ab[:, 1, :], ALU.mult))
                ch.done(v.tensor_tensor(av, sv, ab[:, 1, :].unsqueeze(2).broadcast_to([P, H, DK]), ALU.mult))
                ch.done(v.tensor_copy(add[:, C_CNT:C_CNT + 1], bank[2][:, C_CNT:C_CNT + 1]))
                ch.link(v.memset(add[:, C_LAST:C_EX], 0.0))
                ch.link(v.tensor_tensor(add[:], add[:], node[:], ALU.add))
                v.tensor_scalar(add[:, C_LAST:C_LAST + 1], add[:, C_LAST:C_LAST + 1], 1.0, None, ALU.min).then_inc(merged, 1)
                ch.leave(RB)

        @block.scalar
        def _(a):
            with a.Fori(0, RB) as b:
                a.wait_ge(dw_ready, b + 1)
                a.activation(w[:], dw[:], ACT.Exp).then_inc(w_ready, 1)
                a.wait_ge(dab_ready, b * 2 + 2)
                a.activation(ab[:], dab[:], ACT.Exp).then_inc(ab_ready, 1)

        @block.tensor
        def _(t):
            with t.Fori(0, RB) as b:
                t.wait_ge(m_ready, b + 1)
                t.transpose(bank[0][0:H, 0:P], meff[:], c["ident"][:]).then_inc(m_turned, 1)
                t.wait_ge(mt_ready, b + 1)
                for h in range(H):
                    ins = t.matmul(bank[1][:, h * P:(h + 1) * P], c["ident"][0:H, h:h + 1].broadcast_to([H, P]), mt[:],
                                   start=True, stop=True)
                ins.then_inc(m_spread, 1)
                t.wait_ge(scaled, b * 2 + 2)
                t.matmul(bank[2][:, 0:CW], eq[:], row[:], start=True, stop=True).then_inc(added, 1)

EPS_IN = 1e-5
MH = 8
NI = NT // 2


def mix0_matrix(nc, sem, psum, bank, c, xt, wqkv, wout, wmix, xt_kept):
    INNER = MH * DK
    with ExitStack() as ctx:
        def sbt(nm, shape, dt=F32):
            return ctx.enter_context(nc.sbuf_tensor(f"m0_{nm}", shape, dt))

        def sems(*names):
            return (sem(f"m0_{n}") for n in names)

        w = sbt("w", [P, 12, D])
        wt = sbt("wt", [P, 2, 2 * INNER])
        wo = sbt("wo", [P, 2, INNER])
        wot = sbt("wot", [P, 4, D])
        xs = sbt("xs", [P, 2, 2, P])
        mean = sbt("mean", [P, 2, 16])
        cen = sbt("cen", [P, 2, 16, DK])
        sq = sbt("sq", [P, 2, 16, DK])
        ss = sbt("ss", [P, 2, 16])
        sd = sbt("sd", [P, 2, 16])
        rs = sbt("rs", [P, 2, 16])
        eps = sbt("eps", [P, 1])
        dots = sbt("dots", [P, 4, P])
        m2 = sbt("m2", [P, 4, D])
        w_in, turned, taken, eps_ready, dve, xs_ready, projected, centred, squared, var_ready, sd_ready = sems(
            "w_in", "turned", "taken", "eps_ready", "dve", "xs_ready", "projected", "centred", "squared", "var_ready", "sd_ready")
        means, inverted, moved = sems("means", "inverted", "moved")
        normed, summed, dots_ready, m2_made, m2_ready, mix_made, mix_ready = sems(
            "normed", "summed", "dots_ready", "m2_made", "m2_ready", "mix_made", "mix_ready")
        block = ctx.enter_context(nc.Block())

        @block.sync
        def _(sp):
            sp.dma_start(w[:], wqkv.rearrange("(f p) c -> p f c", p=P)).then_inc(w_in, 16)
            sp.dma_start(wo[:], wout.rearrange("(g p) e -> p g e", p=P)).then_inc(w_in, 16)
            for cc in range(2):
                sp.dma_start(xt_kept[:, cc], xt[:, cc]).then_inc(moved, 16)
            sp.wait_ge(moved, 32)

        @block.tensor
        def _(t):
            t.wait_ge(w_in, 32)
            for n in range(4):
                for j in range(4):
                    ins = t.transpose(bank[n][:, j * P:(j + 1) * P], w[:, 4 + 2 * n + j // 2, (j % 2) * P:(j % 2 + 1) * P],
                                      c["ident"][:])
                ins.then_inc(turned, 1)
            for n in range(2):
                for j in range(4):
                    ins = t.transpose(bank[4 + n][:, j * P:(j + 1) * P],
                                      wo[:, j % 2, (2 * n + j // 2) * P:(2 * n + j // 2 + 1) * P], c["ident"][:])
                ins.then_inc(turned, 1)
            t.wait_ge(taken, 6)
            t.matmul(bank[6], c["zero"][:, 0:P], c["zero"][:], start=True, stop=False, skip_group_check=True)

            def project(i, s):
                k = i * 2 + s
                wait_count(t, xs_ready, k + 1)
                wait_count(t, centred, k - 1)
                for half in range(2):
                    for cc in range(2):
                        ins = t.matmul(bank[2 * s + half], xs[:, s, cc, :], wt[:, cc, half * INNER:(half + 1) * INNER],
                                       start=cc == 0, stop=cc == 1)
                ins.then_inc(projected, 1)

            def add(i, s):
                wait_count(t, normed, i * 2 + s + 1)
                for j in range(4):
                    k_, v_ = (cen[:, s, x + 2 * j:x + 2 * j + 2, :].rearrange("p h d -> p (h d)") for x in (0, MH))
                    ins = t.matmul(bank[6][:, j * P:(j + 1) * P], v_, k_, start=False, stop=False, skip_group_check=True)
                ins.then_inc(summed, 1)

            in_turns(t, NT, 2, ((2, project), (0, add)))
            t.wait_ge(dots_ready, 1)
            for j in range(4):
                ins = t.matmul(bank[j][:, 0:D], dots[:, j, :], wot[:, j, :], start=True, stop=True)
            ins.then_inc(m2_made, 1)
            t.wait_ge(m2_ready, 1)
            for cc in range(2):
                for j in range(4):
                    ins = t.matmul(bank[4][:, cc * D:(cc + 1) * D], w[:, j, cc * P:(cc + 1) * P], m2[:, j, :],
                                   start=j == 0, stop=j == 3)
            ins.then_inc(mix_made, 1)

        @block.scalar
        def _(a):
            a.wait_ge(eps_ready, 1)
            with a.Fori(0, NI) as i:
                for s in range(2):
                    k = i * 2 + s
                    a.wait_ge(var_ready, k + 1)
                    a.activation(sd[:, s, :], ss[:, s, :], ACT.Sqrt, bias=eps[:], scale=1.0 / DK).then_inc(sd_ready, 1)

        @block.gpsimd
        def _(g):
            def copy(i, s):
                k = i * 2 + s
                wait_count(g, projected, k - 1)
                g.tensor_copy(xs[:, s], xt[:, :, bass.ds(k * P, P)]).then_inc(xs_ready, 1)

            def square(i, s):
                k = i * 2 + s
                wait_count(g, centred, k + 1)
                wait_count(g, var_ready, k - 1)
                g.tensor_tensor(sq[:, s], cen[:, s], cen[:, s], ALU.mult).then_inc(squared, 1)

            in_turns(g, NT, 2, ((2, copy), (1, square)))

        @block.vector
        def _(v):
            ch = Chain(v, dve)
            v.memset(eps[:], EPS_IN).then_inc(eps_ready, 1)
            for n in range(4):
                v.wait_ge(turned, n + 1)
                v.tensor_copy(wt[:, :, n * 2 * P:(n + 1) * 2 * P].rearrange("p c (f n) -> p f c n", f=2),
                              bank[n].rearrange("p (f c n) -> p f c n", f=2, c=2)).then_inc(taken, 1)
            for n in range(2):
                v.wait_ge(turned, 5 + n)
                v.tensor_copy(wot[:, 2 * n:2 * n + 2, :].rearrange("p e n -> p (e n)"), bank[4 + n]).then_inc(taken, 1)

            def centre(i, s):
                k = i * 2 + s
                wait_count(v, projected, k + 1)
                y = psum[:, 2 * s:2 * s + 2, :].rearrange("p b (h d) -> p (b h) d", d=DK)
                v.tensor_reduce(mean[:, s, :], y, AX.X, ALU.add).then_inc(means, 1)
                wait_count(v, means, 2 * k + 1)
                v.tensor_scalar(mean[:, s, :], mean[:, s, :], 1.0 / DK, None, ALU.mult).then_inc(means, 1)
                wait_count(v, means, 2 * k + 2)
                wait_count(v, summed, k - 1)
                v.tensor_tensor(cen[:, s], y, mean[:, s, :].unsqueeze(2).broadcast_to([P, 16, DK]), ALU.subtract
                                ).then_inc(centred, 1)

            def norm(i, s):
                k = i * 2 + s
                wait_count(v, inverted, k)
                wait_count(v, sd_ready, k + 1)
                v.reciprocal(rs[:, s, :], sd[:, s, :]).then_inc(inverted, 1)
                wait_count(v, inverted, k + 1)
                v.tensor_tensor(cen[:, s], cen[:, s], rs[:, s, :].unsqueeze(2).broadcast_to([P, 16, DK]), ALU.mult
                                ).then_inc(normed, 1)

            def variance(i, s):
                k = i * 2 + s
                wait_count(v, squared, k + 1)
                v.tensor_reduce(ss[:, s, :], sq[:, s], AX.X, ALU.add).then_inc(var_ready, 1)

            in_turns(v, NT, 2, ((0, variance), (1, centre), (0, norm)))
            ch.link(v.memset(dots[:], 0.0))
            v.wait_ge(summed, NT)
            for hh in range(2):
                a, b = hh * DK, (hh + 1) * DK
                ch.done(v.tensor_scalar(dots[a:b, :, a:b], bank[6].rearrange("p (j n) -> p j n", j=4)[a:b, :, a:b],
                                        1.0 / N, None, ALU.mult))
            ch.settle()
            v.tensor_copy(eps[:], c["ones"][:, 0:1]).then_inc(dots_ready, 1)
            v.wait_ge(m2_made, 1)
            ch.link(v.tensor_copy(m2[:], psum[:, 0:4, 0:D]))
            v.tensor_copy(eps[:], c["ones"][:, 0:1]).then_inc(m2_ready, 1)
            v.wait_ge(mix_made, 1)
            v.tensor_copy(wmix[:].rearrange("p c n -> p (c n)"), bank[4]).then_inc(mix_ready, 1)


def after_attention(nc, sem, psum, bank, c, xt, wmix, w, dram, x_in, x_out, dinv):
    with ExitStack() as ctx:
        def sbt(nm, shape, dt=F32):
            return ctx.enter_context(nc.sbuf_tensor(f"aa_{nm}", shape, dt))

        def sems(*names):
            return (sem(f"aa_{n}") for n in names)

        S = 5
        wa = sbt("wa", [P, 2, 4, D])
        skip = sbt("skip", [P, 4])
        sg = sbt("sg", [P, 4])
        bout = sbt("bout", [P, D])
        types = sbt("types", [P, S, P], I32)
        mask = sbt("mask", [P, S, 4, P])
        rows = sbt("rows", [P, S, CW])
        xr = sbt("xr", [P, S, D])
        den = sbt("den", [P, S, H])
        agg = sbt("agg", [P, S, D])
        aggt = sbt("aggt", [P, S, D])
        am = sbt("am", [P, S, 2, 4, P])
        xs = sbt("xs", [P, S, 2, P])
        y = sbt("y", [P, S, D])
        cnt = sbt("cnt", [P, NT])
        w_in, sg_ready, wa_ready, loaded, agg_ready, turned, aggt_ready, am_ready, xs_ready, made, out_ready, stored = sems(
            "w_in", "sg_ready", "wa_ready", "loaded", "agg_ready", "turned", "aggt_ready", "am_ready", "xs_ready",
            "made", "out_ready", "stored")
        dve, cnt_ready, sd_ready, biased = sems("dve", "cnt_ready", "sd_ready", "biased")
        slot_in = [sem(f"aa_slot_in{s}") for s in range(S)]
        slot_out = [sem(f"aa_slot_out{s}") for s in range(S)]
        block = ctx.enter_context(nc.Block())

        @block.sync
        def _(sp):
            for cc in range(2):
                sp.dma_start(wa[:, cc], w["a"][:, cc * P:(cc + 1) * P, :].rearrange("t p o -> p t o")).then_inc(w_in, 16)
            sp.dma_start(skip[:], w["skip"].unsqueeze(0).broadcast_to([P, 4])).then_inc(w_in, 16)
            sp.dma_start(bout[:], w["bout"].unsqueeze(0).broadcast_to([P, D])).then_inc(w_in, 16)

            def load(i, s):
                k = i * S + s
                wait_count(sp, out_ready, k - S + 1)
                sp.dma_start(rows[:, s, :], dram["sums"][bass.ds(k * P, P), :]).then_inc(slot_in[s], 16)
                sp.dma_start(xr[:, s, :], x_in[bass.ds(k * P, P), :]).then_inc(slot_in[s], 16)
                sp.dma_start(types[:, s, :], dram["types"][bass.ds(k * P, P)].unsqueeze(0).broadcast_to([P, P])
                             ).then_inc(slot_in[s], 16)

            in_turns(sp, NT, S, ((0, load),))

        @block.gpsimd
        def _(g):
            def copy(i, s):
                k = i * S + s
                wait_count(g, made, k - S + 1)
                g.tensor_copy(xs[:, s], xt[:, :, bass.ds(k * P, P)]).then_inc(xs_ready, 1)

            def store(i, s):
                k = i * S + s
                wait_count(g, out_ready, k + 1)
                g.dma_start(x_out[bass.ds(k * P, P), :], y[:, s, :]).then_inc(slot_out[s], 16)

            in_turns(g, NT, S, ((2, copy), (0, store)))
            for s in range(S):
                g.wait_ge(slot_out[s], NT // S * 16)

        @block.scalar
        def _(a):
            a.wait_ge(w_in, 64)
            a.activation(sg[:], skip[:], ACT.Sigmoid).then_inc(sg_ready, 1)

            def take(i, s):
                k = i * S + s
                wait_count(a, turned, k + 1)
                wait_count(a, am_ready, k - S + 1)
                a.activation(aggt[:, s, :], bank[s][:, 0:D], ACT.Copy).then_inc(aggt_ready, 1)

            in_turns(a, NT, S, ((0, take),))
            a.wait_ge(cnt_ready, 1)
            a.activation(dinv[:], cnt[:], ACT.Sqrt, bias=c["ones"][:, 0:1]).then_inc(sd_ready, 1)

        @block.vector
        def _(v):
            ch = Chain(v, dve)
            v.wait_ge(sg_ready, 1)
            v.tensor_tensor(wa[:], wa[:], sg[:].unsqueeze(1).unsqueeze(3).broadcast_to([P, 2, 4, D]), ALU.mult
                            ).then_inc(wa_ready, 1)
            v.wait_ge(w_in, 64)

            def divide(i, s):
                k = i * S + s
                wait_after(v, slot_in, i, s, per=48)
                wait_count(v, am_ready, k - S + 1)
                wait_count(v, turned, k - S + 1)
                v.tensor_scalar(den[:, s, :], rows[:, s, C_EX:C_V], 1e-30, None, ALU.max).then_inc(dve, 1)
                v.tensor_tensor(mask[:, s], types[:, s, :].unsqueeze(1).broadcast_to([P, 4, P]),
                                c["iota"][:, 0:4].unsqueeze(2).broadcast_to([P, 4, P]), ALU.is_equal).then_inc(dve, 1)
                wait_count(v, dve, 4 * k + 2)
                v.reciprocal(den[:, s, :], den[:, s, :]).then_inc(dve, 1)
                v.tensor_copy(cnt[:, bass.ds(k, 1)], rows[:, s, 0:1]).then_inc(dve, 1)
                wait_count(v, dve, 4 * k + 4)
                v.tensor_tensor(agg[:, s].rearrange("p (h d) -> p h d", h=H),
                                rows[:, s, C_V:CW].rearrange("p (h d) -> p h d", h=H),
                                den[:, s, :].unsqueeze(2).broadcast_to([P, H, DK]), ALU.mult).then_inc(agg_ready, 1)

            def by_type(i, s):
                k = i * S + s
                wait_count(v, aggt_ready, k + 1)
                wait_count(v, made, k - S + 1)
                v.tensor_tensor(am[:, s], aggt[:, s].rearrange("p (c n) -> p c n", c=2).unsqueeze(2)
                                .broadcast_to([P, 2, 4, P]), mask[:, s].unsqueeze(1).broadcast_to([P, 2, 4, P]),
                                ALU.mult).then_inc(am_ready, 1)

            def residual(i, s):
                k = i * S + s
                wait_after(v, slot_out, i, s, S, per=16)
                v.tensor_tensor(xr[:, s], xr[:, s], bout[:], ALU.add).then_inc(biased, 1)

            def finish(i, s):
                k = i * S + s
                wait_count(v, made, k + 1)
                wait_count(v, biased, k + 1)
                v.tensor_tensor(y[:, s], bank[s][:, D:2 * D], xr[:, s], ALU.add).then_inc(out_ready, 1)

            in_turns(v, NT, S, ((2, divide), (1, by_type), (1, residual), (0, finish)))
            v.wait_ge(dve, 4 * NT)
            ch.base = 4 * NT
            ch.link(v.tensor_copy(cnt[:, 0:1], cnt[:, 0:1]))
            v.tensor_copy(cnt[:, 1:2], cnt[:, 1:2]).then_inc(cnt_ready, 1)
            v.wait_ge(sd_ready, 1)
            ch.link(v.reciprocal(dinv[:], dinv[:]))

        @block.tensor
        def _(t):
            t.wait_ge(wa_ready, 1)

            def turn(i, s):
                k = i * S + s
                wait_count(t, agg_ready, k + 1)
                wait_count(t, out_ready, k - S + 1)
                t.transpose(bank[s][:, 0:P], agg[:, s, 0:P], c["ident"][:])
                t.transpose(bank[s][:, P:D], agg[:, s, P:D], c["ident"][:]).then_inc(turned, 1)

            def product(i, s):
                k = i * S + s
                wait_count(t, xs_ready, k + 1)
                wait_count(t, am_ready, k + 1)
                for cc in range(2):
                    t.matmul(bank[s][:, D:2 * D], xs[:, s, cc, :], wmix[:, cc, :], start=cc == 0, stop=False)
                for n in range(8):
                    ins = t.matmul(bank[s][:, D:2 * D], am[:, s, n // 4, n % 4, :], wa[:, n // 4, n % 4, :],
                                   start=False, stop=n == 7)
                ins.then_inc(made, 1)

            in_turns(t, NT, S, ((2, turn), (1, product)))

FH = 1024
FC = FH // P
CAP = max(1, int(0.5 * N)) - 1
LOW = -3.0e38


def routed_ffn(nc, sem, psum, bank, c, xt, w, dram, x_in, xn_in, x_out):
    with ExitStack() as ctx:
        def sbt(nm, shape, dt=F32):
            return ctx.enter_context(nc.sbuf_tensor(f"rf_{nm}", shape, dt))

        def sems(*names):
            return (sem(f"rf_{n}") for n in names)

        w1, w2 = sbt("w1", [P, 2, FH]), sbt("w2", [P, FC, D])
        b1, b2 = sbt("b1", [P, FC]), sbt("b2", [P, D])
        wr, br = sbt("wr", [P, 2]), sbt("br", [1, 1])
        wrow = sbt("wrow", [1, NP])
        wbc = sbt("wbc", [P, NP])
        junk = sbt("junk", [P, NP], mybir.dt.bfloat16)
        wcol, gt, sel, eq = sbt("wcol", [P, NT]), sbt("gt", [P, NT]), sbt("sel", [P, NT]), sbt("eq", [P, NT])
        node = sbt("node", [P, NT])
        tile_i = sbt("node_i", [P, NT], I32)
        tri = sbt("tri", [P, P])
        gm = sbt("gm", [P, 1])
        g1 = sbt("g1", [1, 1])
        gbc = sbt("gbc", [P, 1])
        before, tot, coef = sbt("before", [P, NT]), sbt("tot", [P, NT]), sbt("coef", [P, NT])
        ht = sbt("ht", [P, FC, 2 * P])
        y = sbt("y", [P, NT, D])
        S = 5
        xr, xn, o = (wbc[:, n * S * D:(n + 1) * S * D].rearrange("p (s d) -> p s d", d=D) for n in range(3))
        w_in, row_made, row_taken, row_stored, row_in, masked, counted, dve = sems(
            "w_in", "row_made", "row_taken", "row_stored", "row_in", "masked", "counted", "dve")
        h_made, h_ready, h_used, y_made, y_taken, iota_made, tri_made = sems(
            "h_made", "h_ready", "h_used", "y_made", "y_taken", "iota_made", "tri_made")
        gm_ready, gm_turned, g1_ready, g_spread, eq_ready, ranked, out_ready, joined = sems(
            "gm_ready", "gm_turned", "g1_ready", "g_spread", "eq_ready", "ranked", "out_ready", "joined")
        slot_in = [sem(f"rf_slot_in{s}") for s in range(S)]
        slot_out = [sem(f"rf_slot_out{s}") for s in range(S)]
        LOADS = 6
        block = ctx.enter_context(nc.Block())

        @block.sync
        def _(sp):
            sp.dma_start(wr[:], w["wr"].rearrange("(c p) o -> p (c o)", p=P), allow_slow_non_contiguous=True
                         ).then_inc(w_in, 16)
            sp.dma_start(br[:], w["br"].unsqueeze(0)).then_inc(w_in, 16)
            sp.dma_start(w1[:], w["w1"].rearrange("(c p) n -> p c n", p=P)).then_inc(w_in, 16)
            sp.dma_start(w2[:], w["w2"].rearrange("(c p) n -> p c n", p=P)).then_inc(w_in, 16)
            sp.dma_start(b1[:], w["b1"].rearrange("(c p) -> p c", p=P), allow_slow_non_contiguous=True).then_inc(w_in, 16)
            sp.dma_start(b2[:], w["b2"].unsqueeze(0).broadcast_to([P, D])).then_inc(w_in, 16)
            sp.wait_ge(row_taken, NI)
            sp.dma_start(dram["router"].unsqueeze(0), wrow[:]).then_inc(row_stored, 16)
            sp.wait_ge(row_stored, 16)
            sp.dma_start(wcol[:], dram["router"].rearrange("(t p) -> p t", p=P), allow_slow_non_contiguous=True
                         ).then_inc(row_in, 16)
            sp.dma_start(wbc[:], dram["router"].unsqueeze(0).broadcast_to([P, NP])).then_inc(row_in, 16)

            def load(i, s):
                k = i * S + s
                wait_count(sp, out_ready, k - S + 1)
                sp.dma_start(xr[:, s, :], x_in[bass.ds(k * P, P), :]).then_inc(slot_in[s], 16)
                sp.dma_start(xn[:, s, :], xn_in[bass.ds(k * P, P), :]).then_inc(slot_in[s], 16)

            sp.wait_ge(eq_ready, 1)
            in_turns(sp, NT, S, ((0, load),))

        @block.gpsimd
        def _(g):
            g.iota(tile_i[:], pattern=[[P, NT]], base=0, channel_multiplier=1).then_inc(iota_made, 1)
            g.affine_select(out=tri[:], in_=c["ones"][:], compare_op=ALU.is_gt, fill=0.0, base=0, pattern=[[1, P]],
                            channel_multiplier=-1).then_inc(tri_made, 1)

            def store(i, s):
                k = i * S + s
                wait_count(g, out_ready, k + 1)
                g.dma_start(x_out[bass.ds(k * P, P), :], o[:, s, :]).then_inc(slot_out[s], 16)

            in_turns(g, NT, S, ((0, store),))
            for s in range(S):
                g.wait_ge(slot_out[s], NT // S * 16)

        @block.tensor
        def _(t):
            t.wait_ge(w_in, 16 * LOADS)
            with t.Fori(0, NI) as i:
                t.wait_ge(row_taken, i)
                for cc in range(2):
                    ins = t.matmul(bank[6][0:1, 0:2 * P], wr[:, cc:cc + 1], xt[:, cc, bass.ds(i * 2 * P, 2 * P)],
                                   start=cc == 0, stop=cc == 1)
                ins.then_inc(row_made, 1)
            with t.Fori(0, NI) as i:
                for b in range(4):
                    t.wait_ge(h_ready, i * 4)
                    for j in range(2):
                        f = 2 * b + j
                        for cc in range(2):
                            ins = t.matmul(bank[b][:, j * 2 * P:(j + 1) * 2 * P], w1[:, cc, f * P:(f + 1) * P],
                                           xt[:, cc, bass.ds(i * 2 * P, 2 * P)], start=cc == 0, stop=cc == 1)
                    ins.then_inc(h_made, 1)
                t.wait_ge(h_ready, i * 4 + 4)
                for s in range(2):
                    t.wait_ge(y_taken, i * 2)
                    for f in range(FC):
                        ins = t.matmul(bank[4 + s][:, 0:D], ht[:, f, s * P:(s + 1) * P], w2[:, f, :],
                                       start=f == 0, stop=f == FC - 1)
                    ins.then_inc(y_made, 1)
            t.wait_ge(gm_ready, 1)
            t.transpose(bank[6][0:1, 0:P], gm[:], c["ident"][:]).then_inc(gm_turned, 1)
            t.wait_ge(g1_ready, 1)
            t.matmul(bank[7][:, 0:1], c["ones"][0:1, :], g1[:], start=True, stop=True).then_inc(g_spread, 1)
            t.wait_ge(eq_ready, 1)
            t.wait_ge(tri_made, 1)
            t.matmul(bank[6][:, 0:NT], tri[:], eq[:], start=True, stop=True)
            t.matmul(bank[6][:, NT:2 * NT], c["ones"][:], eq[:], start=True, stop=True).then_inc(ranked, 1)

        @block.scalar
        def _(a):
            a.wait_ge(w_in, 16 * LOADS)
            with a.Fori(0, NI) as i:
                a.wait_ge(row_made, i + 1)
                a.activation(wrow[:, bass.ds(i * 2 * P, 2 * P)], bank[6][0:1, 0:2 * P], ACT.Identity, bias=br[:]
                             ).then_inc(row_taken, 1)
            with a.Fori(0, NI) as i:
                for b in range(4):
                    a.wait_ge(h_made, i * 4 + b + 1)
                    a.wait_ge(y_made, i * 2)
                    for j in range(2):
                        f = 2 * b + j
                        ins = a.activation(ht[:, f, :], bank[b][:, j * 2 * P:(j + 1) * 2 * P], ACT.Gelu_apprx_tanh,
                                           bias=b1[:, f:f + 1])
                        if j:
                            ins.then_inc(h_ready, 1)

        @block.vector
        def _(v):
            ch = Chain(v, dve)
            v.wait_ge(iota_made, 1)
            ch.link(v.tensor_copy(node[:], tile_i[:]))
            v.wait_ge(row_in, 32)
            ch.link(v.tensor_scalar(node[:], node[:], float(N), LOW, ALU.is_ge, ALU.mult))
            ch.done(v.tensor_tensor(wcol[:], wcol[:], node[:], ALU.add))
            ch.done(v.memset(wbc[:, N:NP], LOW))
            ch.settle()
            with v.Fori(0, NI) as i:
                ch.enter(i, 2)
                for s in range(2):
                    k = i * 2 + s
                    ch.settle()
                    ch.done(v.tensor_scalar(junk[:], wbc[:], wcol[:, bass.ds(k, 1)], 0.0, ALU.is_gt, ALU.add,
                                            accum_out=gt[:, bass.ds(k, 1)]))
                    v.wait_ge(y_made, k + 1)
                    v.tensor_tensor(y[:, bass.ds(k, 1), :].rearrange("p t d -> p (t d)"), bank[4 + s][:, 0:D], b2[:],
                                    ALU.add).then_inc(y_taken, 1)
                ch.leave(NI)
            ch.settle()
            ch.link(v.tensor_scalar(sel[:], gt[:], float(CAP), None, ALU.is_lt))
            ch.link(v.tensor_tensor(eq[:], gt[:], sel[:], ALU.mult))
            v.tensor_reduce(gm[:], eq[:], AX.X, ALU.max).then_inc(gm_ready, 1)
            v.wait_ge(gm_turned, 1)
            v.tensor_reduce(g1[:], bank[6][0:1, 0:P], AX.X, ALU.max).then_inc(g1_ready, 1)
            v.wait_ge(g_spread, 1)
            ch.link(v.tensor_copy(gbc[:], bank[7][:, 0:1]))
            ch.done(v.tensor_scalar(sel[:], gt[:], gbc[:], None, ALU.is_lt))
            v.tensor_scalar(eq[:], gt[:], gbc[:], None, ALU.is_equal).then_inc(eq_ready, 1)
            v.wait_ge(ranked, 1)
            ch.done(v.tensor_copy(tot[:], bank[6][:, NT:2 * NT]))
            ch.link(v.tensor_scalar(before[:], bank[6][:, 0:NT], gbc[:], None, ALU.add))
            ch.link(v.tensor_tensor_scan(coef[:], tot[:], c["zero"][:, 0:NT], 0.0, ALU.add, ALU.add))
            ch.link(v.tensor_tensor(coef[:], coef[:], tot[:], ALU.subtract))
            ch.link(v.tensor_tensor(before[:], before[:], coef[:], ALU.add))
            ch.link(v.scalar_tensor_tensor(before[:], before[:], float(CAP), eq[:], ALU.is_lt, ALU.mult))
            ch.link(v.tensor_tensor(sel[:], sel[:], before[:], ALU.add))
            ch.link(v.tensor_tensor(coef[:], sel[:], wcol[:], ALU.mult))

            def join(i, s):
                k = i * S + s
                wait_after(v, slot_in, i, s, per=32)
                wait_after(v, slot_out, i, s, S, per=16)
                v.tensor_tensor(o[:, s], xr[:, s], xn[:, s], ALU.add).then_inc(joined, 1)

            def finish(i, s):
                k = i * S + s
                wait_count(v, joined, k + 1)
                v.scalar_tensor_tensor(o[:, s], y[:, bass.ds(k, 1), :].rearrange("p t d -> p (t d)"),
                                       coef[:, bass.ds(k, 1)], o[:, s], ALU.mult, ALU.add).then_inc(out_ready, 1)

            in_turns(v, NT, S, ((1, join), (0, finish)))



EPS_RMS = 1e-6
EPS_BN = 1e-5
HID = 64
HD1 = D // MH
QKV = 3 * D


def project_layer1(nc, sem, psum, bank, c, xt, w, xn_in, q_out, y_out, dinv, ksum, kvm):
    with ExitStack() as ctx:
        def sbt(nm, shape, dt=F32):
            return ctx.enter_context(nc.sbuf_tensor(f"p1_{nm}", shape, dt))

        def sems(*names):
            return (sem(f"p1_{n}") for n in names)

        W = QKV + HID
        wa = sbt("wa", [P, 2, W])
        wn = sbt("wn", [P, 2])
        wo = sbt("wo", [P, 2, D])
        SQ = 5
        xn = sbt("xn", [P, SQ, D])
        junk = sbt("junk", [P, SQ, D])
        ss, rs = sbt("ss", [P, NT]), sbt("rs", [P, NT])
        eps = sbt("eps", [P, 1])
        node, valid = sbt("node_i", [P, NT], I32), sbt("valid", [P, NT])
        xs = sbt("xs", [P, 2, 2, P])
        z = sbt("z", [P, 2, 2 * D])
        ez = sbt("ez", [P, 2, 2 * D])
        qk = sbt("qk", [P, 2, 2 * D])
        vv = sbt("vv", [P, 2, D])
        yy = sbt("yy", [P, 2, HID])
        kvd = sbt("kvd", [P, 2, P])
        w_in, dve, ready, ss_ready, sd_ready, xs_ready, made, z_ready, exped, k_ready, summed = sems(
            "w_in", "dve", "ready", "ss_ready", "sd_ready", "xs_ready", "made", "z_ready", "exped", "k_ready", "summed")
        v_ready, both = sems("v_ready", "both")
        kvd_ready, joined, iota_made, y_ready, sq_done, pos = sems(
            "kvd_ready", "joined", "iota_made", "y_ready", "sq_done", "pos")
        row_in = [sem(f"p1_row_in{s}") for s in range(SQ)]
        slot_out = [sem(f"p1_slot_out{s}") for s in range(2)]
        y_stored = [sem(f"p1_y_stored{s}") for s in range(2)]
        block = ctx.enter_context(nc.Block())

        @block.sync
        def _(sp):
            sp.dma_start(wa[:, :, 0:QKV], w["w_qkv"].rearrange("(c p) n -> p c n", p=P)).then_inc(w_in, 16)
            sp.dma_start(wa[:, :, QKV:W], w["W1"].rearrange("(c p) n -> p c n", p=P)).then_inc(w_in, 16)
            sp.dma_start(wn[:], w["w_norm1"].rearrange("(c p) -> p c", p=P), allow_slow_non_contiguous=True).then_inc(w_in, 16)
            sp.dma_start(wo[:], w["w_out"].rearrange("(c p) n -> p c n", p=P)).then_inc(w_in, 16)

            def load(i, s):
                k = i * SQ + s
                wait_count(sp, sq_done, k - SQ + 1)
                sp.dma_start(xn[:, s, :], xn_in[bass.ds(k * P, P), :]).then_inc(row_in[s], 16)

            in_turns(sp, NT, SQ, ((0, load),))

        @block.gpsimd
        def _(g):
            g.iota(node[:], pattern=[[P, NT]], base=0, channel_multiplier=1).then_inc(iota_made, 1)

            def copy(i, s):
                k = i * 2 + s
                wait_count(g, made, k - 1)
                g.tensor_copy(xs[:, s], xt[:, :, bass.ds(k * P, P)]).then_inc(xs_ready, 1)

            def store(i, s):
                k = i * 2 + s
                wait_count(g, y_ready, k + 1)
                g.dma_start(y_out[bass.ds(k * P, P), :], yy[:, s, :]).then_inc(y_stored[s], 16)
                wait_count(g, k_ready, k + 1)
                g.dma_start(q_out[bass.ds(k * P, P), :], qk[:, s, 0:D]).then_inc(slot_out[s], 16)

            in_turns(g, NT, 2, ((2, copy), (0, store)))
            for s in range(2):
                g.wait_ge(slot_out[s], NI * 16)
                g.wait_ge(y_stored[s], NI * 16)

        @block.scalar
        def _(a):
            a.wait_ge(ss_ready, 1)
            a.activation(rs[:], ss[:], ACT.Sqrt, bias=eps[:], scale=1.0 / D).then_inc(sd_ready, 1)

            def exponential(i, s):
                k = i * 2 + s
                wait_count(a, z_ready, k + 1)
                wait_count(a, k_ready, k - 1)
                a.activation(ez[:, s], z[:, s], ACT.Exp).then_inc(exped, 1)

            in_turns(a, NT, 2, ((0, exponential),))

        @block.vector
        def _(v):
            ch = Chain(v, dve)
            ch.done(v.memset(eps[:], EPS_RMS))
            v.wait_ge(iota_made, 1)
            ch.link(v.tensor_copy(valid[:], node[:]))
            ch.done(v.tensor_scalar(valid[:], valid[:], float(N), None, ALU.is_lt))
            v.wait_ge(w_in, 64)
            for cc in range(2):
                ch.done(v.tensor_scalar(wa[:, cc, 0:QKV], wa[:, cc, 0:QKV], wn[:, cc:cc + 1], None, ALU.mult))
            ch.settle()

            def squares(i, s):
                k = i * SQ + s
                wait_after(v, row_in, i, s, per=16)
                wait_count(v, sq_done, k - 1)
                v.scalar_tensor_tensor(junk[:, s], xn[:, s], 1.0, xn[:, s], ALU.mult, ALU.mult,
                                       accum_out=ss[:, bass.ds(k, 1)]).then_inc(sq_done, 1)

            in_turns(v, NT, SQ, ((0, squares),))
            v.wait_ge(sq_done, NT)
            v.tensor_copy(junk[:, 0, 0:1], eps[:]).then_inc(ss_ready, 1)
            v.wait_ge(sd_ready, 1)
            ch.link(v.reciprocal(rs[:], rs[:]))
            v.tensor_copy(junk[:, 1, 0:1], rs[:, 0:1]).then_inc(ready, 1)

            def scale(i, s):
                k = i * 2 + s
                wait_count(v, made, k + 1)
                wait_count(v, summed, k - 1)
                wait_after(v, y_stored, i, s, 2, per=16)
                r = rs[:, bass.ds(k, 1)]
                v.tensor_scalar(z[:, s], bank[2 * s], r, None, ALU.mult).then_inc(z_ready, 1)
                v.tensor_scalar(vv[:, s], bank[2 * s + 1][:, 0:D], r, None, ALU.mult).then_inc(v_ready, 1)
                v.tensor_scalar(yy[:, s], bank[2 * s + 1][:, D:D + HID], dinv[:, bass.ds(k, 1)], None, ALU.mult
                                ).then_inc(y_ready, 1)

            def positive(i, s):
                k = i * 2 + s
                wait_count(v, exped, k + 1)
                v.tensor_scalar(z[:, s], z[:, s], 0.0, None, ALU.max).then_inc(pos, 1)

            def keys(i, s):
                k = i * 2 + s
                wait_count(v, pos, k + 1)
                wait_after(v, slot_out, i, s, 2, per=16)
                v.scalar_tensor_tensor(qk[:, s], ez[:, s], 1.0, z[:, s], ALU.min, ALU.add).then_inc(both, 1)
                wait_count(v, both, k + 1)
                v.tensor_scalar(qk[:, s, D:2 * D], qk[:, s, D:2 * D], valid[:, bass.ds(k, 1)], None, ALU.mult
                                ).then_inc(k_ready, 1)

            in_turns(v, NT, 2, ((0, positive), (1, scale), (0, keys)))
            v.wait_ge(summed, NT)
            ch.done(v.tensor_copy(ksum[:], bank[5][:, 0:D]))
            ch.link(v.memset(kvd[:], 0.0))
            for b in range(4):
                a_, b_ = b * HD1, (b + 1) * HD1
                ch.done(v.tensor_copy(kvd[a_:b_, :, a_:b_],
                                      bank[4][:, 0:D].rearrange("p (c n) -> p c n", c=2)[a_:b_, :, a_:b_]))
            ch.settle()
            v.tensor_copy(junk[:, 0, 0:1], rs[:, 0:1]).then_inc(kvd_ready, 1)
            v.wait_ge(joined, 1)
            ch.link(v.tensor_copy(kvm[:].rearrange("p c n -> p (c n)"), bank[6]))

        @block.tensor
        def _(t):
            t.wait_ge(ready, 1)
            for b in (4, 5):
                t.matmul(bank[b], c["zero"][:, 0:P], c["zero"][:], start=True, stop=False, skip_group_check=True)

            def product(i, s):
                k = i * 2 + s
                wait_count(t, xs_ready, k + 1)
                wait_count(t, y_ready, k - 1)
                for b, (lo, hi) in enumerate(((0, 512), (512, W))):
                    for cc in range(2):
                        ins = t.matmul(bank[2 * s + b][:, 0:hi - lo], xs[:, s, cc, :], wa[:, cc, lo:hi],
                                       start=cc == 0, stop=cc == 1)
                ins.then_inc(made, 1)

            def add(i, s):
                k = i * 2 + s
                wait_count(t, k_ready, k + 1)
                wait_count(t, v_ready, k + 1)
                for cc in range(2):
                    t.matmul(bank[4][:, cc * P:(cc + 1) * P], vv[:, s, cc * P:(cc + 1) * P],
                             qk[:, s, D + cc * P:D + (cc + 1) * P], start=False, stop=False, skip_group_check=True)
                t.matmul(bank[5][:, 0:D], c["ones"][:], qk[:, s, D:2 * D], start=False, stop=False,
                         skip_group_check=True).then_inc(summed, 1)

            in_turns(t, NT, 2, ((2, product), (0, add)))
            t.wait_ge(kvd_ready, 1)
            for cc in range(2):
                ins = t.matmul(bank[6][:, cc * D:(cc + 1) * D], kvd[:, cc, :], wo[:, cc, :], start=True, stop=True)
            ins.then_inc(joined, 1)


def gcn_edges(nc, sem, psum, bank, c, dram, name, W, table, out):
    with ExitStack() as ctx:
        S = 6

        def sbt(nm, shape, dt=F32):
            return ctx.enter_context(nc.sbuf_tensor(f"{name}_{nm}", shape, dt))

        def slots(nm):
            return [sem(f"{name}_{nm}{s}") for s in range(S)]

        acc = sbt("acc", [P, NB, W])
        row = sbt("row", [P, S, G, W])
        col = sbt("col", [P, S, 5, G])
        hot = sbt("hot", [P, S, G, P])
        step_sums = sbt("step_sums", [P, S, G, W])
        blocks = sbt("blocks", [1, T], I32)
        zrow = sbt("zrow", [NP - NB * BW, W])
        blocks_in, cleared, added, stored, gate = (sem(f"{name}_{n}") for n in ("blocks_in", "cleared", "added", "stored", "gate"))
        loaded, gathered, hot_made, made, copied = (slots(n) for n in ("loaded", "gathered", "hot_made", "made", "copied"))
        block = ctx.enter_context(nc.Block())
        ITER = GROUPS // S

        @block.sync
        def _(sp):
            sp.dma_start(blocks[:], dram["blocks"].unsqueeze(0)).then_inc(blocks_in, 16)
            with sp.Fori(0, ITER) as i:
                for s in range(S):
                    k = i * S + s
                    sp.wait_ge(made[s], i)
                    sp.dma_start(col[:, s], dram["cols"][:, bass.ds(k, 1)].rearrange("p k c g -> p (k c) g")
                                 ).then_inc(loaded[s], 16)
            sp.wait_ge(added, GROUPS * G)
            sp.wait_ge(cleared, 2)
            for a, b in ((0, 112), (112, BW)):
                sp.dma_start(out[0:NB * BW].rearrange("(b p) n -> p b n", p=BW)[a:b], acc[a:b]).then_inc(stored, 16)
            sp.dma_start(out[NB * BW:NP], zrow[:]).then_inc(stored, 16)
            sp.wait_ge(stored, 48)

        @block.gpsimd
        def _(g):
            g.memset(acc[:], 0.0).then_inc(cleared, 1)
            g.memset(zrow[:], 0.0).then_inc(cleared, 1)
            with g.Fori(0, ITER) as i:
                for half in range(2):
                    ready = range(half * S // 2, (half + 1) * S // 2)
                    for s in ready:
                        g.wait_ge(loaded[s], i * 16 + 16)
                    wait_alone(g, gate)
                    for s in ready:
                        for n in range(G):
                            g.indirect_dma_start(out=row[:, s, n, :], out_offset=None, in_=table,
                                                 in_offset=bass.IndirectOffsetOnAxis(
                                                     ap=col[:, s, 1, n:n + 1].bitcast(U32), axis=0)).then_inc(gathered[s], 16)

        @block.vector
        def _(v):
            v.wait_ge(cleared, 1)
            v.wait_ge(blocks_in, 16)

            def front(i, s):
                v.wait_ge(loaded[s], i * 16 + 16)
                v.wait_ge(made[s], i)
                v.tensor_tensor(hot[:, s], c["iota"][:].unsqueeze(1).broadcast_to([P, G, P]),
                                col[:, s, 3, :].unsqueeze(2).broadcast_to([P, G, P]), ALU.is_equal).then_inc(hot_made[s], 1)

            def back(i, s):
                k = i * S + s
                regs = [v.value_load(blocks[0:1, bass.ds(k * G + n, 1)], min_val=0, max_val=NB - 1) for n in range(G)]
                v.wait_ge(copied[s], i + 1)
                for n in range(G):
                    v.wait_ge(added, k * G + n)
                    o = acc[:, bass.ds(regs[n], 1), :].rearrange("p b n -> p (b n)")
                    v.tensor_tensor(o, o, step_sums[:, s, n, :], ALU.add).then_inc(added, 1)

            front(0, 0)
            with v.Fori(0, ITER - 1) as i:
                for s in range(S):
                    front(i + (s + 1) // S, (s + 1) % S)
                    back(i, s)
            for s in range(S):
                if s + 1 < S:
                    front(ITER - 1, s + 1)
                back(ITER - 1, s)

        @block.scalar
        def _(a):
            with a.Fori(0, ITER) as i:
                for s in range(S):
                    a.wait_ge(made[s], i + 1)
                    a.wait_ge(added, i * S * G)
                    a.activation(step_sums[:, s].rearrange("p g n -> p (g n)"), bank[s][:, 0:G * W], ACT.Copy
                                 ).then_inc(copied[s], 1)

        @block.tensor
        def _(t):
            with t.Fori(0, ITER) as i:
                for s in range(S):
                    t.wait_ge(hot_made[s], i + 1)
                    t.wait_ge(gathered[s], i * 16 * G + 16 * G)
                    t.wait_ge(copied[s], i)
                    for n in range(G):
                        ins = t.matmul(bank[s][:, n * W:(n + 1) * W], hot[:, s, n, :], row[:, s, n, :], start=True, stop=True)
                    ins.then_inc(made[s], 1)


def gcn_norm(nc, sem, psum, bank, c, name, W, sums_in, own, dinv, w, relu, w_next, out):
    with ExitStack() as ctx:
        def sbt(nm, shape, dt=F32):
            return ctx.enter_context(nc.sbuf_tensor(f"{name}_{nm}", shape, dt))

        def sems(*names):
            return (sem(f"{name}_{n}") for n in names)

        h, o, sq = sbt("h", [P, NT, W]), sbt("o", [P, NT, W]), sbt("sq", [P, NT, W])
        vec = sbt("vec", [P, 3, W])
        wnx = sbt("wnx", [P, W, 2]) if w_next is not None else None
        node, valid = sbt("node_i", [P, NT], I32), sbt("valid", [P, NT])
        part, mu, sd, eps = sbt("part", [P, W]), sbt("mu", [P, W]), sbt("sd", [P, W]), sbt("eps", [P, 1])
        w_in, dve, iota_made, part_ready, mean_made, var_ready, sd_ready, out_ready, stored = sems(
            "w_in", "dve", "iota_made", "part_ready", "mean_made", "var_ready", "sd_ready", "out_ready", "stored")
        on_chip = w_next is None
        loads = 5 - 2 * on_chip + (w_next is not None)
        block = ctx.enter_context(nc.Block())

        @block.sync
        def _(sp):
            if not on_chip:
                sp.dma_start(h[:], sums_in.rearrange("(t p) n -> p t n", p=P)).then_inc(w_in, 16)
                sp.dma_start(o[:], own.rearrange("(t p) n -> p t n", p=P)).then_inc(w_in, 16)
            for n, x in enumerate(w):
                sp.dma_start(vec[:, n, :], x.unsqueeze(0).broadcast_to([P, W])).then_inc(w_in, 16)
            if w_next is not None:
                sp.dma_start(wnx[:].rearrange("p a b -> p (a b)"),
                             w_next.rearrange("a b -> (a b)").unsqueeze(0).broadcast_to([P, W * 2])).then_inc(w_in, 16)

        @block.gpsimd
        def _(g):
            g.iota(node[:], pattern=[[P, NT]], base=0, channel_multiplier=1).then_inc(iota_made, 1)

        @block.tensor
        def _(t):
            for n in range(2):
                t.wait_ge(part_ready, n + 1)
                t.matmul(bank[0][:, 0:W], c["ones"][:], part[:], start=True, stop=True).then_inc(mean_made, 1)

        @block.scalar
        def _(a):
            a.wait_ge(var_ready, 1)
            a.activation(sd[:], part[:], ACT.Sqrt, bias=eps[:]).then_inc(sd_ready, 1)

        @block.vector
        def _(v):
            ch = Chain(v, dve)

            def over_nodes(x):
                return x.unsqueeze(1).broadcast_to([P, NT, W])

            def over_features(x):
                return x.unsqueeze(2).broadcast_to([P, NT, W])

            ch.done(v.memset(eps[:], EPS_BN))
            v.wait_ge(iota_made, 1)
            ch.link(v.tensor_copy(valid[:], node[:]))
            ch.done(v.tensor_scalar(valid[:], valid[:], float(N), None, ALU.is_lt))
            v.wait_ge(w_in, 16 * loads)
            ch.link(v.tensor_tensor(h[:], (sums_in if on_chip else h)[:], (own if on_chip else o)[:], ALU.add))
            ch.link(v.tensor_tensor(h[:], h[:], over_features(dinv[:]), ALU.mult))
            ch.link(v.tensor_tensor(h[:], h[:], over_nodes(vec[:, 0, :]), ALU.add))
            ch.link(v.tensor_tensor(h[:], h[:], over_features(valid[:]), ALU.mult))
            v.tensor_reduce(part[:], h[:].rearrange("p t n -> p n t"), AX.X, ALU.add).then_inc(part_ready, 1)
            v.wait_ge(mean_made, 1)
            ch.link(v.tensor_scalar(mu[:], bank[0][:, 0:W], 1.0 / N, None, ALU.mult))
            ch.link(v.tensor_tensor(h[:], h[:], over_nodes(mu[:]), ALU.subtract))
            ch.link(v.tensor_tensor(h[:], h[:], over_features(valid[:]), ALU.mult))
            ch.link(v.tensor_tensor(sq[:], h[:], h[:], ALU.mult))
            v.tensor_reduce(part[:], sq[:].rearrange("p t n -> p n t"), AX.X, ALU.add).then_inc(part_ready, 1)
            v.wait_ge(mean_made, 2)
            v.tensor_scalar(part[:], bank[0][:, 0:W], 1.0 / N, None, ALU.mult).then_inc(var_ready, 1)
            v.wait_ge(sd_ready, 1)
            ch.link(v.reciprocal(mu[:], sd[:]))
            ch.link(v.tensor_tensor(mu[:], mu[:], vec[:, 1, :], ALU.mult))
            ch.link(v.tensor_tensor(h[:], h[:], over_nodes(mu[:]), ALU.mult))
            dst_ = out if w_next is None else h
            ch.link(v.tensor_tensor(dst_[:], h[:], over_nodes(vec[:, 2, :]), ALU.add))
            if w_next is not None:
                ch.link(v.tensor_scalar(h[:], h[:], 0.0, None, ALU.max))
                for n in range(2):
                    ch.link(v.tensor_tensor(sq[:], h[:], over_nodes(wnx[:, :, n]), ALU.mult))
                    ch.link(v.tensor_reduce(out[:, :, n], sq[:], AX.X, ALU.add))
                v.tensor_tensor(out[:], out[:], dinv[:].unsqueeze(2).broadcast_to([P, NT, 2]), ALU.mult
                                ).then_inc(out_ready, 1)
                v.wait_ge(out_ready, 1)


def finish_layer1(nc, sem, psum, bank, c, w, x_in, xn_in, q_in, zn, ksum, kvm, x_out):
    with ExitStack() as ctx:
        def sbt(nm, shape, dt=F32):
            return ctx.enter_context(nc.sbuf_tensor(f"f1_{nm}", shape, dt))

        def sems(*names):
            return (sem(f"f1_{n}") for n in names)

        S = 5
        vec = sbt("vec", [P, 5, D])
        x, xn, q = sbt("x", [P, S, D]), sbt("xn", [P, S, D]), sbt("q", [P, S, D])
        qt = sbt("qt", [P, S, D])
        t1, h, o = sbt("t1", [P, S, D]), sbt("h", [P, S, D]), sbt("o", [P, S, D])
        den, ss, sd, eps = sbt("den", [P, S, MH]), sbt("ss", [P, S]), sbt("sd", [P, S]), sbt("eps", [P, 1])
        w_in, dve, q_ready, turned, qt_ready, made, ss_ready, sd_ready, out_ready, scaled = sems(
            "w_in", "dve", "q_ready", "turned", "qt_ready", "made", "ss_ready", "sd_ready", "out_ready", "scaled")
        dens, biased, h_ready, outs, roots = sems("dens", "biased", "h_ready", "outs", "roots")
        slot_in = [sem(f"f1_slot_in{s}") for s in range(S)]
        slot_out = [sem(f"f1_slot_out{s}") for s in range(S)]
        block = ctx.enter_context(nc.Block())

        @block.sync
        def _(sp):
            for n, a in enumerate((w["b_out"], w["w_norm2"], w["bd"], w["Wd"][0], w["Wd"][1])):
                sp.dma_start(vec[:, n, :], a.unsqueeze(0).broadcast_to([P, D])).then_inc(w_in, 16)

            def load(i, s):
                k = i * S + s
                wait_count(sp, out_ready, k - S + 1)
                for dst_, src_ in ((x, x_in), (xn, xn_in), (q, q_in)):
                    sp.dma_start(dst_[:, s, :], src_[bass.ds(k * P, P), :]).then_inc(slot_in[s], 16)

            in_turns(sp, NT, S, ((0, load),))

        @block.gpsimd
        def _(g):
            def store(i, s):
                k = i * S + s
                wait_count(g, out_ready, k + 1)
                g.dma_start(x_out[bass.ds(k * P, P), :], o[:, s, :]).then_inc(slot_out[s], 16)

            in_turns(g, NT, S, ((0, store),))
            for s in range(S):
                g.wait_ge(slot_out[s], NT // S * 16)

        @block.scalar
        def _(a):
            def take(i, s):
                k = i * S + s
                wait_count(a, turned, k + 1)
                wait_count(a, made, k - S + 1)
                a.activation(qt[:, s], bank[s][:, 0:D], ACT.Identity).then_inc(qt_ready, 1)

            def root(i, s):
                k = i * S + s
                wait_count(a, ss_ready, k + 1)
                wait_count(a, out_ready, k - S + 1)
                a.activation(sd[:, s:s + 1], ss[:, s:s + 1], ACT.Sqrt, bias=eps[:], scale=1.0 / D).then_inc(sd_ready, 1)

            in_turns(a, NT, S, ((2, take), (0, root)))

        @block.tensor
        def _(t):
            def turn(i, s):
                k = i * S + s
                wait_count(t, q_ready, k + 1)
                wait_count(t, h_ready, k - S + 1)
                t.transpose(bank[s][:, 0:P], q[:, s, 0:P], c["ident"][:])
                t.transpose(bank[s][:, P:D], q[:, s, P:D], c["ident"][:]).then_inc(turned, 1)

            def product(i, s):
                k = i * S + s
                wait_count(t, qt_ready, k + 1)
                for cc in range(2):
                    ins = t.matmul(bank[s][:, D:2 * D], qt[:, s, cc * P:(cc + 1) * P], kvm[:, cc, :],
                                   start=cc == 0, stop=cc == 1)
                ins.then_inc(made, 1)

            in_turns(t, NT, S, ((2, turn), (1, product)))

        @block.vector
        def _(v):
            ch = Chain(v, dve)
            ch.link(v.memset(eps[:], EPS_RMS))
            v.wait_ge(w_in, 80)

            def denominators(i, s):
                k = i * S + s
                wait_after(v, slot_in, i, s, per=48)
                wait_count(v, out_ready, k - S + 1)
                v.tensor_tensor(t1[:, s], q[:, s], ksum[:], ALU.mult).then_inc(dens, 1)
                v.tensor_tensor(x[:, s], x[:, s], vec[:, 2, :], ALU.add).then_inc(biased, 1)
                wait_count(v, dens, k * 4 + 1)
                v.tensor_reduce(den[:, s, :], t1[:, s].rearrange("p (h d) -> p h d", h=MH), AX.X, ALU.add).then_inc(dens, 1)
                v.tensor_tensor(xn[:, s], xn[:, s], vec[:, 0, :], ALU.add).then_inc(biased, 1)
                wait_count(v, dens, k * 4 + 2)
                v.tensor_scalar(den[:, s, :], den[:, s, :], EPS_RMS, None, ALU.add).then_inc(dens, 1)
                wait_count(v, dens, k * 4 + 3)
                v.reciprocal(den[:, s, :], den[:, s, :]).then_inc(dens, 1)
                wait_count(v, dens, k * 4 + 4)
                qh = q[:, s].rearrange("p (h d) -> p h d", h=MH)
                v.tensor_tensor(qh, qh, den[:, s, :].unsqueeze(2).broadcast_to([P, MH, HD1]), ALU.mult).then_inc(q_ready, 1)

            def residual(i, s):
                k = i * S + s
                wait_count(v, made, k + 1)
                wait_count(v, biased, 2 * k + 2)
                v.tensor_tensor(h[:, s], xn[:, s], bank[s][:, D:2 * D], ALU.add).then_inc(h_ready, 1)
                wait_after(v, slot_out, i, s, S, per=16)
                v.scalar_tensor_tensor(o[:, s], vec[:, 3, :], zn[:, bass.ds(k, 1), 0:1].rearrange("p a b -> p (a b)"),
                                       x[:, s], ALU.mult, ALU.add).then_inc(outs, 1)
                wait_count(v, h_ready, k + 1)
                v.scalar_tensor_tensor(t1[:, s], h[:, s], 1.0, h[:, s], ALU.mult, ALU.mult,
                                       accum_out=ss[:, s:s + 1]).then_inc(ss_ready, 1)
                wait_count(v, outs, 2 * k + 1)
                v.scalar_tensor_tensor(o[:, s], vec[:, 4, :], zn[:, bass.ds(k, 1), 1:2].rearrange("p a b -> p (a b)"),
                                       o[:, s], ALU.mult, ALU.add).then_inc(outs, 1)

            def finish(i, s):
                k = i * S + s
                wait_count(v, sd_ready, k + 1)
                v.reciprocal(ss[:, s:s + 1], sd[:, s:s + 1]).then_inc(roots, 1)
                wait_count(v, outs, 2 * k + 2)
                v.tensor_tensor(o[:, s], o[:, s], h[:, s], ALU.add).then_inc(scaled, 1)
                wait_count(v, roots, k + 1)
                v.scalar_tensor_tensor(t1[:, s], h[:, s], ss[:, s:s + 1], vec[:, 1, :], ALU.mult, ALU.mult
                                       ).then_inc(scaled, 1)
                wait_count(v, scaled, 2 * k + 2)
                v.tensor_tensor(o[:, s], o[:, s], t1[:, s], ALU.add).then_inc(out_ready, 1)

            in_turns(v, NT, S, ((2, denominators), (0, residual), (-1, finish)))




def gcn_edges_narrow(nc, sem, psum, bank, c, dram, zt, sums):
    W = 2
    S = 2
    groups = -(-(FULL + 1) // (G * S)) * S
    with ExitStack() as ctx:
        def sbt(nm, shape, dt=F32):
            return ctx.enter_context(nc.sbuf_tensor(f"gn_{nm}", shape, dt))

        def slots(nm):
            return [sem(f"gn_{nm}{s}") for s in range(S)]

        ends = sbt("ends", [P, RB, 2, P])
        ends_i = sbt("ends_i", [P, RB, 2, P], I32)
        part_i = sbt("part_i", [P, RB, 2, P], I32)
        tiles, places = sbt("tiles", [P, RB, 2, P]), sbt("places", [P, RB, 2, P])
        cols = sbt("cols", [P, 3, T])
        row = sbt("row", [P, S, G * P])
        tile_hot = sbt("tile_hot", [P, S, 2, G, NT])
        place = sbt("place", [P, S, G, P])
        picked = sbt("picked", [P, G, NT, W])
        pair = sbt("pair", [P, G, W])
        spread = sbt("spread", [P, S, G, NT, W])
        less_p = sbt("less_partition", [P, 1])
        ends_in, chain, split, turned, kept, low_stored, less_ready, ready, summed = (
            sem(f"gn_{n}") for n in ("ends_in", "chain", "split", "turned", "kept", "low_stored", "less_ready", "ready",
                                     "summed"))
        row_in, row_hot, tiles_far, tiles_hot, place_hot, looked_up, chosen, paired, spread_made, added = (
            slots(n) for n in ("row_in", "row_hot", "tiles_far", "tiles_hot", "place_hot", "looked_up", "chosen", "paired",
                               "spread_made", "added"))
        block = ctx.enter_context(nc.Block())

        @block.sync
        def _(sp):
            sp.dma_start(ends[:].rearrange("p b c j -> p b (c j)"),
                         dram["tile_rows"].rearrange("(b p) n -> p b n", p=P)[:, :, 0:2 * P]).then_inc(ends_in, 16)
            sp.wait_ge(split, 1)
            sp.dma_start(dram["low"].rearrange("(b p) j -> p b j", p=P), places[:, :, 1, :]).then_inc(low_stored, 16)
            sp.wait_ge(low_stored, 16)
            with sp.Fori(0, groups // S) as i:
                for s in range(S):
                    sp.wait_ge(looked_up[s], i)
                    sp.dma_start(row[:, s, :], dram["low"][bass.ds((i * S + s) * G, G)].rearrange("g n -> (g n)")
                                 .unsqueeze(0).broadcast_to([P, G * P])).then_inc(row_in[s], 16)

        @block.scalar
        def _(a):
            a.wait_ge(less_ready, 1)

            def hot(i, s):
                wait_after(a, row_in, i, s, per=16)
                a.activation(row[:, s, :], row[:, s, :], ACT.Square, bias=less_p[:]).then_inc(row_hot[s], 1)
                wait_after(a, row_hot, i, s, per=2, less=1)
                a.activation(row[:, s, :], row[:, s, :], ACT.Relu, bias=c["ones"][:, 0:1], scale=-1.0
                             ).then_inc(row_hot[s], 1)
                both = tile_hot[:, s].rearrange("p x n t -> p (x n t)")
                wait_after(a, tiles_far, i, s, per=2)
                a.activation(both, both, ACT.Square).then_inc(tiles_hot[s], 1)
                wait_after(a, tiles_hot, i, s, per=2, less=1)
                a.activation(both, both, ACT.Relu, bias=c["ones"][:, 0:1], scale=-1.0).then_inc(tiles_hot[s], 1)

            in_turns(a, groups, S, ((0, hot),))

        @block.gpsimd
        def _(g):
            g.wait_ge(ready, 1)

            def distance(i, s):
                wait_after(g, spread_made, i, s, S)
                first = (i * S + s) * G
                for x in range(2):
                    g.tensor_tensor(tile_hot[:, s, x], c["iota"][:, 0:NT].unsqueeze(1).broadcast_to([P, G, NT]),
                                    cols[:, x, bass.ds(first, G)].unsqueeze(2).broadcast_to([P, G, NT]), ALU.subtract
                                    ).then_inc(tiles_far[s], 1)

            in_turns(g, groups, S, ((0, distance),))

        @block.tensor
        def _(t):
            t.wait_ge(split, 1)
            for b in range(RB):
                if b >= 2:
                    t.wait_ge(kept, b - 1)
                for x, a in enumerate((tiles[:, b, 0, :], tiles[:, b, 1, :], places[:, b, 0, :])):
                    ins = t.transpose(bank[b % 2][:, x * P:(x + 1) * P], a, c["ident"][:])
                ins.then_inc(turned, 1)
            t.wait_ge(kept, RB)
            t.matmul(bank[6], c["zero"][:, 0:P], c["zero"][:], start=True, stop=False, skip_group_check=True)

            def look_up(i, s):
                wait_after(t, row_hot, i, s, per=2)
                wait_after(t, chosen, i, s, S, per=2)
                for n in range(G):
                    ins = t.matmul(bank[2 * s + n // 4][:, (n % 4) * NT * W:(n % 4 + 1) * NT * W], row[:, s, n * P:(n + 1) * P],
                                   zt[:].rearrange("p t c -> p (t c)"), start=True, stop=True)
                ins.then_inc(looked_up[s], 1)

            def scatter(i, s):
                wait_after(t, spread_made, i, s)
                wait_after(t, place_hot, i, s)
                for n in range(G):
                    ins = t.matmul(bank[6][:, 0:NT * W], place[:, s, n, :], spread[:, s, n].rearrange("p t c -> p (t c)"),
                                   start=False, stop=False, skip_group_check=True)
                ins.then_inc(added[s], 1)

            in_turns(t, groups, S, ((1, look_up), (0, scatter)))
            for s in range(S):
                t.wait_ge(added[s], groups // S)
            t.sem_inc(summed, 1)

        @block.vector
        def _(v):
            ch = Chain(v, chain)
            v.tensor_scalar(less_p[:], c["pcol"][:], -1.0, None, ALU.mult).then_inc(less_ready, 1)
            v.wait_ge(ends_in, 16)
            ch.link(v.tensor_copy(ends_i[:], ends[:]))
            ch.link(v.tensor_scalar(part_i[:], ends_i[:], 7, None, ALU.logical_shift_right))
            ch.link(v.tensor_copy(tiles[:], part_i[:]))
            ch.link(v.scalar_tensor_tensor(places[:], tiles[:], float(-P), ends[:], ALU.mult, ALU.add))
            v.tensor_copy(ends[:, 0, 0, 0:1], tiles[:, 0, 0, 0:1]).then_inc(split, 1)
            for b in range(RB):
                v.wait_ge(turned, b + 1)
                v.tensor_copy(cols[:, :, b * P:(b + 1) * P], bank[b % 2][:, 0:3 * P].rearrange("p (c n) -> p c n", c=3)
                              ).then_inc(kept, 1)
            v.wait_ge(kept, RB)
            v.tensor_copy(ends[:, 0, 0, 0:1], tiles[:, 0, 0, 0:1]).then_inc(ready, 1)

            def choose(i, s):
                first = (i * S + s) * G
                wait_after(v, looked_up, i, s)
                wait_after(v, tiles_hot, i, s, per=2)
                wait_after(v, paired, i, s, 1)
                for h in range(2):
                    v.tensor_tensor(picked[:, 4 * h:4 * h + 4], bank[2 * s + h][:, 0:4 * NT * W]
                                    .rearrange("p (n t c) -> p n t c", t=NT, c=W),
                                    tile_hot[:, s, 1, 4 * h:4 * h + 4].unsqueeze(3).broadcast_to([P, 4, NT, W]), ALU.mult
                                    ).then_inc(chosen[s], 1)
                wait_after(v, added, i, s, S)
                v.tensor_tensor(place[:, s], c["iota"][:].unsqueeze(1).broadcast_to([P, G, P]),
                                cols[:, 2, bass.ds(first, G)].unsqueeze(2).broadcast_to([P, G, P]), ALU.is_equal
                                ).then_inc(place_hot[s], 1)
                wait_after(v, chosen, i, s, per=2)
                wait_after(v, spread_made, i, s, 1)
                v.tensor_reduce(pair[:], picked[:].rearrange("p n t c -> p n c t"), AX.X, ALU.add).then_inc(paired[s], 1)
                wait_after(v, paired, i, s)
                v.tensor_tensor(spread[:, s], tile_hot[:, s, 0].unsqueeze(3).broadcast_to([P, G, NT, W]),
                                pair[:].unsqueeze(2).broadcast_to([P, G, NT, W]), ALU.mult).then_inc(spread_made[s], 1)

            in_turns(v, groups, S, ((0, choose),))
            v.wait_ge(summed, 1)
            v.tensor_copy(sums[:].rearrange("p t c -> p (t c)"), bank[6][:, 0:NT * W])

NE = 8
EPS_EXP = 1e-3


def expert_mixture(nc, sem, psum, bank, c, xt, w, x_in, out):
    with ExitStack() as ctx:
        def sbt(nm, shape, dt=F32):
            return ctx.enter_context(nc.sbuf_tensor(f"em_{nm}", shape, dt))

        def sems(*names):
            return (sem(f"em_{n}") for n in names)

        w1, w2, wo = (sbt(n, [P, 2, NE, D]) for n in ("w1", "w2", "wo"))
        bo = sbt("bo", [P, NE, D])
        wr, br = sbt("wr", [P, 2, NE]), sbt("br", [NE, 1])
        bn = sbt("bn", [2 * NE, 2, 5, P])
        root, fac = sbt("root", [2 * NE, 2, P]), sbt("fac", [2 * NE, 2, 2, P])
        affine = sbt("affine", [P, 2, 2, 2 * NE])
        eps = sbt("eps", [2 * NE, 1])
        lt = sbt("logits_turned", [NE, 2 * P])
        we, top, tot = sbt("weights", [P, NT, NE]), sbt("top", [P, NT]), sbt("tot", [P, NT])
        h1, h2 = sbt("h1", [P, 2, 2, 2 * P]), sbt("h2", [P, 2, 2, 2 * P])
        x, o = sbt("x", [P, 2, D]), sbt("o", [P, 2, D])
        w_in, bn_in, dve, eps_ready, root_ready, fac_ready, fac_turned, affine_ready = sems(
            "w_in", "bn_in", "dve", "eps_ready", "root_ready", "fac_ready", "fac_turned", "affine_ready")
        logits_made, logits_biased, logits_turned, logits_taken, centred, exped, x_in_sem, started = sems(
            "logits_made", "logits_biased", "logits_turned", "logits_taken", "centred", "exped", "x_in", "started")
        h1_made, h1_taken, h2_made, h2_taken, y_made, y_added, stored = sems(
            "h1_made", "h1_taken", "h2_made", "h2_taken", "y_made", "y_added", "stored")
        gate = sem("em_gate")
        block = ctx.enter_context(nc.Block())
        rows = x_in.rearrange("(t p) d -> p t d", p=P)
        ROW_LAST = N - (NT - 2) * P

        @block.sync
        def _(sp):
            for n, l in enumerate(("1", "2")):
                for m, a in enumerate(("b", "g", "be", "m", "v")):
                    sp.dma_start(bn[:, n, m, :], w[a + l].rearrange("e (c p) -> (e c) p", p=P)).then_inc(bn_in, 16)
            sp.dma_start(wr[:], w["Wr"].rearrange("(c p) e -> p c e", p=P)).then_inc(w_in, 16)
            sp.dma_start(br[:], w["br"].unsqueeze(1), allow_slow_non_contiguous=True).then_inc(w_in, 16)
            for o_, i_ in ((w1, w["W1"]), (w2, w["W2"]), (wo, w["Wo"])):
                for cc in range(2):
                    sp.dma_start(o_[:, cc], i_[:, cc * P:(cc + 1) * P, :].rearrange("e p n -> p e n")).then_inc(w_in, 16)
            sp.dma_start(bo[:].rearrange("p e n -> p (e n)"),
                         w["bo"].rearrange("e n -> (e n)").unsqueeze(0).broadcast_to([P, NE * D])).then_inc(w_in, 16)
            with sp.Fori(0, NI) as i:
                sp.wait_ge(started, i * 2)
                sp.dma_start(x[:], rows[:, bass.ds(i * 2, 2), :]).then_inc(x_in_sem, 16)

        @block.gpsimd
        def _(g):
            with g.Fori(0, NI - 1) as i:
                g.wait_ge(y_added, i * 2 * NE + 2 * NE)
                g.dma_start(out[bass.ds(i * 2 * P, 2 * P), :].rearrange("(t p) d -> p t d", p=P), o[:]).then_inc(stored, 16)
            g.wait_ge(y_added, NI * 2 * NE)
            g.dma_start(out[(NT - 2) * P:N, :], o[0:ROW_LAST, 0, :]).then_inc(stored, 16)
            g.wait_ge(stored, 16 * NI)

        @block.tensor
        def _(t):
            t.wait_ge(fac_ready, 1)
            for n in range(4):
                ins = t.transpose(bank[7][:, n * 2 * NE:(n + 1) * 2 * NE], fac[:, n // 2, n % 2, :],
                                  c["ident"][0:2 * NE, 0:2 * NE])
            ins.then_inc(fac_turned, 1)
            t.wait_ge(affine_ready, 1)
            t.wait_ge(w_in, 16 * 9)
            with t.Fori(0, NI) as i:
                t.wait_ge(logits_biased, i)
                for cc in range(2):
                    ins = t.matmul(bank[6][0:NE, 0:2 * P], wr[:, cc, :], xt[:, cc, bass.ds(i * 2 * P, 2 * P)],
                                   start=cc == 0, stop=cc == 1)
                ins.then_inc(logits_made, 1)
                t.wait_ge(logits_taken, i)
                t.wait_ge(logits_biased, i + 1)
                wait_alone(t, gate)
                for s in range(2):
                    ins = t.transpose(bank[7][:, s * NE:(s + 1) * NE], lt[:, s * P:(s + 1) * P], c["ident"][0:NE, 0:NE])
                ins.then_inc(logits_turned, 1)
            with t.Fori(0, NI) as i:
                for e in range(NE + 2):
                    if e < NE:
                        t.wait_ge(h1_taken, i * NE + max(e - 1, 0))
                        for o_ in range(2):
                            for cc in range(2):
                                ins = t.matmul(bank[e % 2][:, o_ * 2 * P:(o_ + 1) * 2 * P], w1[:, cc, e, o_ * P:(o_ + 1) * P],
                                               xt[:, cc, bass.ds(i * 2 * P, 2 * P)], start=cc == 0, stop=cc == 1)
                        ins.then_inc(h1_made, 1)
                    if 1 <= e <= NE:
                        f = e - 1
                        t.wait_ge(h1_taken, i * NE + f + 1)
                        t.wait_ge(h2_taken, i * NE + max(f - 1, 0))
                        for o_ in range(2):
                            for cc in range(2):
                                ins = t.matmul(bank[2 + f % 2][:, o_ * 2 * P:(o_ + 1) * 2 * P],
                                               w2[:, cc, f, o_ * P:(o_ + 1) * P], h1[:, f % 2, cc, :],
                                               start=cc == 0, stop=cc == 1)
                        ins.then_inc(h2_made, 1)
                    if e >= 2:
                        f = e - 2
                        t.wait_ge(h2_taken, i * NE + f + 1)
                        t.wait_ge(y_added, i * 2 * NE + 2 * max(f - 1, 0))
                        for s in range(2):
                            for cc in range(2):
                                ins = t.matmul(bank[4 + f % 2][:, s * D:(s + 1) * D], h2[:, f % 2, cc, s * P:(s + 1) * P],
                                               wo[:, cc, f, :], start=cc == 0, stop=cc == 1)
                        ins.then_inc(y_made, 1)

        @block.scalar
        def _(a):
            a.wait_ge(bn_in, 160)
            a.wait_ge(eps_ready, 1)
            a.activation(root[:], bn[:, :, 4, :], ACT.Sqrt, bias=eps[:]).then_inc(root_ready, 1)
            a.wait_ge(w_in, 16 * 9)
            with a.Fori(0, NI) as i:
                a.wait_ge(logits_made, i + 1)
                a.wait_ge(logits_turned, i)
                a.activation(lt[:], bank[6][0:NE, 0:2 * P], ACT.Identity, bias=br[:]).then_inc(logits_biased, 1)
            a.wait_ge(centred, 1)
            a.activation(we[:], we[:], ACT.Exp).then_inc(exped, 1)
            a.wait_ge(affine_ready, 1)
            with a.Fori(0, NI) as i:
                for e in range(NE + 1):
                    for layer, f, made, taken, read, b, h in ((0, e, h1_made, h1_taken, h2_made, 0, h1),
                                                              (1, e - 1, h2_made, h2_taken, y_made, 2, h2)):
                        if not 0 <= f < NE:
                            continue
                        a.wait_ge(made, i * NE + f + 1)
                        a.wait_ge(read, i * NE + max(f - 1, 0))
                        for cc in range(2):
                            k = 2 * f + cc
                            ins = a.activation(h[:, f % 2, cc, :], bank[b + f % 2][:, cc * 2 * P:(cc + 1) * 2 * P], ACT.Relu,
                                               bias=affine[:, layer, 1, k:k + 1], scale=affine[:, layer, 0, k:k + 1])
                        ins.then_inc(taken, 1)

        @block.vector
        def _(v):
            ch = Chain(v, dve)
            v.memset(eps[:], EPS_EXP).then_inc(eps_ready, 1)
            v.wait_ge(root_ready, 1)
            ch.link(v.reciprocal(root[:], root[:]))
            ch.link(v.tensor_tensor(fac[:, :, 0, :], root[:], bn[:, :, 1, :], ALU.mult))
            ch.link(v.tensor_tensor(root[:], bn[:, :, 0, :], bn[:, :, 3, :], ALU.subtract))
            ch.link(v.tensor_tensor(root[:], root[:], fac[:, :, 0, :], ALU.mult))
            v.tensor_tensor(fac[:, :, 1, :], root[:], bn[:, :, 2, :], ALU.add).then_inc(fac_ready, 1)
            v.wait_ge(fac_turned, 1)
            v.tensor_copy(affine[:].rearrange("p l a k -> p (l a k)"), bank[7][:, 0:8 * NE]).then_inc(affine_ready, 1)
            with v.Fori(0, NI) as i:
                v.wait_ge(logits_turned, i + 1)
                v.tensor_copy(we[:, bass.ds(i * 2, 2), :].rearrange("p t e -> p (t e)"), bank[7][:, 0:2 * NE]
                              ).then_inc(logits_taken, 1)
            v.wait_ge(logits_taken, NI)
            ch.link(v.tensor_reduce(top[:], we[:], AX.X, ALU.max))
            v.tensor_tensor(we[:], we[:], top[:].unsqueeze(2).broadcast_to([P, NT, NE]), ALU.subtract).then_inc(centred, 1)
            v.wait_ge(exped, 1)
            ch.link(v.tensor_reduce(tot[:], we[:], AX.X, ALU.add))
            ch.link(v.reciprocal(tot[:], tot[:]))
            ch.link(v.tensor_tensor(we[:], we[:], tot[:].unsqueeze(2).broadcast_to([P, NT, NE]), ALU.mult))
            v.wait_ge(w_in, 16 * 9)
            with v.Fori(0, NI) as i:
                ch.enter(i, 2 * (NE - 1))

                def weight(s, e):
                    return we[:, bass.ds(i * 2 + s, 1), e:e + 1].rearrange("p a b -> p (a b)")

                v.wait_ge(x_in_sem, i * 16 + 16)
                v.wait_ge(stored, i * 16)
                for e in range(NE):
                    for s in range(2):
                        ins = v.scalar_tensor_tensor(o[:, s, :], bo[:, e, :], weight(s, e), (x if e == 0 else o)[:, s, :],
                                                     ALU.mult, ALU.add)
                        if e == 0:
                            ins.then_inc(started, 1)
                        else:
                            ch.done(ins)
                    if e == 0:
                        v.wait_ge(started, i * 2 + 2)
                    else:
                        ch.settle()
                for e in range(NE):
                    v.wait_ge(y_made, i * NE + e + 1)
                    v.wait_ge(y_added, i * 2 * NE + 2 * e)
                    for s in range(2):
                        v.scalar_tensor_tensor(o[:, s, :], bank[4 + e % 2][:, s * D:(s + 1) * D], weight(s, e), o[:, s, :],
                                               ALU.mult, ALU.add).then_inc(y_added, 1)
                ch.leave(NI)
def padded_inputs(nc, sem, c, x, types, x_pad, types_pad):
    rest = (NP - N)
    with ExitStack() as ctx:
        z = ctx.enter_context(nc.sbuf_tensor("pad_types", [1, rest], I32))
        cleared, stored = sem("pad_cleared"), sem("pad_stored")
        block = ctx.enter_context(nc.Block())

        @block.vector
        def _(v):
            v.memset(z[:], 0).then_inc(cleared, 1)

        @block.sync
        def _(sp):
            sp.dma_start(x_pad[0:N, :], x).then_inc(stored, 16)
            sp.dma_start(types_pad[0:N], types).then_inc(stored, 16)
            sp.wait_ge(c["ready"], c["n"])
            sp.dma_start(x_pad[N:N + P, :], c["zero"][:, 0:D]).then_inc(stored, 16)
            sp.dma_start(x_pad[N + P:NP, :], c["zero"][0:rest - P, 0:D]).then_inc(stored, 16)
            sp.wait_ge(cleared, 1)
            sp.dma_start(types_pad[N:NP].unsqueeze(0), z[:]).then_inc(stored, 16)
            sp.wait_ge(stored, 80)


def stage(build, nc, *args):
    taken = []

    def sem(name):
        taken.append(nc.alloc_semaphore(name=name))
        return taken[-1]

    build(nc, sem, *args)
    nc.all_engine_barrier()
    nc.clear_and_free_semaphores(taken)
    nc.all_engine_barrier()


def graph_network(nc, args, out):
    def scratch(name, shape, dt=F32):
        return nc.dram_tensor(name, shape, dt).ap()

    L0 = {k[3:]: v for k, v in args.items() if k.startswith("L0_")}
    L1 = {k[3:]: v for k, v in args.items() if k.startswith("L1_")}
    gnn0, mix0, ffn0 = ({k[4:]: v for k, v in L0.items() if k.startswith(g)} for g in ("gnn_", "mix_", "ffn_"))
    gnn1, mix1, ffn1 = ({k[4:]: v for k, v in L1.items() if k.startswith(g)} for g in ("gnn_", "mix_", "ffn_"))

    dram = dict(
        tile_rows=scratch("tile_rows", (T, 5 * P)), starts=scratch("starts", (T,)), rel_rows=scratch("rel_rows", (T, P)),
        mask=scratch("run_ends", (T, H, P + 1)), keys=scratch("carry_keys", (T,)), blocks=scratch("step_blocks", (T,), I32),
        cols=scratch("edge_columns", (P, T // G, 5, G)), table=scratch("edge_table", (R * NP, 2 * D)),
        q=scratch("queries", (NP, D)), sums=scratch("node_sums", (NP, CW)), carry=scratch("carried", (T, CW)),
        types=scratch("types_padded", (NP,), I32), router=scratch("router", (NP,)), low=scratch("source_places", (T, P)))
    x0, x1, x2, x3 = (scratch(f"x{n}", (NP, D)) for n in range(4))
    xn1, xn2 = scratch("xn1", (NP, D)), scratch("xn2", (NP, D))
    q1, y1, s1 = scratch("q1", (NP, D)), scratch("y1", (NP, HID)), scratch("s1", (NP, HID))
    xt_kept = scratch("xt_kept", (P, 2, NP))

    with ExitStack() as ctx:
        def sb(name, shape, dt=F32):
            return ctx.enter_context(nc.sbuf_tensor(name, shape, dt))

        psum = ctx.enter_context(nc.psum_tensor("psum", [P, 8, 512], F32))
        bank = [psum[:, b, :] for b in range(8)]
        c = constants(nc, sb, lambda name: ctx.enter_context(nc.semaphore(name)))
        wmix, dinv = sb("wmix", [P, 2, D]), sb("dinv", [P, NT])
        ksum, kvm = sb("ksum", [P, D]), sb("kvm", [P, 2, D])
        zt, zs, zn = (sb(n, [P, NT, 2]) for n in ("zt", "zs", "zn"))

        stage(padded_inputs, nc, c, args["x"], args["node_type_4"], x0, dram["types"])
        stage(index_tables, nc, bank, c, dram, args["src"], args["dst"], args["edge_type_8"])
        with nc.sbuf_tensor("xt0", [P, 2, NP], F32) as xt:
            stage(layernorm_turned, nc, "ln0", bank, c, x0, xt)
            stage(edge_node_tables, nc, bank, c, xt, dict(
                k=gnn0["k_linears"], q=gnn0["q_linears"], v=gnn0["v_linears"], att=gnn0["relation_att"],
                msg=gnn0["relation_msg"], pri=gnn0["relation_pri"]), dram)
            stage(mix0_matrix, nc, psum, bank, c, xt, mix0["Wqkv"], mix0["Wout"], wmix, xt_kept)
        stage(attention_edges, nc, psum, bank, c, dram)
        with nc.sbuf_tensor("xt1", [P, 2, NP], F32) as xt:
            stage(merge_carried, nc, psum, bank, c, dram, xt_kept, xt)
            stage(after_attention, nc, psum, bank, c, xt, wmix, dict(
                a=gnn0["a_linears"], skip=gnn0["skip"], bout=mix0["bout"]), dram, x0, x1, dinv)
            stage(layernorm_turned, nc, "ln1", bank, c, x1, xt, xn1)
            stage(routed_ffn, nc, psum, bank, c, xt, ffn0, dram, x1, xn1, x2)
        w1 = dict(mix1, W1=gnn1["W1"], bd=gnn1["bd"], Wd=gnn1["Wd"])
        with nc.sbuf_tensor("xt2", [P, 2, NP], F32) as xt:
            stage(layernorm_turned, nc, "ln2", bank, c, x2, xt, xn2)
            stage(project_layer1, nc, psum, bank, c, xt, w1, xn2, q1, y1, dinv, ksum, kvm)
        stage(gcn_edges, nc, psum, bank, c, dram, "g1", HID, y1, s1)
        stage(gcn_norm, nc, psum, bank, c, "n1", HID, s1, y1, dinv, (gnn1["b1"], gnn1["g1"], gnn1["be1"]), True,
              gnn1["W2"], zt)
        stage(gcn_edges_narrow, nc, psum, bank, c, dram, zt, zs)
        stage(gcn_norm, nc, psum, bank, c, "n2", 2, zs, zt, dinv, (gnn1["b2"], gnn1["g2"], gnn1["be2"]), False,
              None, zn)
        stage(finish_layer1, nc, psum, bank, c, w1, x2, xn2, q1, zn, ksum, kvm, x3)
        with nc.sbuf_tensor("xt3", [P, 2, NP], F32) as xt:
            stage(layernorm_turned, nc, "ln3", bank, c, x3, xt)
            stage(expert_mixture, nc, psum, bank, c, xt, ffn1, x3, out)



def kernel(**inputs):
    import concourse.bacc as bacc
    from concourse.bass_utils import run_bass_kernel_spmd

    nc = bacc.Bacc("TRN2", target_bir_lowering=False, num_devices=1)
    arrays, args = {}, {}
    for name in inputs:
        if name == "L0_ffn_attention_mask":
            continue
        a = np.ascontiguousarray(inputs[name])
        arrays[f"in_{name}"] = a
        args[name] = nc.dram_tensor(f"in_{name}", a.shape, mybir.dt.from_np(a.dtype), kind="ExternalInput").ap()
    out = nc.dram_tensor("out", (N, D), F32, kind="ExternalOutput").ap()
    graph_network(nc, args, out)
    return run_bass_kernel_spmd(nc, [arrays], core_ids=[0]).results[0]["out"]
```
